# Optimizing a Trainium2 kernel written in Bass

```python
import numpy as np
import jax
import jax.numpy as jnp

def _softmax(x, axis=-1):
    return jax.nn.softmax(x, axis=axis)

def _gelu(x):
    return jax.nn.gelu(x, approximate=True)

def _silu(x):
    return jax.nn.silu(x)

def _sigmoid(x):
    return jax.nn.sigmoid(x)

def _layernorm(x, axis=-1, eps=1e-05):
    m = jnp.mean(x, axis=axis, keepdims=True)
    v = jnp.var(x, axis=axis, keepdims=True)
    return (x - m) / jnp.sqrt(v + eps)

def _scatter_add(tgt, idx, src, axis=0):
    return tgt.at[idx].add(src)

def _segment_sum(src, seg, n):
    return jax.ops.segment_sum(src, seg, n)
kernel_name = 'mk_hybrid_d1_jaxref_r8_5c95a9'

def setup_inputs(seed: int=0):
    np.random.seed(seed)
    _w = jnp.asarray

    def _L0_attn_a_setup():
        import jax, jax.numpy as jnp
        import numpy as np
        D_MODEL = 128
        NUM_HEADS = 16
        D_HEAD = D_MODEL // NUM_HEADS
        NEG_BIG = 10000000000.0
        key = jax.random.key(seed)
        ks = jax.random.split(key, 9)
        d = D_MODEL
        scale = 1.0 / np.sqrt(d)
        inp = {'x': jax.random.normal(ks[0], (2, 256, d), dtype=jnp.float32), 'W_q': jax.random.normal(ks[1], (d, d), dtype=jnp.float32) * scale, 'b_q': jnp.zeros((d,), dtype=jnp.float32), 'W_k': jax.random.normal(ks[2], (d, d), dtype=jnp.float32) * scale, 'b_k': jnp.zeros((d,), dtype=jnp.float32), 'W_v': jax.random.normal(ks[3], (d, d), dtype=jnp.float32) * scale, 'b_v': jnp.zeros((d,), dtype=jnp.float32), 'W_o': jax.random.normal(ks[4], (d, d), dtype=jnp.float32) * scale, 'b_o': jnp.zeros((d,), dtype=jnp.float32)}
        return inp
    _L0_attn_a_in = _L0_attn_a_setup()

    def _L0_attn_b_setup():
        import jax, jax.numpy as jnp
        import numpy as np
        from math import sqrt
        N_HEAD = 16
        W_SCALE = 0.02

        def _reference_tuple_inner(x, W_dq, W_uq, W_dkv, W_uk, W_uv, W_o):
            B, T, C = x.shape
            nh = N_HEAD
            hs = C // nh
            n_kvl = W_dkv.shape[0]
            k_eff = (W_dq.T @ W_uq.T @ W_uk).reshape(nh, hs, n_kvl)
            v_eff = jnp.transpose((W_uv.T @ W_o.T).reshape(n_kvl, nh, hs), (1, 0, 2))
            c_kv = x @ W_dkv.T
            q = x @ W_dq.T @ W_uq.T
            q = q.reshape(B, T, nh, hs)
            q_lat = jnp.einsum('bqhd,hdl->bhql', q, k_eff)
            attn = jnp.einsum('bhql,bkl->bhqk', q_lat, c_kv) / sqrt(hs)
            causal = jnp.tril(jnp.ones((T, T), dtype=bool))
            attn = jnp.where(causal[None, None], attn, -jnp.inf)
            attn = jax.nn.softmax(attn, axis=-1)
            y_lat = jnp.einsum('bhqk,bkl->bhql', attn, c_kv)
            y = jnp.einsum('bhql,hld->bqhd', y_lat, v_eff).reshape(B, T, C)
            return (y, c_kv)
        key = jax.random.key(seed)
        ks = jax.random.split(key, 7)
        B, T, C = (2, 256, 128)
        QL, KVL = (64, 64)
        return {'x': jax.random.normal(ks[0], (B, T, C), dtype=jnp.float32), 'W_dq': jax.random.normal(ks[1], (QL, C), dtype=jnp.float32) * W_SCALE, 'W_uq': jax.random.normal(ks[2], (C, QL), dtype=jnp.float32) * W_SCALE, 'W_dkv': jax.random.normal(ks[3], (KVL, C), dtype=jnp.float32) * W_SCALE, 'W_uk': jax.random.normal(ks[4], (C, KVL), dtype=jnp.float32) * W_SCALE, 'W_uv': jax.random.normal(ks[5], (C, KVL), dtype=jnp.float32) * W_SCALE, 'W_o': jax.random.normal(ks[6], (C, C), dtype=jnp.float32) * W_SCALE}
    _L0_attn_b_in = _L0_attn_b_setup()

    def _L0_ffn_setup():
        import jax, jax.numpy as jnp
        import numpy as np
        EPS = 1e-06
        N_EXPERTS = 8

        def _rms_norm(x, scale, eps=EPS):
            mean_sq = jnp.mean(x.astype(jnp.float32) ** 2, axis=-1, keepdims=True)
            s = scale.astype(jnp.float32) * jax.lax.rsqrt(mean_sq + eps)
            return x * s.astype(x.dtype)

        def _dist2(x, y):
            nx = jnp.sum(x ** 2, axis=-1)[..., :, None]
            ny = jnp.sum(y ** 2, axis=-1)[..., None, :]
            return nx + ny - 2.0 * (x @ y.T)
        key = jax.random.key(seed)
        ks = jax.random.split(key, 5)
        dim, hidden, E = (128, 256, N_EXPERTS)
        x = jax.random.normal(ks[0], (4, 256, dim), dtype=jnp.float32)
        scale = jnp.ones((dim,), dtype=jnp.float32)
        centroids = jax.random.normal(ks[1], (E, dim), dtype=jnp.float32)
        up_w = jax.random.normal(ks[2], (E, dim, hidden * 2), dtype=jnp.float32) * dim ** (-0.5)
        down_w = jax.random.normal(ks[3], (E, hidden, dim), dtype=jnp.float32) * hidden ** (-0.5)
        return {'x': x, 'scale': scale, 'centroids': centroids, 'up_w': up_w, 'down_w': down_w}
    _L0_ffn_in = _L0_ffn_setup()
    _d = {'L0_attn_a_x': _L0_attn_a_in['x'], 'L0_attn_a_W_q': _L0_attn_a_in['W_q'], 'L0_attn_a_b_q': _L0_attn_a_in['b_q'], 'L0_attn_a_W_k': _L0_attn_a_in['W_k'], 'L0_attn_a_b_k': _L0_attn_a_in['b_k'], 'L0_attn_a_W_v': _L0_attn_a_in['W_v'], 'L0_attn_a_b_v': _L0_attn_a_in['b_v'], 'L0_attn_a_W_o': _L0_attn_a_in['W_o'], 'L0_attn_a_b_o': _L0_attn_a_in['b_o'], 'L0_attn_b_W_dq': _L0_attn_b_in['W_dq'], 'L0_attn_b_W_uq': _L0_attn_b_in['W_uq'], 'L0_attn_b_W_dkv': _L0_attn_b_in['W_dkv'], 'L0_attn_b_W_uk': _L0_attn_b_in['W_uk'], 'L0_attn_b_W_uv': _L0_attn_b_in['W_uv'], 'L0_attn_b_W_o': _L0_attn_b_in['W_o'], 'L0_ffn_scale': _L0_ffn_in['scale'], 'L0_ffn_centroids': _L0_ffn_in['centroids'], 'L0_ffn_up_w': _L0_ffn_in['up_w'], 'L0_ffn_down_w': _L0_ffn_in['down_w']}
    _x0 = _d['L0_attn_a_x']
    _d['L0_attn_a_x'] = jax.random.normal(jax.random.fold_in(jax.random.key(seed), 1), (8, 512, 128), dtype=_x0.dtype)
    del _x0
    return _d

def reference(L0_attn_a_x, L0_attn_a_W_q, L0_attn_a_b_q, L0_attn_a_W_k, L0_attn_a_b_k, L0_attn_a_W_v, L0_attn_a_b_v, L0_attn_a_W_o, L0_attn_a_b_o, L0_attn_b_W_dq, L0_attn_b_W_uq, L0_attn_b_W_dkv, L0_attn_b_W_uk, L0_attn_b_W_uv, L0_attn_b_W_o, L0_ffn_scale, L0_ffn_centroids, L0_ffn_up_w, L0_ffn_down_w):

    def _L0_attn_a_ref(x, W_q, b_q, W_k, b_k, W_v, b_v, W_o, b_o):
        import jax, jax.numpy as jnp
        import numpy as np
        D_MODEL = 128
        NUM_HEADS = 16
        D_HEAD = D_MODEL // NUM_HEADS
        NEG_BIG = 10000000000.0
        B, S, d = x.shape
        H, Dh = (NUM_HEADS, D_HEAD)
        Q = x @ W_q + b_q
        K = x @ W_k + b_k
        V = x @ W_v + b_v
        Qh = Q.reshape(B, S, H, Dh).transpose(0, 2, 1, 3)
        Kh = K.reshape(B, S, H, Dh).transpose(0, 2, 1, 3)
        Vh = V.reshape(B, S, H, Dh).transpose(0, 2, 1, 3)
        scores = jnp.einsum('bhid,bhjd->bhij', Qh, Kh) / jnp.sqrt(jnp.asarray(Dh, dtype=x.dtype))
        causal = jnp.tril(jnp.ones((S, S), dtype=x.dtype))
        scores = scores * causal - NEG_BIG * (1.0 - causal)
        attn = jax.nn.softmax(scores, axis=-1)
        vals = jnp.einsum('bhij,bhjd->bhid', attn, Vh)
        vals = vals.transpose(0, 2, 1, 3).reshape(B, S, d)
        return vals @ W_o + b_o

    def _L0_attn_b_ref(x, W_dq, W_uq, W_dkv, W_uk, W_uv, W_o):
        import jax, jax.numpy as jnp
        import numpy as np
        from math import sqrt
        N_HEAD = 16
        W_SCALE = 0.02

        def _reference_tuple_inner(x, W_dq, W_uq, W_dkv, W_uk, W_uv, W_o):
            B, T, C = x.shape
            nh = N_HEAD
            hs = C // nh
            n_kvl = W_dkv.shape[0]
            k_eff = (W_dq.T @ W_uq.T @ W_uk).reshape(nh, hs, n_kvl)
            v_eff = jnp.transpose((W_uv.T @ W_o.T).reshape(n_kvl, nh, hs), (1, 0, 2))
            c_kv = x @ W_dkv.T
            q = x @ W_dq.T @ W_uq.T
            q = q.reshape(B, T, nh, hs)
            q_lat = jnp.einsum('bqhd,hdl->bhql', q, k_eff)
            attn = jnp.einsum('bhql,bkl->bhqk', q_lat, c_kv) / sqrt(hs)
            causal = jnp.tril(jnp.ones((T, T), dtype=bool))
            attn = jnp.where(causal[None, None], attn, -jnp.inf)
            attn = jax.nn.softmax(attn, axis=-1)
            y_lat = jnp.einsum('bhqk,bkl->bhql', attn, c_kv)
            y = jnp.einsum('bhql,hld->bqhd', y_lat, v_eff).reshape(B, T, C)
            return (y, c_kv)
        return _reference_tuple_inner(x, W_dq, W_uq, W_dkv, W_uk, W_uv, W_o)[0]

    def _L0_ffn_ref(x, scale, centroids, up_w, down_w):
        import jax, jax.numpy as jnp
        import numpy as np
        EPS = 1e-06
        N_EXPERTS = 8

        def _rms_norm(x, scale, eps=EPS):
            mean_sq = jnp.mean(x.astype(jnp.float32) ** 2, axis=-1, keepdims=True)
            s = scale.astype(jnp.float32) * jax.lax.rsqrt(mean_sq + eps)
            return x * s.astype(x.dtype)

        def _dist2(x, y):
            nx = jnp.sum(x ** 2, axis=-1)[..., :, None]
            ny = jnp.sum(y ** 2, axis=-1)[..., None, :]
            return nx + ny - 2.0 * (x @ y.T)
        skip = x
        xn = _rms_norm(x, scale)
        ids = jnp.argmin(_dist2(xn, centroids), axis=-1)
        out = jnp.zeros_like(x)
        for e in range(N_EXPERTS):
            h = jnp.einsum('bsd,dh->bsh', xn, up_w[e])
            a, g = jnp.split(h, 2, axis=-1)
            y = jnp.einsum('bsh,hd->bsd', a * jax.nn.silu(g), down_w[e])
            out = jnp.where((ids == e)[..., None], y, out)
        return out + skip
    x = L0_attn_a_x
    x = x + _L0_attn_a_ref(_layernorm(x, axis=-1), L0_attn_a_W_q, L0_attn_a_b_q, L0_attn_a_W_k, L0_attn_a_b_k, L0_attn_a_W_v, L0_attn_a_b_v, L0_attn_a_W_o, L0_attn_a_b_o)
    x = x + _L0_ffn_ref(_layernorm(x, axis=-1), L0_ffn_scale, L0_ffn_centroids, L0_ffn_up_w, L0_ffn_down_w)
    x = x + _L0_attn_b_ref(_layernorm(x, axis=-1), L0_attn_b_W_dq, L0_attn_b_W_uq, L0_attn_b_W_dkv, L0_attn_b_W_uk, L0_attn_b_W_uv, L0_attn_b_W_o)
    x = x + _L0_ffn_ref(_layernorm(x, axis=-1), L0_ffn_scale, L0_ffn_centroids, L0_ffn_up_w, L0_ffn_down_w)
    return x

_drawn_inputs = setup_inputs


def setup_inputs(seed=0):
    import zlib

    import numpy as np

    out = dict(_drawn_inputs(seed))
    spreads = {'L0_attn_a_b_q': (0.0, 0.1),
     'L0_attn_a_b_k': (0.0, 0.8),
     'L0_attn_a_b_v': (0.0, 0.1),
     'L0_attn_a_b_o': (0.0, 0.1),
     'L0_ffn_scale': (1.0, 0.2)}
    factors = {'L0_attn_b_W_dq': 8.0,
     'L0_attn_b_W_uq': 8.0,
     'L0_attn_b_W_dkv': 8.0,
     'L0_attn_b_W_uk': 8.0,
     'L0_attn_b_W_uv': 8.0,
     'L0_attn_b_W_o': 8.0}
    for name, (base, spread) in spreads.items():
        noise = np.random.default_rng([zlib.crc32(name.encode()), seed]).standard_normal(out[name].shape)
        drawn = base * np.exp(spread * noise) if base else spread * noise
        out[name] = jnp.asarray(drawn.astype(out[name].dtype))
    for name, factor in factors.items():
        out[name] = (out[name] * factor).astype(out[name].dtype)
    return out
```

```python
from contextlib import ExitStack

import concourse.bass as bass
from concourse import mybir

F32, BF16, I32 = mybir.dt.float32, mybir.dt.bfloat16, mybir.dt.int32
ALU = mybir.AluOpType
ACT = mybir.ActivationFunctionType
AX = mybir.AxisListType

P = 128
LN_EPS = 1e-5
RMS_EPS = 1e-6
MASKED = -1e30

STACK = 48
DIAGONAL = (4, 4, 3, 3, 2)
MROWS = 2
Q_SLOTS = (0, 1, 2, 0, 1, 0)
K_SLOTS = (0, 0, 0, 1, 1, 2)


def hybrid_layers(nc, x_in, Wq, bq, Wk, bk, Wv, bv, Wo, bo, Wdq, Wuq, Wdkv, Wuk, Wuv, Wob, ffn_scale,
                  centroids, up_w, down_w, out):
    B, S, C = x_in.shape
    NT = S // P
    TILES = B * NT
    H = 16
    DH = C // H
    NJ = H // 2
    QUADS = H // 4
    SCALE = float(DH) ** -0.5
    L = Wdq.shape[0]
    E = centroids.shape[0]
    F = down_w.shape[1]
    FC = F // P
    SLOTS = (TILES * P + E * (P - 1)) // P
    GROUP = 3
    GROUPS = SLOTS // GROUP
    assert SLOTS % GROUP == 0 and 2 * F <= S and E == 8 and TILES == 32
    assert C == P and NT == 4 and DH == 8 and L == 64

    with ExitStack() as ctx:
        def sb(name, shape, dt=F32):
            return ctx.enter_context(nc.sbuf_tensor(name, shape, dt))

        def psum(name, shape, dt=F32):
            return ctx.enter_context(nc.psum_tensor(name, shape, dt))

        def sem(name):
            return ctx.enter_context(nc.semaphore(name))

        x_sb = sb("x_sb", [P, TILES, C])
        ident = sb("ident", [P, P])
        ident_bf = sb("ident_bf", [P, P], BF16)
        mask2 = sb("mask2", [P, 2, P], BF16)
        mask2T = sb("mask2T", [P, 2, P], BF16)
        ones_row = sb("ones_row", [1, P])
        minus_half = sb("minus_half", [P, 8])
        w_q = sb("w_q", [P, 2, C])
        w_k = sb("w_k", [P, 2, C])
        w_v = sb("w_v", [P, 2, C])
        w_o = sb("w_o", [P, C])
        b_q = sb("b_q", [P, 2])
        b_k = sb("b_k", [P, 2])
        b_v = sb("b_v", [1, 2, C])
        b_o = sb("b_o", [1, C])
        w_dq = sb("w_dq", [L, C])
        w_uq = sb("w_uq", [C, L])
        w_dkv = sb("w_dkv", [L, C])
        w_uk = sb("w_uk", [C, L])
        w_uv = sb("w_uv", [C, L])
        w_ob = sb("w_ob", [C, C])
        w_uqT = sb("w_uqT", [L, C])
        w_obT = sb("w_obT", [C, C])
        qeffT = sb("qeffT", [C, C])
        keffT = sb("keffT", [L, C])
        veff = sb("veff", [L, C])

        credit = sb("credit", [P, 8])
        stats = sb("stats", [P, NT, 6])
        mean_var = sb("mean_var", [P, NT, 2])
        var_eps = sb("var_eps", [P, NT])
        rstd = sb("rstd", [P, NT])
        xn = sb("xn", [P, NT, C])
        xnT = sb("xnT", [P, S])
        qf = sb("qf", [P, S])
        kf = sb("kf", [P, S])
        rest = sb("rest", [P, S])
        q3 = sb("q3", [P, 3, S], BF16)
        k3 = sb("k3", [P, 3, S], BF16)
        q_stack = sb("q_stack", [P, 2, NJ, S], BF16)
        k_stack = sb("k_stack", [P, 2, NJ, S], BF16)
        v_ext = sb("v_ext", [P, 2, NT, H, 32])
        arena = sb("arena", [P, 2 * 10 * S])
        probs = arena[:].rearrange("p (b k s) -> p b k s", b=2, k=10)
        x_routed = arena[:, 0:TILES * C].rearrange("p (t c) -> p t c", c=C)
        y_routed = arena[:, TILES * C:2 * TILES * C].rearrange("p (t c) -> p t c", c=C)
        neg_max = sb("neg_max", [P, 4, 16])
        neg_maxT = sb("neg_maxT", [16, 4, P])
        max_parts = sb("max_parts", [16, 4, 2, P], BF16)
        o_T = sb("o_T", [P, 2, S])
        recip = sb("recip", [P, NT, 4])
        attn = sb("attn", [P, NT, C])
        attnT = sb("attnT", [P, S])

        w_up = sb("w_up", [P, E, 2 * F])
        w_down = sb("w_down", [P, E, FC, C])
        scale_col = sb("scale_col", [P, 1])
        cent = sb("cent", [E, C])
        centT = sb("centT", [P, E])
        cent_m2T = sb("cent_m2T", [P, E])
        cent_sqT = sb("cent_sqT", [P, E])
        ones_mat = sb("ones_mat", [P, P])
        before = sb("before", [P, P])
        zeros = sb("zeros", [P, C])
        expert_row = sb("expert_row", [P, NT, E])
        slot_row = sb("slot_row", [1, SLOTS, E])
        rms = sb("rms", [P, 5, NT])
        both_rstd = sb("both_rstd", [P, NT])
        xl = sb("xl", [P, NT, C])
        xnT_sq = sb("xnT_sq", [P, S])
        nearest = sb("nearest", [P, NT])
        farther = sb("farther", [P, NT, E])
        candidate = sb("candidate", [P, NT, E])
        chosen = sb("chosen", [P, NT])
        one_hot = sb("one_hot", [P, E, TILES])
        PAD = TILES // 2
        counts = sb("counts", [P, 2, E, PAD + TILES])
        slots_f = sb("slots_f", [P, 2, 2 * E])
        slots_i = sb("slots_i", [P, 2, E], I32)
        slots_of = sb("slots_of", [P, E])
        base_row = sb("base_row", [P, E])
        place = sb("place", [P, 3, E, TILES])
        place_f = sb("place_f", [P, TILES])
        place_i = sb("place_i", [P, TILES], I32)
        slot_past = sb("slot_past", [1, SLOTS, E])
        slot_f = sb("slot_f", [1, SLOTS])
        slot_expert = sb("slot_expert", [1, SLOTS], I32)
        rows = sb("rows", [P, GROUP, C])
        rowsT = sb("rowsT", [P, GROUP, P])
        gate = sb("gate", [P, GROUP, F])
        hidden = sb("hidden", [P, GROUP, F])
        hiddenT = sb("hiddenT", [P, GROUP, F])
        y_out = sb("y_out", [P, GROUP, C])

        x_slots = nc.dram_tensor("x_slots", [SLOTS * P, C], F32, kind="Internal").ap()
        y_slots = nc.dram_tensor("y_slots", [SLOTS * P, C], F32, kind="Internal").ap()
        q3_dram = nc.dram_tensor("q3_dram", [P, 3, S], BF16, kind="Internal").ap()
        k3_dram = nc.dram_tensor("k3_dram", [P, 3, S], BF16, kind="Internal").ap()

        s_ps = [psum(f"s_ps{i}", [P, S]) for i in range(3)]
        st_ps = [psum(f"st_ps{i}", [P, S]) for i in range(2)]
        pv_ps = psum("pv_ps", [P, S])
        a_ps = psum("a_ps", [P, S])
        d_ps = psum("d_ps", [P, S])

        loaded = sem("loaded")
        loaded_x = sem("loaded_x")
        consts_ready = sem("consts_ready")
        pool_step = sem("pool_step")
        ones_ready = sem("ones_ready")
        fold_done = sem("fold_done")
        fold_copied = sem("fold_copied")
        dve_step = sem("dve_step")
        pool_waited = sem("pool_waited")
        dve_waited = sem("dve_waited")
        mean_ready = sem("mean_ready")
        rstd_ready = sem("rstd_ready")
        xn_ready = sem("xn_ready")
        xT_full = sem("xT_full")
        xT_ready = sem("xT_ready")
        q_full = sem("q_full")
        k_full = sem("k_full")
        v_full = sem("v_full")
        qf_ready = sem("qf_ready")
        kf_ready = sem("kf_ready")
        v_ready = sem("v_ready")
        q3_ready = sem("q3_ready")
        k3_ready = sem("k3_ready")
        q3_saved = sem("q3_saved")
        k3_saved = sem("k3_saved")
        q_stacked = [sem(f"q_stacked{i}") for i in range(2)]
        k_stacked = [sem(f"k_stacked{i}") for i in range(2)]
        s_full = sem("s_full")
        s_free = sem("s_free")
        maxT_full = sem("maxT_full")
        maxT_ready = sem("maxT_ready")
        max_parts_ready = sem("max_parts_ready")
        max_placed = [sem(f"max_placed{i}") for i in range(4)]
        st_full = sem("st_full")
        exp_done = sem("exp_done")
        pv_done = sem("pv_done")
        oT_ready = sem("oT_ready")
        oTT_full = sem("oTT_full")
        attn_ready = sem("attn_ready")
        attnT_full = sem("attnT_full")
        attnT_ready = sem("attnT_ready")
        proj_full = sem("proj_full")
        x_updated = sem("x_updated")
        stored = sem("stored")
        dist_full = sem("dist_full")
        norm_sq_ready = sem("norm_sq_ready")
        routed = sem("routed")
        xs_copied = sem("xs_copied")
        counts_full = sem("counts_full")
        place_ready = sem("place_ready")
        ffn_step = sem("ffn_step")
        ffn_pool_step = sem("ffn_pool_step")
        setup_step = sem("setup_step")
        slots_zeroed = sem("slots_zeroed")
        sent = sem("sent")
        rows_loaded = sem("rows_loaded")
        rowsT_full = sem("rowsT_full")
        rowsT_ready = sem("rowsT_ready")
        up_full = sem("up_full")
        gate_ready = sem("gate_ready")
        hidden_ready = sem("hidden_ready")
        hiddenT_full = sem("hiddenT_full")
        hiddenT_ready = sem("hiddenT_ready")
        y_full = sem("y_full")
        y_copied = sem("y_copied")
        y_saved = sem("y_saved")
        returned = [sem(f"returned{i}") for i in range(B)]
        y_added = sem("y_added")

        S_BANKS, ST_BANKS, PT_BUFS, OT_BUFS = 3, 2, 2, 2
        N_LOADS = 34

        block = ctx.enter_context(nc.Block())

        def tok(t):
            return slice(t * P, (t + 1) * P)

        def batches(eng, layer):
            return eng.Fori(layer * B, layer * B + B)

        @block.sync
        def _(sp):
            n = 0

            def load(dst, src):
                sp.dma_start(dst, src).then_inc(loaded, 16)

            for i in range(B):
                sp.dma_start(x_sb[:, i * NT:(i + 1) * NT, :],
                             x_in[i].rearrange("(t p) c -> p t c", p=P)).then_inc(loaded_x, 16)
                if i == 0:
                    for w, src in ((w_q, Wq), (w_k, Wk)):
                        for half in range(2):
                            load(w[:, 0, half * 64:half * 64 + 64].rearrange("p (q e) -> p q e", q=QUADS),
                                 src.rearrange("p (q r e) -> r p q e", q=QUADS, r=2)[half])
                    for b, src in ((b_q, bq), (b_k, bk)):
                        for half in range(2):
                            for q in range(QUADS):
                                c0 = q * 32 + half * 16
                                load(b[half * 64 + q * 16:half * 64 + q * 16 + 16, 0:1],
                                     src[c0:c0 + 16].rearrange("(c o) -> c o", o=1))
                    load(w_v[:, 0, :], Wv)
                    load(b_v[:, 0, :], bv.rearrange("(o c) -> o c", o=1))
                    load(w_o[:], Wo)
                    load(b_o[:], bo.rearrange("(o c) -> o c", o=1))
                    load(w_dq[:], Wdq)
                    load(w_uq[:], Wuq)
                    load(w_dkv[:], Wdkv)
                    load(w_uk[:], Wuk)
                    load(w_uv[:], Wuv)
                    load(w_ob[:], Wob)
                    load(scale_col[:], ffn_scale.rearrange("(c o) -> c o", o=1))
                    load(cent[:], centroids)
                    load(w_up[:], up_w.rearrange("e d n -> d e n"))
                    load(w_down[:], down_w.rearrange("e (c f) d -> f e c d", c=FC))

            def place_max(g, p, q):
                sp.wait_ge(max_parts_ready, 4 * g + q + 1)
                for half in range(2):
                    for part in range(MROWS):
                        row = half * 64 + STACK + part
                        dst = q_stack[row:row + 1, p, 2 * q:2 * q + 2, :]
                        sp.dma_start(dst.rearrange("o j (t q) -> o (j t) q", q=P),
                                     max_parts[8 * half:8 * half + 8, q, part, :]
                                     ).then_inc(max_placed[q], 16)

            sp.wait_ge(ones_ready, 2)
            sp.wait_ge(consts_ready, 7)
            sp.dma_start(x_slots.rearrange("(s p) c -> p s c", p=P),
                         zeros[:].unsqueeze(1).broadcast_to([P, SLOTS, C])).then_inc(slots_zeroed, 16)

            def build_stack(g, p, parts_ready, parts, dram, saved, stack, slots, stacked):
                sp.wait_ge(parts_ready, 1 + g + 1)
                sp.dma_start(dram, parts[:]).then_inc(saved, 16)
                sp.wait_ge(saved, 16 * g + 16)
                for half in range(2):
                    for slot, part in enumerate(slots):
                        row = half * 64 + slot * DH
                        sp.dma_start(stack[row:row + DH, p, :, :],
                                     dram[half * 64:half * 64 + 64, part, :].rearrange("(j d) t -> d j t", d=DH)
                                     ).then_inc(stacked[p], 16)

            def expert_traffic(ffn):
                w0 = ffn * GROUPS

                def load_rows(w):
                    sp.dma_start(rows[:], x_slots[bass.ds((w - w0) * GROUP * P, GROUP * P), :].rearrange(
                        "(s p) c -> p s c", p=P)).then_inc(rows_loaded, 16)

                sp.wait_ge(sent, 16 * TILES * (ffn + 1))
                load_rows(w0)
                with sp.Fori(w0, w0 + GROUPS - 1) as w:
                    sp.wait_ge(rowsT_full, w + 1)
                    load_rows(w + 1)
                    sp.wait_ge(y_copied, w + 1)
                    sp.dma_start(y_slots[bass.ds((w - w0) * GROUP * P, GROUP * P), :].rearrange(
                        "(s p) c -> p s c", p=P), y_out[:]).then_inc(y_saved, 16)
                sp.wait_ge(y_copied, w0 + GROUPS)
                sp.dma_start(y_slots[(GROUPS - 1) * GROUP * P:, :].rearrange("(s p) c -> p s c", p=P),
                             y_out[:]).then_inc(y_saved, 16)

            for layer in range(2):
                with batches(sp, layer) as g:
                    build_stack(g, 0, q3_ready, q3, q3_dram, q3_saved, q_stack, Q_SLOTS, q_stacked)
                    build_stack(g, 0, k3_ready, k3, k3_dram, k3_saved, k_stack, K_SLOTS, k_stacked)
                    for q in range(QUADS):
                        place_max(g, 0, q)
                expert_traffic(layer)
            with sp.Fori(0, B) as i:
                sp.wait_ge(y_added, B + i + 1)
                sp.dma_start(out[i].rearrange("(t p) c -> p t c", p=P),
                             x_sb[:, bass.ds(i * NT, NT), :]).then_inc(stored, 16)
            sp.wait_ge(stored, 16 * B)

        @block.gpsimd
        def _(pool):
            def settle():
                pool.sem_inc(pool_waited, 1)

            def step(ins, n):
                ins.then_inc(pool_step, 1)
                pool.wait_ge(pool_step, n)
                if not isinstance(n, int):
                    settle()

            step(pool.memset(ident[:], 0.0), 1)
            step(pool.affine_select(out=ident[:], in_=ident[:], compare_op=ALU.not_equal, fill=1.0, base=0,
                                    pattern=[[-1, P]], channel_multiplier=1), 2)
            pool.tensor_copy(ident_bf[:], ident[:]).then_inc(consts_ready, 1)
            step(pool.memset(mask2[:], 0.0), 3)
            pool.affine_select(out=mask2[:], in_=mask2[:], compare_op=ALU.is_ge, fill=MASKED, base=0,
                               pattern=[[0, 2], [-1, P]], channel_multiplier=1).then_inc(consts_ready, 1)
            step(pool.memset(mask2T[:], 0.0), 4)
            pool.affine_select(out=mask2T[:], in_=mask2T[:], compare_op=ALU.is_ge, fill=MASKED, base=0,
                               pattern=[[0, 2], [1, P]], channel_multiplier=-1).then_inc(consts_ready, 1)
            pool.memset(ones_row[:], 1.0).then_inc(consts_ready, 1)
            pool.memset(minus_half[:], -0.5).then_inc(consts_ready, 1)
            pool.memset(zeros[:], 0.0).then_inc(setup_step, 1)
            pool.memset(ones_mat[:], 1.0).then_inc(setup_step, 1)
            pool.iota(expert_row[:], pattern=[[0, NT], [1, E]], base=0, channel_multiplier=0,
                      allow_small_or_imprecise_dtypes=True).then_inc(setup_step, 1)
            pool.iota(slot_row[:], pattern=[[1, SLOTS], [0, E]], base=0, channel_multiplier=0,
                      allow_small_or_imprecise_dtypes=True).then_inc(setup_step, 1)
            pool.memset(counts[:], 0.0).then_inc(setup_step, 1)
            pool.memset(slots_f[:], 0.0).then_inc(setup_step, 1)
            pool.wait_ge(setup_step, 6)
            pool.affine_select(out=before[:], in_=ones_mat[:], compare_op=ALU.is_gt, fill=0.0, base=0,
                               pattern=[[1, P]], channel_multiplier=-1).then_inc(setup_step, 1)
            pool.wait_ge(setup_step, 7)
            pool.memset(v_ext[:], 0.0).then_inc(consts_ready, 1)
            pool.wait_ge(consts_ready, 6)
            pool.memset(v_ext[:, :, :, :, DH:DH + 1], 1.0).then_inc(consts_ready, 1)
            pool.memset(credit[:, 0:1], 0.0).then_inc(q3_ready, 1)
            pool.memset(credit[:, 1:2], 0.0).then_inc(k3_ready, 1)
            STEP0 = 4
            STEPS = 1 + 6 + 4

            def root(ln, base):
                pool.wait_ge(mean_ready, ln + 1)
                settle()
                step(pool.tensor_scalar(var_eps[:], mean_var[:, :, 1], LN_EPS, None, ALU.add), base + 1)
                pool.tensor_tensor(out=rstd[:], in0=var_eps[:], in1=minus_half[:, 0:NT],
                                   op=ALU.pow).then_inc(rstd_ready, 1)

            def split3(g, base, full, full_ready, parts, saved, parts_ready):
                pool.wait_ge(full_ready, g + 1)
                settle()
                step(pool.tensor_copy(parts[:, 0, :], full[:]), base + 1)
                step(pool.tensor_tensor(out=rest[:], in0=full[:], in1=parts[:, 0, :], op=ALU.subtract), base + 2)
                step(pool.tensor_copy(parts[:, 1, :], rest[:]), base + 3)
                pool.tensor_tensor(out=parts[:, 2, :], in0=rest[:], in1=parts[:, 1, :],
                                   op=ALU.subtract).then_inc(parts_ready, 1)

            def split_max(g, base, q):
                pool.wait_ge(maxT_ready, 4 * g + q + 1)
                settle()
                step(pool.tensor_copy(max_parts[:, q, 0, :], neg_maxT[:, q, :]), base + 1)
                pool.tensor_tensor(out=max_parts[:, q, 1, :], in0=neg_maxT[:, q, :],
                                   in1=max_parts[:, q, 0, :], op=ALU.subtract).then_inc(max_parts_ready, 1)

            def ffn_root(g, ln, base):
                def next_reads(ins, n):
                    ins.then_inc(ffn_pool_step, 1)
                    pool.wait_ge(ffn_pool_step, base + n)
                    settle()

                half = minus_half[:, 0:NT]
                pool.wait_ge(mean_ready, ln + 1)
                settle()
                pool.wait_ge(routed, g)
                settle()
                next_reads(pool.tensor_scalar(rms[:, 0, :], mean_var[:, :, 1], LN_EPS, None, ALU.add), 1)
                next_reads(pool.tensor_tensor(out=rstd[:], in0=rms[:, 0, :], in1=half, op=ALU.pow), 2)
                next_reads(pool.tensor_tensor(out=rms[:, 1, :], in0=mean_var[:, :, 1], in1=rstd[:], op=ALU.mult), 3)
                next_reads(pool.tensor_tensor(out=rms[:, 2, :], in0=rms[:, 1, :], in1=rstd[:], op=ALU.mult), 4)
                next_reads(pool.tensor_scalar(rms[:, 3, :], rms[:, 2, :], RMS_EPS, None, ALU.add), 5)
                next_reads(pool.tensor_tensor(out=rms[:, 4, :], in0=rms[:, 3, :], in1=half, op=ALU.pow), 6)
                pool.tensor_tensor(out=both_rstd[:], in0=rms[:, 4, :], in1=rstd[:], op=ALU.mult).then_inc(rstd_ready, 1)

            def keep_rows(g, ffn, ln):
                pool.wait_ge(xn_ready, ln + 1)
                settle()
                pool.tensor_copy(x_routed[:, bass.ds((g - ffn * B) * NT, NT), :], xn[:]).then_inc(xs_copied, 1)

            def send_rows(ffn):
                pool.wait_ge(place_ready, ffn + 1)
                pool.wait_ge(xs_copied, B * (ffn + 1))
                pool.wait_ge(slots_zeroed, 16)
                for t in range(TILES):
                    pool.indirect_dma_start(x_slots, bass.IndirectOffsetOnAxis(ap=place_i[:, t:t + 1], axis=0),
                                            x_routed[:, t, :], None).then_inc(sent, 16)

            def fetch_rows(ffn):
                pool.wait_ge(y_saved, 16 * GROUPS * (ffn + 1))
                for t in range(TILES):
                    pool.indirect_dma_start(y_routed[:, t, :], None, y_slots,
                                            bass.IndirectOffsetOnAxis(ap=place_i[:, t:t + 1], axis=0)
                                            ).then_inc(returned[t // NT], 16)

            for layer in range(2):
                with batches(pool, layer) as g:
                    base = STEP0 + STEPS * g
                    root(g + layer * B, base)
                    split3(g, base + 1, qf, qf_ready, q3, q3_saved, q3_ready)
                    split3(g, base + 4, kf, kf_ready, k3, k3_saved, k3_ready)
                    for q in range(QUADS):
                        split_max(g, base + 7 + q, q)
                pool.wait_ge(x_updated, 1 + B * (layer + 1))
                with batches(pool, layer) as g:
                    ffn_root(g + 1, g + (layer + 1) * B, 6 * g)
                    keep_rows(g, layer, g + (layer + 1) * B)
                send_rows(layer)
                fetch_rows(layer)

        def s_bank(k):
            if k < 2:
                return [(k, NT - 1, 0)]
            if k < 4:
                return [(k - 2, 2, 0), (k - 2, 0, 3 * P)]
            return [(0, 1, 0), (1, 1, 2 * P)]

        def st_bank(k):
            if k < 2:
                return [(k, 0, 0)]
            if k < 4:
                return [(k - 2, 1, 0), (k - 2, 3, 3 * P)]
            return [(0, 2, 0), (1, 2, 2 * P)]

        @block.tensor
        def _(pe):
            def mm(o, l, r, start=True, stop=True, **kw):
                return pe.matmul(o, l, r, start=start, stop=stop, skip_group_check=True, **kw)

            pe.wait_ge(consts_ready, 7)
            pe.wait_ge(loaded, 16 * N_LOADS)
            pe.transpose(a_ps[:L, 0:C], w_uq[:], ident[:, :]).then_inc(fold_done, 1)
            pe.transpose(d_ps[:, 0:C], w_ob[:], ident[:, :]).then_inc(fold_done, 1)
            pe.wait_ge(fold_copied, 2)
            mm(a_ps[:, 0:C], w_dq[:], w_uqT[:]).then_inc(fold_done, 1)
            mm(d_ps[:, 0:C], w_uqT[:], w_dq[:]).then_inc(fold_done, 1)
            pe.wait_ge(fold_copied, 4)
            mm(a_ps[:L, 0:C], w_uk[:], qeffT[:]).then_inc(fold_done, 1)
            mm(d_ps[:L, 0:C], w_uv[:], w_obT[:]).then_inc(fold_done, 1)
            pe.wait_ge(fold_copied, 6)
            mm(a_ps[:, 0:C], w_dkv[:], keffT[:]).then_inc(fold_done, 1)
            mm(d_ps[:, 0:C], w_dkv[:], veff[:]).then_inc(fold_done, 1)
            pe.wait_ge(fold_copied, 8)
            pe.transpose(a_ps[:, 0:E], cent[:], ident[0:E, 0:E]).then_inc(fold_done, 1)
            pe.wait_ge(fold_copied, 9)
            mm(s_ps[0][:, 0:P], ident_bf[:], ident_bf[:]).then_inc(xT_full, 1)
            mm(s_ps[1][:, 0:P], ident_bf[:], ident_bf[:]).then_inc(pv_done, PT_BUFS)
            mm(s_ps[2][:, 0:P], ident_bf[:], ident_bf[:]).then_inc(oTT_full, OT_BUFS)

            mm(st_ps[0][:, 0:P], ident_bf[:], ident_bf[:]).then_inc(dist_full, 1)

            def transpose_x(ln):
                pe.wait_ge(xn_ready, ln + 1)
                for t in range(NT):
                    ins = pe.transpose(a_ps[:, tok(t)], xn[:, t, :], ident[:, :])
                ins.then_inc(xT_full, 1)

            def project(g, layer):
                pe.wait_ge(xT_ready, g + layer * B + 1)
                mm(a_ps[:], w_q[:, layer, :], xnT[:]).then_inc(q_full, 1)
                pe.wait_ge(qf_ready, g + 1)
                mm(a_ps[:], w_k[:, layer, :], xnT[:]).then_inc(k_full, 1)
                pe.wait_ge(kf_ready, g + 1)
                for t in range(NT):
                    ins = mm(a_ps[:, tok(t)], xnT[:, tok(t)], w_v[:, layer, :], start=(t == 0), stop=(layer == 1))
                    if layer == 0:
                        ins = mm(a_ps[:, tok(t)], ones_row[:], b_v[:, 0, :], start=False)
                ins.then_inc(v_full, 1)

            def scores(g, p, q, u):
                half, k = u % 2, u // 2
                n = 40 * g + 10 * q + u
                pe.wait_ge(s_free, S_BANKS + n if 10 * q + u == 0 else n + 1)
                ps = s_ps[(10 * q + u) % S_BANKS]
                if k < 2:
                    mm(ps[:, 3 * P:4 * P], ident_bf[:], mask2[:, 0, :], start=True, stop=False)
                elif k < 4:
                    mm(ps[:, 2 * P:4 * P], ident_bf[:], mask2[:], start=True, stop=False)
                else:
                    mm(ps[:, :].rearrange("p (n w) -> p n w", n=2)[:, :, P:2 * P], ident_bf[:], mask2[:],
                       start=True, stop=False)
                r = slice(64 * half, 64 * half + STACK)
                for head, t, col in s_bank(k):
                    w = (t + 1) * P
                    ins = mm(ps[:, col:col + w], q_stack[r, p, 2 * q + head, tok(t)],
                             k_stack[r, p, 2 * q + head, 0:w], start=False, tile_position=(64 * half, 0))
                ins.then_inc(s_full, 1)

            def scores_T(g, p, q, u):
                half, k = u % 2, u // 2
                n = 40 * g + 10 * q + u
                pe.wait_ge(exp_done, n + 1)
                ps = st_ps[(10 * q + u) % ST_BANKS]
                r = slice(64 * half, 64 * half + STACK + MROWS)
                blocks = ps[:].rearrange("p (n w) -> p n w", w=P)[:, ::DIAGONAL[k], :]
                mm(blocks, ident_bf[:], mask2T[:, 0:blocks.shape[1], :], start=True, stop=False)
                for head, t, col in st_bank(k):
                    w = S - t * P
                    ins = mm(ps[:, col:col + w], k_stack[r, p, 2 * q + head, tok(t)],
                             q_stack[r, p, 2 * q + head, t * P:S], start=False, tile_position=(64 * half, 0))
                ins.then_inc(st_full, 1)

            def weigh_values(g, p, q, t):
                n = 4 * g + q
                if t == 0:
                    pe.wait_ge(oT_ready, n + 1)
                pe.wait_ge(exp_done, ST_BANKS + 40 * g + 10 * q + (4, 8, 10, 8)[t])
                for half in range(2):
                    for head in range(2):
                        k = (head, 2 + head, 4, 2 + head)[t]
                        col = (0, 0, 2 * P * head, 3 * P)[t]
                        c = 2 * half + head
                        w = S - t * P
                        ins = mm(pv_ps[32 * c:32 * c + 32, t * P:S], v_ext[:, p, t, 4 * q + c, :],
                                 probs[:, q % 2, 2 * k + half, col:col + w], start=(t == 0), stop=(t == NT - 1),
                                 tile_position=(0, 32 * c))
                if t == NT - 1:
                    ins.then_inc(pv_done, 1)

            def transpose_max(g, q):
                pe.wait_ge(s_free, S_BANKS + 40 * g + 10 * (q + 1))
                pe.transpose(d_ps[0:16, 0:P], neg_max[:, q, :], ident[:, :]).then_inc(maxT_full, 1)

            def transpose_o(g, q):
                n = 4 * g + q
                pe.wait_ge(oT_ready, 1 + n + 1)
                for t in range(NT):
                    ins = pe.transpose(d_ps[:, tok(t)], o_T[:, q % 2, tok(t)], ident[:, :])
                ins.then_inc(oTT_full, 1)

            def project_out(g):
                pe.wait_ge(attn_ready, 4 * g + 4)
                for t in range(NT):
                    ins = pe.transpose(a_ps[:, tok(t)], attn[:, t, :], ident[:, :])
                ins.then_inc(attnT_full, 1)
                pe.wait_ge(attnT_ready, g + 1)
                for t in range(NT):
                    mm(d_ps[:, tok(t)], attnT[:, tok(t)], w_o[:], start=(t == 0), stop=False)
                    ins = mm(d_ps[:, tok(t)], ones_row[:], b_o[:], start=False)
                ins.then_inc(proj_full, 1)

            def distances(g, ln):
                pe.wait_ge(norm_sq_ready, g + 1)
                for t in range(NT):
                    o = d_ps[:, t * E:t * E + E]
                    mm(o, xnT[:, tok(t)], cent_m2T[:], start=(t == 0), stop=False)
                    mm(o, ones_mat[:], cent_sqT[:], start=False, stop=False)
                    ins = mm(o, xnT_sq[:, tok(t)], ones_mat[:, 0:E], start=False)
                ins.then_inc(dist_full, 1)

            def count_tokens():
                mm(s_ps[0][:, 0:E * TILES], before[:], one_hot[:].rearrange("p e t -> p (e t)"))
                mm(s_ps[1][:, 0:E * TILES], ones_mat[:], one_hot[:].rearrange("p e t -> p (e t)")
                   ).then_inc(counts_full, 1)

            def transpose_rows(w):
                pe.wait_ge(rows_loaded, 16 * w + 16)
                for j in range(GROUP):
                    ins = pe.transpose(a_ps[:, j * P:(j + 1) * P], rows[:, j, :], ident[:, :])
                ins.then_inc(rowsT_full, 1)

            def experts(ffn):
                w0 = ffn * GROUPS
                hT_ps = (st_ps[0], st_ps[1], pv_ps)

                def group(w, more):
                    pe.wait_ge(rowsT_ready, w + 1)
                    e_of = []
                    for j in range(GROUP):
                        e = pe.value_load(slot_expert[0:1, bass.ds((w - w0) * GROUP + j, 1)], min_val=0, max_val=E - 1)
                        e_of.append(e)
                        mm(s_ps[j][:, 0:2 * F], rowsT[:, j, :],
                           w_up[:, bass.ds(e, 1), :].rearrange("p o n -> p (o n)")).then_inc(up_full, 1)
                    if more:
                        transpose_rows(w + 1)
                    for j in range(GROUP):
                        pe.wait_ge(hidden_ready, GROUP * w + j + 1)
                        for c in range(FC):
                            ins = pe.transpose(hT_ps[j][:, c * P:(c + 1) * P], hidden[:, j, c * P:(c + 1) * P],
                                               ident[:, :])
                        ins.then_inc(hiddenT_full, 1)
                    for j in range(GROUP):
                        pe.wait_ge(hiddenT_ready, GROUP * w + j + 1)
                        for c in range(FC):
                            ins = mm(d_ps[:, j * P:(j + 1) * P], hiddenT[:, j, c * P:(c + 1) * P],
                                     w_down[:, bass.ds(e_of[j], 1), c, :].rearrange("p o n -> p (o n)"),
                                     start=(j == 0 and c == 0), stop=(c == FC - 1))
                    ins.then_inc(y_full, 1)

                transpose_rows(w0)
                with pe.Fori(w0, w0 + GROUPS - 1) as w:
                    group(w, True)
                group(w0 + GROUPS - 1, False)

            for layer in range(2):
                if layer == 1:
                    pe.wait_ge(y_added, B)
                with batches(pe, layer) as g:
                    pe.wait_ge(v_ready, g + 1)
                    transpose_x(g + layer * B)
                    project(g, layer)
                    pe.wait_ge(q_stacked[0], 16 * 12 * (g + 1))
                    pe.wait_ge(k_stacked[0], 16 * 12 * (g + 1))
                    for q in range(QUADS):
                        for u in range(10):
                            scores(g, 0, q, u)
                    pe.wait_ge(x_updated, g + 1)
                    for q in range(QUADS):
                        if q:
                            pe.wait_ge(maxT_ready, 4 * g + q)
                        transpose_max(g, q)
                    pe.wait_ge(v_ready, 1 + g + 1)
                    for q in range(QUADS):
                        pe.wait_ge(max_placed[q], 64 * (g + 1))
                        for u in range(10):
                            scores_T(g, 0, q, u)
                        for t in range(NT):
                            weigh_values(g, 0, q, t)
                        if q == 0:
                            pe.wait_ge(maxT_ready, 4 * g + 4)
                        else:
                            pe.wait_ge(attn_ready, 4 * g + q)
                        transpose_o(g, q)
                    if layer == 0:
                        project_out(g)
                pe.wait_ge(x_updated, 1 + B * (layer + 1))
                with batches(pe, layer) as g:
                    transpose_x(g + (layer + 1) * B)
                    distances(g, g + (layer + 1) * B)
                pe.wait_ge(routed, 1 + B * (layer + 1))
                count_tokens()
                pe.wait_ge(place_ready, layer + 1)
                experts(layer)

        @block.scalar
        def _(act):
            act.wait_ge(consts_ready, 7)
            act.copy(credit[0:1, 4:5], ones_row[0:1, 0:1]).then_inc(exp_done, ST_BANKS)
            act.copy(credit[0:1, 5:6], ones_row[0:1, 0:1]).then_inc(oT_ready, 1)
            act.copy(credit[0:1, 6:7], ones_row[0:1, 0:1]).then_inc(v_ready, 1)
            act.wait_ge(loaded, 16 * N_LOADS)

            def copy_xT(ln):
                act.wait_ge(xT_full, 1 + ln + 1)
                act.copy(xnT[:], a_ps[:]).then_inc(xT_ready, 1)

            def scale_xT(g, ln):
                act.wait_ge(xT_full, 1 + ln + 1)
                act.wait_ge(dist_full, g + 1)
                act.activation(xnT[:], a_ps[:], ACT.Identity, scale=scale_col[:, 0:1]).then_inc(xT_ready, 1)
                act.activation(xnT_sq[:], a_ps[:], ACT.Square, scale=scale_col[:, 0:1]).then_inc(norm_sq_ready, 1)

            def expert_group(w):
                for j in range(GROUP):
                    act.wait_ge(up_full, GROUP * w + j + 1)
                    act.activation(gate[:, j, :], s_ps[j][:, F:2 * F], ACT.Silu).then_inc(gate_ready, 1)

            def copy_rowsT(w):
                act.wait_ge(rowsT_full, w + 1)
                act.activation(rowsT[:].rearrange("p s t -> p (s t)"), a_ps[:, 0:GROUP * P], ACT.Identity,
                               scale=scale_col[:, 0:1]).then_inc(rowsT_ready, 1)

            def copy_qkv(g, p, layer):
                act.wait_ge(q_full, g + 1)
                act.wait_ge(q3_ready, g + 1)
                if layer == 0:
                    act.activation(qf[:], a_ps[:], ACT.Identity, bias=b_q[:, 0:1]).then_inc(qf_ready, 1)
                else:
                    act.copy(qf[:], a_ps[:]).then_inc(qf_ready, 1)
                act.wait_ge(k_full, g + 1)
                act.wait_ge(k3_ready, g + 1)
                if layer == 0:
                    act.activation(kf[:], a_ps[:], ACT.Identity, bias=b_k[:, 0:1]).then_inc(kf_ready, 1)
                else:
                    act.copy(kf[:], a_ps[:]).then_inc(kf_ready, 1)
                act.wait_ge(v_full, g + 1)
                for t in range(NT):
                    ins = act.copy(v_ext[:, p, t, :, 0:DH], a_ps[:, tok(t)].rearrange("p (h d) -> p h d", h=H))
                ins.then_inc(v_ready, 1)

            def exps(g, q):
                act.wait_ge(pv_done, 4 * g + q + 1)
                for bank in range(10):
                    n = 40 * g + 10 * q + bank
                    act.wait_ge(st_full, n + 1)
                    act.activation(probs[:, q % 2, bank, :], st_ps[(10 * q + bank) % ST_BANKS][:], ACT.Exp,
                                   scale=SCALE).then_inc(exp_done, 1)

            def copy_oT(g, q):
                n = 4 * g + q
                act.wait_ge(pv_done, PT_BUFS + n + 1)
                act.wait_ge(oTT_full, n + 1)
                act.copy(o_T[:, q % 2, :], pv_ps[:]).then_inc(oT_ready, 1)

            for layer in range(2):
                with batches(act, layer) as g:
                    copy_xT(g + layer * B)
                    copy_qkv(g, 0, layer)
                    for q in range(QUADS):
                        exps(g, q)
                        copy_oT(g, q)
                    if layer == 0:
                        act.wait_ge(attnT_full, g + 1)
                        act.copy(attnT[:], a_ps[:]).then_inc(attnT_ready, 1)
                with batches(act, layer) as g:
                    scale_xT(g, g + (layer + 1) * B)
                w0 = layer * GROUPS
                copy_rowsT(w0)
                with act.Fori(w0, w0 + GROUPS - 1) as w:
                    expert_group(w)
                    copy_rowsT(w + 1)
                expert_group(w0 + GROUPS - 1)

        @block.vector
        def _(dve):
            def split_columns(dst, src):
                for half in range(2):
                    ins = dve.tensor_copy(dst[:, half * 64:half * 64 + 64].rearrange("p (q e) -> p q e", q=QUADS),
                                          src.rearrange("p (q r e) -> p r q e", q=QUADS, r=2)[:, half])
                return ins

            for half in range(2):
                dve.memset(k_stack[half * 64 + 32:half * 64 + 64, :, :, :], 1.0).then_inc(ones_ready, 1)
            dve.wait_ge(fold_done, 1)
            dve.tensor_copy(w_uqT[:], a_ps[:L, 0:C]).then_inc(fold_copied, 1)
            dve.wait_ge(fold_done, 2)
            dve.tensor_copy(w_obT[:], d_ps[:, 0:C]).then_inc(fold_copied, 1)
            dve.wait_ge(fold_done, 3)
            split_columns(w_q[:, 1, :], a_ps[:, 0:C]).then_inc(fold_copied, 1)
            dve.wait_ge(fold_done, 4)
            dve.tensor_copy(qeffT[:], d_ps[:, 0:C]).then_inc(fold_copied, 1)
            dve.wait_ge(fold_done, 5)
            dve.tensor_copy(keffT[:], a_ps[:L, 0:C]).then_inc(fold_copied, 1)
            dve.wait_ge(fold_done, 6)
            dve.tensor_copy(veff[:], d_ps[:L, 0:C]).then_inc(fold_copied, 1)
            dve.wait_ge(fold_done, 7)
            split_columns(w_k[:, 1, :], a_ps[:, 0:C]).then_inc(fold_copied, 1)
            dve.wait_ge(fold_done, 8)
            dve.tensor_copy(w_v[:, 1, :], d_ps[:, 0:C]).then_inc(fold_copied, 1)
            dve.wait_ge(fold_done, 9)
            dve.tensor_copy(centT[:], a_ps[:, 0:E]).then_inc(ffn_step, 1)
            dve.wait_ge(ffn_step, 1)
            dve.tensor_scalar(cent_m2T[:], centT[:], -2.0, None, ALU.mult)
            dve.tensor_tensor(out=cent_sqT[:], in0=centT[:], in1=centT[:], op=ALU.mult).then_inc(fold_copied, 1)
            dve.memset(credit[:, 7:8], 0.0).then_inc(routed, 1)
            dve.memset(credit[:, 2:3], 0.0).then_inc(s_free, S_BANKS)
            dve.memset(credit[:, 3:4], 0.0).then_inc(x_updated, 1)
            dve.wait_ge(loaded_x, 16 * B)

            DVE_STEPS = 1 + QUADS
            FFN_STEP0 = 1

            def x_tile(g, layer, t, n=1):
                return x_sb[:, bass.ds((g - layer * B) * NT + t, n), :]

            def means(g, layer, step_sem, base):
                for t in range(NT):
                    ins = dve.bn_stats(out=stats[:, t, :], in_=x_tile(g, layer, t).rearrange("p o c -> p (o c)"))
                ins.then_inc(step_sem, 1)
                dve.wait_ge(step_sem, base + 1)
                dve.sem_inc(dve_waited, 1)
                for t in range(NT):
                    ins = dve.bn_aggr(out=mean_var[:, t, :], in_=stats[:, t, :])
                ins.then_inc(mean_ready, 1)

            def normalize(g, layer):
                dve.wait_ge(rstd_ready, g + layer * B + 1)
                dve.wait_ge(xT_full, g + layer * B + 1)
                for t in range(NT):
                    ins = dve.tensor_scalar(xn[:, t, :], x_tile(g, layer, t).rearrange("p o c -> p (o c)"),
                                            mean_var[:, t, 0:1], rstd[:, t:t + 1], ALU.subtract, ALU.mult)
                ins.then_inc(xn_ready, 1)

            def row_max(g, q, u):
                half, k = u % 2, u // 2
                dve.wait_ge(s_full, 40 * g + 10 * q + u + 1)
                ps = s_ps[(10 * q + u) % S_BANKS]
                out_ = neg_max[:, q, :].rearrange("p (h j t) -> p h j t", h=2, j=2)[:, half]
                if k == 4:
                    ins = dve.tensor_reduce(out_[:, :, 1], ps[:].rearrange("p (h w) -> p h w", h=2),
                                            axis=AX.X, op=ALU.max, negate=True)
                else:
                    for head, t, col in s_bank(k):
                        ins = dve.tensor_reduce(out_[:, head, t:t + 1], ps[:, col:col + (t + 1) * P],
                                                axis=AX.X, op=ALU.max, negate=True)
                ins.then_inc(s_free, 1)

            def copy_maxT(g, q):
                dve.wait_ge(maxT_full, 4 * g + q + 1)
                dve.tensor_copy(neg_maxT[:, q, :], d_ps[0:16, 0:P]).then_inc(maxT_ready, 1)

            def divide(g, q, layer, base):
                n = 4 * g + q
                dve.wait_ge(oTT_full, OT_BUFS + n + 1)
                o = d_ps[:].rearrange("p (t h e) -> p t h e", t=NT, h=4)
                dve.reciprocal(recip[:], o[:, :, :, DH]).then_inc(dve_step, 1)
                dve.wait_ge(dve_step, base + 1)
                dve.tensor_tensor(out=attn[:, :, 32 * q:32 * q + 32].rearrange("p t (h d) -> p t h d", h=4),
                                  in0=o[:, :, :, 0:DH], in1=recip[:][:, :, :, None].broadcast_to([P, NT, 4, DH]),
                                  op=ALU.mult).then_inc(attn_ready, 1)

            ROUTE_STEPS = 8
            PLACE_STEPS = 20

            def flat(ap):
                return ap.rearrange("p o c -> p (o c)")

            def ffn_normalize(g, ffn, ln, base):
                dve.wait_ge(rstd_ready, ln + 1)
                dve.wait_ge(xT_full, ln + 1)
                dve.wait_ge(xs_copied, g)
                for t in range(NT):
                    x_t = flat(x_tile(g, ffn, t))
                    dve.tensor_scalar(xl[:, t, :], x_t, mean_var[:, t, 0:1], rstd[:, t:t + 1], ALU.subtract, ALU.mult)
                    ins = dve.tensor_scalar(xn[:, t, :], x_t, mean_var[:, t, 0:1], both_rstd[:, t:t + 1],
                                            ALU.subtract, ALU.mult)
                ins.then_inc(xn_ready, 1)
                dve.wait_ge(xn_ready, ln + 1)
                dve.tensor_tensor(out=x_tile(g, ffn, 0, NT), in0=xl[:], in1=x_tile(g, ffn, 0, NT),
                                  op=ALU.add).then_inc(ffn_step, 1)

            def choose(g, ffn, base):
                def next_reads(ins, n):
                    ins.then_inc(ffn_step, 1)
                    dve.wait_ge(ffn_step, base + n)

                dve.wait_ge(dist_full, 1 + g + 1)
                dist = d_ps[:, 0:NT * E].rearrange("p (t e) -> p t e", e=E)
                next_reads(dve.tensor_reduce(nearest[:], dist, axis=AX.X, op=ALU.min), 3)
                next_reads(dve.tensor_tensor(out=farther[:], in0=dist,
                                             in1=nearest[:].unsqueeze(2).broadcast_to([P, NT, E]), op=ALU.is_gt), 4)
                next_reads(dve.scalar_tensor_tensor(out=candidate[:].rearrange("p t e -> p (t e)"),
                                                    in0=farther[:].rearrange("p t e -> p (t e)"), scalar=float(E),
                                                    in1=expert_row[:].rearrange("p t e -> p (t e)"),
                                                    op0=ALU.mult, op1=ALU.add), 5)
                next_reads(dve.tensor_reduce(chosen[:], candidate[:], axis=AX.X, op=ALU.min), 6)
                dve.tensor_tensor(out=one_hot[:, :, bass.ds((g - ffn * B) * NT, NT)].rearrange("p e t -> p t e"),
                                  in0=expert_row[:], in1=chosen[:].unsqueeze(2).broadcast_to([P, NT, E]),
                                  op=ALU.is_equal).then_inc(routed, 1)

            def places(ffn, base):
                n = [base]

                def next_reads(ins):
                    ins.then_inc(ffn_step, 1)
                    n[0] += 1
                    dve.wait_ge(ffn_step, n[0])

                dve.wait_ge(counts_full, ffn + 1)
                next_reads(dve.tensor_copy(counts[:, 0, :, PAD:], s_ps[1][:, 0:E * TILES].rearrange(
                    "p (e t) -> p e t", e=E)))
                k, shift = 0, 1
                while shift < TILES:
                    next_reads(dve.tensor_tensor(out=counts[:, 1 - k, :, PAD:], in0=counts[:, k, :, PAD:],
                                                 in1=counts[:, k, :, PAD - shift:PAD - shift + TILES], op=ALU.add))
                    k, shift = 1 - k, 2 * shift
                next_reads(dve.tensor_scalar(slots_i[:, 0, :], counts[:, k, :, PAD + TILES - 1], float(P - 1), None,
                                             ALU.add))
                next_reads(dve.tensor_scalar(slots_i[:, 1, :], slots_i[:, 0, :], P.bit_length() - 1, None,
                                             ALU.arith_shift_right))
                next_reads(dve.tensor_copy(slots_of[:], slots_i[:, 1, :]))
                next_reads(dve.tensor_copy(slots_f[:, 0, E:], slots_of[:]))
                j, shift = 0, 1
                while shift < E:
                    next_reads(dve.tensor_tensor(out=slots_f[:, 1 - j, E:], in0=slots_f[:, j, E:],
                                                 in1=slots_f[:, j, E - shift:2 * E - shift], op=ALU.add))
                    j, shift = 1 - j, 2 * shift
                next_reads(dve.tensor_tensor(out=base_row[:], in0=slots_f[:, j, E:], in1=slots_of[:],
                                             op=ALU.subtract))
                next_reads(dve.scalar_tensor_tensor(
                    out=place[:, 0], in0=base_row[:].unsqueeze(2).broadcast_to([P, E, TILES]), scalar=float(P),
                    in1=counts[:, k, :, PAD - 1:PAD - 1 + TILES], op0=ALU.mult, op1=ALU.add))
                next_reads(dve.tensor_tensor(out=place[:, 1], in0=s_ps[0][:, 0:E * TILES].rearrange(
                    "p (e t) -> p e t", e=E), in1=place[:, 0], op=ALU.add))
                next_reads(dve.tensor_tensor(out=place[:, 2], in0=place[:, 1], in1=one_hot[:], op=ALU.mult))
                next_reads(dve.tensor_reduce(place_f[:], place[:, 2].rearrange("p e t -> p t e"), axis=AX.X,
                                             op=ALU.add))
                next_reads(dve.tensor_tensor(out=slot_past[:], in0=slot_row[:],
                                             in1=slots_f[0:1, j, E:].unsqueeze(1).broadcast_to([1, SLOTS, E]),
                                             op=ALU.is_ge))
                next_reads(dve.tensor_reduce(slot_f[:], slot_past[:], axis=AX.X, op=ALU.add))
                dve.tensor_scalar(slot_expert[:], slot_f[:], float(E - 1), None, ALU.min)
                dve.tensor_copy(place_i[:], place_f[:]).then_inc(place_ready, 1)
                assert n[0] - base == PLACE_STEPS, n[0] - base

            def expert_group(w):
                for j in range(GROUP):
                    n = GROUP * w + j + 1
                    dve.wait_ge(gate_ready, n)
                    dve.tensor_tensor(out=hidden[:, j, :], in0=s_ps[j][:, 0:F], in1=gate[:, j, :],
                                      op=ALU.mult).then_inc(hidden_ready, 1)
                hT_ps = (st_ps[0], st_ps[1], pv_ps)
                for j in range(GROUP):
                    dve.wait_ge(hiddenT_full, GROUP * w + j + 1)
                    dve.tensor_copy(hiddenT[:, j, :], hT_ps[j][:, 0:F]).then_inc(hiddenT_ready, 1)
                dve.wait_ge(y_full, w + 1)
                dve.tensor_copy(y_out[:].rearrange("p s c -> p (s c)"), d_ps[:, 0:GROUP * C]).then_inc(y_copied, 1)

            for layer in range(2):
                if layer == 1:
                    dve.wait_ge(y_added, B)
                with batches(dve, layer) as g:
                    base = DVE_STEPS * g
                    means(g, layer, dve_step, base)
                    normalize(g, layer)
                    for q in range(QUADS):
                        for u in range(10):
                            row_max(g, q, u)
                    for q in range(QUADS):
                        copy_maxT(g, q)
                    for q in range(QUADS):
                        divide(g, q, layer, base + 1 + q)
                    if layer == 0:
                        dve.wait_ge(proj_full, g + 1)
                        dve.tensor_tensor(out=x_tile(g, 0, 0, NT), in0=d_ps[:].rearrange("p (t c) -> p t c", t=NT),
                                          in1=x_tile(g, 0, 0, NT), op=ALU.add).then_inc(x_updated, 1)
                    else:
                        dve.wait_ge(attn_ready, 4 * g + 4)
                        dve.tensor_tensor(out=x_tile(g, 1, 0, NT), in0=attn[:], in1=x_tile(g, 1, 0, NT),
                                          op=ALU.add).then_inc(x_updated, 1)
                dve.wait_ge(x_updated, 1 + B * (layer + 1))
                route0 = 1 + layer * PLACE_STEPS
                with batches(dve, layer) as g:
                    base = route0 + 6 * g
                    means(g, layer, ffn_step, base)
                    ffn_normalize(g, layer, g + (layer + 1) * B, base)
                    choose(g, layer, base)
                places(layer, route0 + 6 * B * (layer + 1))
                w0 = layer * GROUPS
                expert_group(w0)
                with dve.Fori(w0 + 1, w0 + GROUPS) as w:
                    dve.wait_ge(y_saved, 16 * w)
                    expert_group(w)
                for b in range(B):
                    dve.wait_ge(returned[b], 16 * NT * (layer + 1))
                    dve.tensor_tensor(out=x_sb[:, b * NT:(b + 1) * NT, :], in0=y_routed[:, b * NT:(b + 1) * NT, :],
                                      in1=x_sb[:, b * NT:(b + 1) * NT, :], op=ALU.add).then_inc(y_added, 1)


_INS = ['L0_attn_a_x', 'L0_attn_a_W_q', 'L0_attn_a_b_q', 'L0_attn_a_W_k', 'L0_attn_a_b_k', 'L0_attn_a_W_v',
        'L0_attn_a_b_v', 'L0_attn_a_W_o', 'L0_attn_a_b_o', 'L0_attn_b_W_dq', 'L0_attn_b_W_uq', 'L0_attn_b_W_dkv',
        'L0_attn_b_W_uk', 'L0_attn_b_W_uv', 'L0_attn_b_W_o', 'L0_ffn_scale', 'L0_ffn_centroids', 'L0_ffn_up_w',
        'L0_ffn_down_w']


def kernel(**inputs):
    import numpy as _np
    import concourse.bacc as _bacc
    from concourse import mybir as _mybir
    from concourse.bass_utils import run_bass_kernel_spmd as _run

    nc = _bacc.Bacc("TRN2", target_bir_lowering=False, num_devices=1)
    arrays, args = {}, []
    for name in _INS:
        a = _np.ascontiguousarray(inputs[name])
        arrays[f"in_{name}_dram"] = a
        args.append(nc.dram_tensor(f"in_{name}_dram", a.shape, _mybir.dt.from_np(a.dtype), kind="ExternalInput").ap())
    shape = inputs['L0_attn_a_x'].shape
    args.append(nc.dram_tensor("out_0_dram", shape, _mybir.dt.float32, kind="ExternalOutput").ap())
    hybrid_layers(nc, *args)
    r = _run(nc, [arrays], core_ids=[0])
    return r.results[0]["out_0_dram"]
```

```python
from contextlib import ExitStack

import concourse.bass as bass
from concourse import mybir

F32, BF16, I32 = mybir.dt.float32, mybir.dt.bfloat16, mybir.dt.int32
ALU = mybir.AluOpType
ACT = mybir.ActivationFunctionType
AX = mybir.AxisListType

P = 128
LN_EPS = 1e-5
RMS_EPS = 1e-6
MASKED = -1e30

STACK = 48
DIAGONAL = (4, 4, 3, 3, 2)
MROWS = 2
Q_SLOTS = (0, 1, 2, 0, 1, 0)
K_SLOTS = (0, 0, 0, 1, 1, 2)


def hybrid_layers(nc, x_in, Wq, bq, Wk, bk, Wv, bv, Wo, bo, Wdq, Wuq, Wdkv, Wuk, Wuv, Wob, ffn_scale,
                  centroids, up_w, down_w, out):
    B, S, C = x_in.shape
    NT = S // P
    TILES = B * NT
    H = 16
    DH = C // H
    NJ = H // 2
    QUADS = H // 4
    SCALE = float(DH) ** -0.5
    L = Wdq.shape[0]
    E = centroids.shape[0]
    F = down_w.shape[1]
    FC = F // P
    SLOTS = (TILES * P + E * (P - 1)) // P
    GROUP = 3
    GROUPS = SLOTS // GROUP
    assert SLOTS % GROUP == 0 and 2 * F <= S and E == 8 and TILES == 32
    assert C == P and NT == 4 and DH == 8 and L == 64

    with ExitStack() as ctx:
        def sb(name, shape, dt=F32):
            return ctx.enter_context(nc.sbuf_tensor(name, shape, dt))

        def psum(name, shape, dt=F32):
            return ctx.enter_context(nc.psum_tensor(name, shape, dt))

        def sem(name):
            return ctx.enter_context(nc.semaphore(name))

        x_sb = sb("x_sb", [P, TILES, C])
        ident = sb("ident", [P, P])
        ident_bf = sb("ident_bf", [P, P], BF16)
        mask2 = sb("mask2", [P, 2, P], BF16)
        mask2T = sb("mask2T", [P, 2, P], BF16)
        ones_row = sb("ones_row", [1, P])
        minus_half = sb("minus_half", [P, TILES])
        w_q = sb("w_q", [P, 2, C])
        w_k = sb("w_k", [P, 2, C])
        w_v = sb("w_v", [P, 2, C])
        w_o = sb("w_o", [P, C])
        w_natural = sb("w_natural", [P, 2, C])
        b_natural = sb("b_natural", [1, 2, C])
        b_ordered = sb("b_ordered", [1, 2, C])
        b_qk = sb("b_qk", [P, 2, E])
        b_v = sb("b_v", [1, 2, C])
        b_o = sb("b_o", [1, C])
        w_dq = sb("w_dq", [L, C])
        w_uq = sb("w_uq", [C, L])
        w_dkv = sb("w_dkv", [L, C])
        w_uk = sb("w_uk", [C, L])
        w_uv = sb("w_uv", [C, L])
        w_ob = sb("w_ob", [C, C])
        w_uqT = sb("w_uqT", [L, C])
        w_obT = sb("w_obT", [C, C])
        qeffT = sb("qeffT", [C, C])
        keffT = sb("keffT", [L, C])
        veff = sb("veff", [L, C])

        credit = sb("credit", [P, 8])
        stats = sb("stats", [P, NT, 6])
        att_stats = sb("att_stats", [P, TILES, 6])
        att_mean_var = sb("att_mean_var", [P, TILES, 2])
        att_var_eps = sb("att_var_eps", [P, TILES])
        att_rstd = sb("att_rstd", [P, TILES])
        mean_var = sb("mean_var", [P, NT, 2])
        rstd = sb("rstd", [P, NT])
        xn = sb("xn", [P, NT, C])
        xnT = sb("xnT", [P, S])
        qf = sb("qf", [P, S])
        kf = sb("kf", [P, S])
        q_rest = sb("q_rest", [P, S])
        k_rest = sb("k_rest", [P, S])
        q3 = sb("q3", [P, 3, S], BF16)
        k3 = sb("k3", [P, 3, S], BF16)
        q_stack = sb("q_stack", [P, 2, NJ, S], BF16)
        k_stack = sb("k_stack", [P, 2, NJ, S], BF16)
        v_ext = sb("v_ext", [P, 2, NT, H, 32])
        arena = sb("arena", [P, 2 * 10 * S])
        probs = arena[:].rearrange("p (b k s) -> p b k s", b=2, k=10)
        x_routed = arena[:, 0:TILES * C].rearrange("p (t c) -> p t c", c=C)
        y_routed = arena[:, TILES * C:2 * TILES * C].rearrange("p (t c) -> p t c", c=C)
        neg_max = sb("neg_max", [P, 4, 16])
        neg_maxT = sb("neg_maxT", [16, 4, P])
        max_parts = sb("max_parts", [16, 4, 2, P], BF16)
        o_T = sb("o_T", [P, 2, S])
        recip = sb("recip", [P, NT, 4])
        attn = sb("attn", [P, NT, C])
        attnT = sb("attnT", [P, S])

        w_up = sb("w_up", [P, E, 2 * F])
        w_down = sb("w_down", [P, E, FC, C])
        scale_col = sb("scale_col", [P, 1])
        cent = sb("cent", [E, C])
        centT = sb("centT", [P, E])
        cent_m2T = sb("cent_m2T", [P, E])
        cent_sqT = sb("cent_sqT", [P, E])
        ones_mat = sb("ones_mat", [P, P])
        before = sb("before", [P, P])
        zeros = sb("zeros", [P, C])
        expert_row = sb("expert_row", [P, NT, E])
        slot_row = sb("slot_row", [1, SLOTS, E])
        rms = sb("rms", [P, 5, NT])
        both_rstd = sb("both_rstd", [P, NT])
        xl = sb("xl", [P, NT, C])
        xnT_sq = sb("xnT_sq", [P, S])
        nearest = sb("nearest", [P, NT])
        farther = sb("farther", [P, NT, E])
        candidate = sb("candidate", [P, NT, E])
        chosen = sb("chosen", [P, NT])
        one_hot = sb("one_hot", [P, E, TILES])
        PAD = TILES // 2
        counts = sb("counts", [P, 2, E, PAD + TILES])
        slots_f = sb("slots_f", [P, 2, 2 * E])
        slots_i = sb("slots_i", [P, 2, E], I32)
        slots_of = sb("slots_of", [P, E])
        base_row = sb("base_row", [P, E])
        place = sb("place", [P, 3, E, TILES])
        place_f = sb("place_f", [P, TILES])
        place_i = sb("place_i", [P, TILES], I32)
        slot_past = sb("slot_past", [1, SLOTS, E])
        slot_f = sb("slot_f", [1, SLOTS])
        slot_expert = sb("slot_expert", [1, SLOTS], I32)
        rows = sb("rows", [P, GROUP, C])
        rowsT = sb("rowsT", [P, GROUP, P])
        gate = sb("gate", [P, GROUP, F])
        hidden = sb("hidden", [P, GROUP, F])
        hiddenT = sb("hiddenT", [P, GROUP, F])
        y_out = sb("y_out", [P, GROUP, C])

        x_slots = nc.dram_tensor("x_slots", [SLOTS * P, C], F32, kind="Internal").ap()
        y_slots = nc.dram_tensor("y_slots", [SLOTS * P, C], F32, kind="Internal").ap()
        q_rows = nc.dram_tensor("q_rows", [2, len(Q_SLOTS), 64, S], BF16, kind="Internal").ap()
        k_rows = nc.dram_tensor("k_rows", [2, len(K_SLOTS), 64, S], BF16, kind="Internal").ap()

        s_ps = [psum(f"s_ps{i}", [P, S]) for i in range(3)]
        st_ps = [psum(f"st_ps{i}", [P, S]) for i in range(2)]
        pv_ps = psum("pv_ps", [P, S])
        a_ps = psum("a_ps", [P, S])
        d_ps = psum("d_ps", [P, S])

        loaded = sem("loaded")
        loaded_x = sem("loaded_x")
        consts_ready = sem("consts_ready")
        pool_step = sem("pool_step")
        ones_ready = sem("ones_ready")
        fold_done = sem("fold_done")
        fold_copied = sem("fold_copied")
        dve_step = sem("dve_step")
        pool_waited = sem("pool_waited")
        sp_waited = sem("sp_waited")
        dve_waited = sem("dve_waited")
        att_stats_done = sem("att_stats_done")
        att_root_step = sem("att_root_step")
        att_mean_ready = sem("att_mean_ready")
        att_rstd_ready = sem("att_rstd_ready")
        mean_ready = sem("mean_ready")
        rstd_ready = sem("rstd_ready")
        xn_ready = sem("xn_ready")
        xT_full = sem("xT_full")
        xT_ready = sem("xT_ready")
        q_full = sem("q_full")
        k_full = sem("k_full")
        v_full = sem("v_full")
        qf_ready = sem("qf_ready")
        kf_ready = sem("kf_ready")
        v_ready = sem("v_ready")
        q3_ready = sem("q3_ready")
        k3_ready = sem("k3_ready")
        q3_saved = sem("q3_saved")
        k3_saved = sem("k3_saved")
        stacked = [[sem(f"stacked{i}_{pair}") for pair in range(2)] for i in range(2)]
        k_split_step = sem("k_split_step")
        ordered = sem("ordered")
        s_full = sem("s_full")
        s_free = sem("s_free")
        maxT_full = sem("maxT_full")
        maxT_ready = sem("maxT_ready")
        max_parts_ready = sem("max_parts_ready")
        max_placed = [sem(f"max_placed{i}") for i in range(4)]
        st_full = sem("st_full")
        exp_done = sem("exp_done")
        pv_done = sem("pv_done")
        oT_ready = sem("oT_ready")
        oTT_full = sem("oTT_full")
        attn_ready = sem("attn_ready")
        attnT_full = sem("attnT_full")
        attnT_ready = sem("attnT_ready")
        proj_full = sem("proj_full")
        x_updated = sem("x_updated")
        stored = sem("stored")
        dist_full = sem("dist_full")
        norm_sq_ready = sem("norm_sq_ready")
        routed = sem("routed")
        xs_copied = sem("xs_copied")
        counts_full = sem("counts_full")
        place_ready = sem("place_ready")
        ffn_step = sem("ffn_step")
        ffn_pool_step = sem("ffn_pool_step")
        setup_step = sem("setup_step")
        slots_zeroed = sem("slots_zeroed")
        sent = sem("sent")
        rows_loaded = sem("rows_loaded")
        rowsT_full = sem("rowsT_full")
        rowsT_ready = sem("rowsT_ready")
        up_full = sem("up_full")
        gate_ready = sem("gate_ready")
        hidden_ready = sem("hidden_ready")
        hiddenT_full = sem("hiddenT_full")
        hiddenT_ready = sem("hiddenT_ready")
        y_full = sem("y_full")
        y_copied = sem("y_copied")
        y_saved = sem("y_saved")
        returned = [sem(f"returned{i}") for i in range(B)]
        y_added = sem("y_added")

        S_BANKS, ST_BANKS, PT_BUFS, OT_BUFS = 3, 2, 2, 2
        N_LOADS = 18

        block = ctx.enter_context(nc.Block())

        def tok(t):
            return slice(t * P, (t + 1) * P)

        def batches(eng, layer):
            return eng.Fori(layer * B, layer * B + B)

        def run_slots(eng, layer, slot):
            b0 = layer * B
            for n in range(QUADS + 1):
                slot(b0 + n // QUADS, n // QUADS % 2, b0 // 2, n % QUADS)
            with eng.Fori(b0 // 2, b0 // 2 + B // 2 - 1) as i:
                for k in (1, 2):
                    for q in (1, 2, 3):
                        slot(2 * i + k, k % 2, i + k // 2, q)
                    slot(2 * i + k + 1, (k + 1) % 2, i + (k + 1) // 2, 0)
            for n in range(QUADS * (B - 1) + 1, QUADS * (B + 1) + 1):
                slot(b0 + n // QUADS, n // QUADS % 2, b0 // 2 + n // QUADS // 2, n % QUADS)

        def earlier(g, p, h, q, lag):
            if q >= lag:
                return g, p, q - lag
            return g - 1, 1 - p, q + QUADS - lag

        VALUES_AT = (2, 4, 7, 8)

        def within(g, layer):
            return not isinstance(g, int) or layer * B <= g < layer * B + B

        @block.sync
        def _(sp):
            def load(dst, src):
                sp.dma_start(dst, src).then_inc(loaded, 16)

            for i in range(B):
                sp.dma_start(x_sb[:, i * NT:(i + 1) * NT, :],
                             x_in[i].rearrange("(t p) c -> p t c", p=P)).then_inc(loaded_x, 16)
                if i == 0:
                    for n, (w, b) in enumerate(((Wq, bq), (Wk, bk))):
                        load(w_natural[:, n, :], w)
                        load(b_natural[:, n, :], b.rearrange("(o c) -> o c", o=1))
                    load(w_v[:, 0, :], Wv)
                    load(b_v[:, 0, :], bv.rearrange("(o c) -> o c", o=1))
                    load(w_o[:], Wo)
                    load(b_o[:], bo.rearrange("(o c) -> o c", o=1))
                    load(w_dq[:], Wdq)
                    load(w_uq[:], Wuq)
                    load(w_dkv[:], Wdkv)
                    load(w_uk[:], Wuk)
                    load(w_uv[:], Wuv)
                    load(w_ob[:], Wob)
                    load(scale_col[:], ffn_scale.rearrange("(c o) -> c o", o=1))
                    load(cent[:], centroids)
                    load(w_up[:], up_w.rearrange("e d n -> d e n"))
                    load(w_down[:], down_w.rearrange("e (c f) d -> f e c d", c=FC))

            def place_max(g, p, q):
                sp.wait_ge(max_parts_ready, 4 * g + q + 1)
                for half in range(2):
                    for part in range(MROWS):
                        row = half * 64 + STACK + part
                        dst = q_stack[row:row + 1, p, 2 * q:2 * q + 2, :]
                        sp.dma_start(dst.rearrange("o j (t q) -> o (j t) q", q=P),
                                     max_parts[8 * half:8 * half + 8, q, part, :]
                                     ).then_inc(max_placed[q % 2], 16)

            sp.wait_ge(ones_ready, 2)
            sp.wait_ge(consts_ready, 7)
            sp.dma_start(x_slots.rearrange("(s p) c -> p s c", p=P),
                         zeros[:].unsqueeze(1).broadcast_to([P, SLOTS, C])).then_inc(slots_zeroed, 16)

            def save_rows(g, ready, parts, rows, runs, saved):
                sp.wait_ge(ready, 1 + g + 1)
                for half in range(2):
                    r = slice(64 * half, 64 * half + 64)
                    for slot, n, part, part_step in runs:
                        src = (parts[r, part:part + n, :] if part_step else
                               parts[r, part, :].unsqueeze(1).broadcast_to([64, n, S]))
                        sp.dma_start(rows[half, slot:slot + n].rearrange("s r t -> r s t"), src).then_inc(saved, 16)

            Q_RUNS = ((0, 3, 0, 1), (3, 2, 0, 1), (5, 1, 0, 1))
            K_RUNS = ((0, 3, 0, 0), (3, 2, 1, 0), (5, 1, 2, 0))

            def save_keys(g):
                save_rows(g, k3_ready, k3, k_rows, K_RUNS, k3_saved)

            def save_queries(g):
                save_rows(g, q3_ready, q3, q_rows, Q_RUNS, q3_saved)

            def load_stacks(g, p, pair):
                sp.wait_ge(k3_saved, 96 * g + 96)
                sp.wait_ge(q3_saved, 96 * g + 96)
                for rows, stack in ((k_rows, k_stack), (q_rows, q_stack)):
                    for half in range(2):
                        sp.dma_start(stack[half * 64:half * 64 + STACK, p, 4 * pair:4 * pair + 4, :],
                                     rows[half].rearrange("s (d j) t -> (s d) j t", j=NJ)[:, 4 * pair:4 * pair + 4, :]
                                     ).then_inc(stacked[p][pair], 16)

            def expert_traffic(ffn):
                w0 = ffn * GROUPS

                def load_rows(w):
                    sp.dma_start(rows[:], x_slots[bass.ds((w - w0) * GROUP * P, GROUP * P), :].rearrange(
                        "(s p) c -> p s c", p=P)).then_inc(rows_loaded, 16)

                sp.wait_ge(sent, 16 * TILES * (ffn + 1))
                load_rows(w0)
                with sp.Fori(w0, w0 + GROUPS - 1) as w:
                    sp.wait_ge(rowsT_full, w + 1)
                    load_rows(w + 1)
                    sp.wait_ge(y_copied, w + 1)
                    sp.dma_start(y_slots[bass.ds((w - w0) * GROUP * P, GROUP * P), :].rearrange(
                        "(s p) c -> p s c", p=P), y_out[:]).then_inc(y_saved, 16)
                sp.wait_ge(y_copied, w0 + GROUPS)
                sp.dma_start(y_slots[(GROUPS - 1) * GROUP * P:, :].rearrange("(s p) c -> p s c", p=P),
                             y_out[:]).then_inc(y_saved, 16)

            for layer in range(2):
                if layer == 1:
                    sp.wait_ge(stacked[1][1], 64 * (B // 2))
                save_keys(layer * B)
                save_queries(layer * B)
                for pair in range(2):
                    load_stacks(layer * B, 0, pair)

                def slot(g, p, h, q):
                    g1, p1, q1 = earlier(g, p, h, q, 1)
                    if q == 1 and within(g + 1, layer):
                        sp.wait_ge(stacked[p][1], 64 * (h + 1))
                        sp.sem_inc(sp_waited, 1)
                    if within(g1, layer):
                        place_max(g1, p1, q1)
                    if within(g + 1, layer):
                        if q == 1:
                            save_keys(g + 1)
                            save_queries(g + 1)
                        if q >= 2:
                            if not (isinstance(g, int) and g == layer * B):
                                sp.wait_ge(st_full, 40 * g - 20 if q == 2 else 40 * g)
                                sp.sem_inc(sp_waited, 1)
                            load_stacks(g + 1, 1 - p, q - 2)

                run_slots(sp, layer, slot)
                expert_traffic(layer)
            with sp.Fori(0, B) as i:
                sp.wait_ge(y_added, B + i + 1)
                sp.dma_start(out[i].rearrange("(t p) c -> p t c", p=P),
                             x_sb[:, bass.ds(i * NT, NT), :]).then_inc(stored, 16)
            sp.wait_ge(stored, 16 * B)

        @block.gpsimd
        def _(pool):
            def settle():
                pool.sem_inc(pool_waited, 1)

            def step(ins, n):
                ins.then_inc(pool_step, 1)
                pool.wait_ge(pool_step, n)
                if not isinstance(n, int):
                    settle()

            step(pool.memset(ident[:], 0.0), 1)
            step(pool.affine_select(out=ident[:], in_=ident[:], compare_op=ALU.not_equal, fill=1.0, base=0,
                                    pattern=[[-1, P]], channel_multiplier=1), 2)
            pool.tensor_copy(ident_bf[:], ident[:]).then_inc(consts_ready, 1)
            step(pool.memset(mask2[:], 0.0), 3)
            pool.affine_select(out=mask2[:], in_=mask2[:], compare_op=ALU.is_ge, fill=MASKED, base=0,
                               pattern=[[0, 2], [-1, P]], channel_multiplier=1).then_inc(consts_ready, 1)
            step(pool.memset(mask2T[:], 0.0), 4)
            pool.affine_select(out=mask2T[:], in_=mask2T[:], compare_op=ALU.is_ge, fill=MASKED, base=0,
                               pattern=[[0, 2], [1, P]], channel_multiplier=-1).then_inc(consts_ready, 1)
            pool.memset(ones_row[:], 1.0).then_inc(consts_ready, 1)
            pool.memset(minus_half[:], -0.5).then_inc(consts_ready, 1)
            pool.memset(zeros[:], 0.0).then_inc(setup_step, 1)
            pool.memset(ones_mat[:], 1.0).then_inc(setup_step, 1)
            pool.iota(expert_row[:], pattern=[[0, NT], [1, E]], base=0, channel_multiplier=0,
                      allow_small_or_imprecise_dtypes=True).then_inc(setup_step, 1)
            pool.iota(slot_row[:], pattern=[[1, SLOTS], [0, E]], base=0, channel_multiplier=0,
                      allow_small_or_imprecise_dtypes=True).then_inc(setup_step, 1)
            pool.memset(counts[:], 0.0).then_inc(setup_step, 1)
            pool.memset(slots_f[:], 0.0).then_inc(setup_step, 1)
            pool.wait_ge(setup_step, 6)
            pool.affine_select(out=before[:], in_=ones_mat[:], compare_op=ALU.is_gt, fill=0.0, base=0,
                               pattern=[[1, P]], channel_multiplier=-1).then_inc(setup_step, 1)
            pool.wait_ge(setup_step, 7)
            pool.memset(v_ext[:], 0.0).then_inc(consts_ready, 1)
            pool.wait_ge(consts_ready, 6)
            pool.memset(v_ext[:, :, :, :, DH:DH + 1], 1.0).then_inc(consts_ready, 1)
            pool.memset(credit[:, 1:2], 0.0).then_inc(q3_ready, 1)
            STEP0 = 4
            STEPS = 2 + 4

            def attention_root(layer):
                pool.wait_ge(att_mean_ready, layer + 1)
                pool.tensor_scalar(att_var_eps[:], att_mean_var[:, :, 1], LN_EPS, None,
                                   ALU.add).then_inc(att_root_step, 1)
                pool.wait_ge(att_root_step, layer + 1)
                pool.tensor_tensor(out=att_rstd[:], in0=att_var_eps[:], in1=minus_half[:],
                                   op=ALU.pow).then_inc(att_rstd_ready, 1)

            def split_queries(g, base):
                pool.wait_ge(qf_ready, g + 1)
                settle()
                step(pool.tensor_tensor(out=q_rest[:], in0=qf[:], in1=q3[:, 0, :], op=ALU.subtract), base + 1)
                step(pool.tensor_copy(q3[:, 1, :], q_rest[:]), base + 2)
                pool.tensor_tensor(out=q3[:, 2, :], in0=q_rest[:], in1=q3[:, 1, :],
                                   op=ALU.subtract).then_inc(q3_ready, 1)

            def split_max(g, base, q):
                pool.wait_ge(maxT_ready, 4 * g + q + 1)
                settle()
                step(pool.tensor_copy(max_parts[:, q, 0, :], neg_maxT[:, q, :]), base + 1)
                pool.tensor_tensor(out=max_parts[:, q, 1, :], in0=neg_maxT[:, q, :],
                                   in1=max_parts[:, q, 0, :], op=ALU.subtract).then_inc(max_parts_ready, 1)

            def ffn_root(g, ln, base):
                def next_reads(ins, n):
                    ins.then_inc(ffn_pool_step, 1)
                    pool.wait_ge(ffn_pool_step, base + n)
                    settle()

                half = minus_half[:, 0:NT]
                pool.wait_ge(mean_ready, g)
                settle()
                pool.wait_ge(routed, g)
                settle()
                next_reads(pool.tensor_scalar(rms[:, 0, :], mean_var[:, :, 1], LN_EPS, None, ALU.add), 1)
                next_reads(pool.tensor_tensor(out=rstd[:], in0=rms[:, 0, :], in1=half, op=ALU.pow), 2)
                next_reads(pool.tensor_tensor(out=rms[:, 1, :], in0=mean_var[:, :, 1], in1=rstd[:], op=ALU.mult), 3)
                next_reads(pool.tensor_tensor(out=rms[:, 2, :], in0=rms[:, 1, :], in1=rstd[:], op=ALU.mult), 4)
                next_reads(pool.tensor_scalar(rms[:, 3, :], rms[:, 2, :], RMS_EPS, None, ALU.add), 5)
                next_reads(pool.tensor_tensor(out=rms[:, 4, :], in0=rms[:, 3, :], in1=half, op=ALU.pow), 6)
                pool.tensor_tensor(out=both_rstd[:], in0=rms[:, 4, :], in1=rstd[:], op=ALU.mult).then_inc(rstd_ready, 1)

            def keep_rows(g, ffn, ln):
                pool.wait_ge(xn_ready, ln + 1)
                settle()
                pool.tensor_copy(x_routed[:, bass.ds((g - ffn * B) * NT, NT), :], xn[:]).then_inc(xs_copied, 1)

            def send_rows(ffn):
                pool.wait_ge(place_ready, ffn + 1)
                pool.wait_ge(xs_copied, B * (ffn + 1))
                pool.wait_ge(slots_zeroed, 16)
                for t in range(TILES):
                    pool.indirect_dma_start(x_slots, bass.IndirectOffsetOnAxis(ap=place_i[:, t:t + 1], axis=0),
                                            x_routed[:, t, :], None).then_inc(sent, 16)

            def fetch_rows(ffn):
                pool.wait_ge(y_saved, 16 * GROUPS * (ffn + 1))
                for t in range(TILES):
                    pool.indirect_dma_start(y_routed[:, t, :], None, y_slots,
                                            bass.IndirectOffsetOnAxis(ap=place_i[:, t:t + 1], axis=0)
                                            ).then_inc(returned[t // NT], 16)

            for layer in range(2):
                attention_root(layer)
                split_queries(layer * B, STEP0 + STEPS * layer * B)

                def slot(g, p, h, q):
                    g1, p1, q1 = earlier(g, p, h, q, 1)
                    base = STEP0 + 2 + STEPS * g
                    if within(g1, layer):
                        if q == 0:
                            n = base - 1 if within(g, layer) else base - 1 - 2
                        else:
                            n = base + q - 1 + (2 if q >= 2 and within(g + 1, layer) else 0)
                        split_max(g1, n, q1)
                    if q == 1 and within(g + 1, layer):
                        split_queries(g + 1, base + 1)

                run_slots(pool, layer, slot)
                pool.wait_ge(x_updated, 1 + B * (layer + 1))
                with batches(pool, layer) as g:
                    ffn_root(g + 1, g + (layer + 1) * B, 6 * g)
                    keep_rows(g, layer, g + (layer + 1) * B)
                send_rows(layer)
                fetch_rows(layer)

        def s_bank(k):
            if k < 2:
                return [(k, NT - 1, 0)]
            if k < 4:
                return [(k - 2, 2, 0), (k - 2, 0, 3 * P)]
            return [(0, 1, 0), (1, 1, 2 * P)]

        def st_bank(k):
            if k < 2:
                return [(k, 0, 0)]
            if k < 4:
                return [(k - 2, 1, 0), (k - 2, 3, 3 * P)]
            return [(0, 2, 0), (1, 2, 2 * P)]

        @block.tensor
        def _(pe):
            def mm(o, l, r, start=True, stop=True, **kw):
                return pe.matmul(o, l, r, start=start, stop=stop, skip_group_check=True, **kw)

            pe.wait_ge(consts_ready, 7)
            pe.wait_ge(loaded, 16 * N_LOADS)
            pe.transpose(a_ps[:L, 0:C], w_uq[:], ident[:, :]).then_inc(fold_done, 1)
            pe.transpose(d_ps[:, 0:C], w_ob[:], ident[:, :]).then_inc(fold_done, 1)
            pe.wait_ge(fold_copied, 2)
            mm(a_ps[:, 0:C], w_dq[:], w_uqT[:]).then_inc(fold_done, 1)
            mm(d_ps[:, 0:C], w_uqT[:], w_dq[:]).then_inc(fold_done, 1)
            pe.wait_ge(fold_copied, 4)
            mm(a_ps[:L, 0:C], w_uk[:], qeffT[:]).then_inc(fold_done, 1)
            mm(d_ps[:L, 0:C], w_uv[:], w_obT[:]).then_inc(fold_done, 1)
            pe.wait_ge(fold_copied, 6)
            mm(a_ps[:, 0:C], w_dkv[:], keffT[:]).then_inc(fold_done, 1)
            mm(d_ps[:, 0:C], w_dkv[:], veff[:]).then_inc(fold_done, 1)
            pe.wait_ge(fold_copied, 8)
            pe.transpose(a_ps[:, 0:E], cent[:], ident[0:E, 0:E]).then_inc(fold_done, 1)
            pe.wait_ge(ordered, 1)
            for n in range(2):
                ins = mm(d_ps[:, n * E:n * E + E], b_ordered[:, n, :], ones_row[:, 0:E])
            ins.then_inc(fold_done, 1)
            pe.wait_ge(fold_copied, 10)
            mm(s_ps[0][:, 0:P], ident_bf[:], ident_bf[:]).then_inc(xT_full, 1)
            mm(s_ps[1][:, 0:P], ident_bf[:], ident_bf[:]).then_inc(pv_done, PT_BUFS)
            mm(s_ps[2][:, 0:P], ident_bf[:], ident_bf[:]).then_inc(oTT_full, OT_BUFS)

            mm(st_ps[0][:, 0:P], ident_bf[:], ident_bf[:]).then_inc(dist_full, 1)

            def transpose_x(ln):
                pe.wait_ge(xn_ready, ln + 1)
                for t in range(NT):
                    ins = pe.transpose(a_ps[:, tok(t)], xn[:, t, :], ident[:, :])
                ins.then_inc(xT_full, 1)

            def project_q(g, layer):
                pe.wait_ge(xT_ready, g + layer * B + 1)
                mm(a_ps[:], w_q[:, layer, :], xnT[:]).then_inc(q_full, 1)

            def project_k(g, layer):
                pe.wait_ge(qf_ready, g + 1)
                mm(a_ps[:], w_k[:, layer, :], xnT[:]).then_inc(k_full, 1)

            def project_v(g, layer):
                pe.wait_ge(kf_ready, g + 1)
                for t in range(NT):
                    ins = mm(a_ps[:, tok(t)], xnT[:, tok(t)], w_v[:, layer, :], start=(t == 0), stop=(layer == 1))
                    if layer == 0:
                        ins = mm(a_ps[:, tok(t)], ones_row[:], b_v[:, 0, :], start=False)
                ins.then_inc(v_full, 1)

            def scores(g, p, q, u):
                half, k = u % 2, u // 2
                n = 40 * g + 10 * q + u
                pe.wait_ge(s_free, S_BANKS + n if 10 * q + u == 0 else n + 1)
                ps = s_ps[(10 * q + u) % S_BANKS]
                if k < 2:
                    mm(ps[:, 3 * P:4 * P], ident_bf[:], mask2[:, 0, :], start=True, stop=False)
                elif k < 4:
                    mm(ps[:, 2 * P:4 * P], ident_bf[:], mask2[:], start=True, stop=False)
                else:
                    mm(ps[:, :].rearrange("p (n w) -> p n w", n=2)[:, :, P:2 * P], ident_bf[:], mask2[:],
                       start=True, stop=False)
                r = slice(64 * half, 64 * half + STACK)
                for head, t, col in s_bank(k):
                    w = (t + 1) * P
                    ins = mm(ps[:, col:col + w], q_stack[r, p, 2 * q + head, tok(t)],
                             k_stack[r, p, 2 * q + head, 0:w], start=False, tile_position=(64 * half, 0))
                ins.then_inc(s_full, 1)

            def scores_T(g, p, q, u):
                half, k = u % 2, u // 2
                n = 40 * g + 10 * q + u
                pe.wait_ge(exp_done, n + 1)
                ps = st_ps[(10 * q + u) % ST_BANKS]
                r = slice(64 * half, 64 * half + STACK + MROWS)
                blocks = ps[:].rearrange("p (n w) -> p n w", w=P)[:, ::DIAGONAL[k], :]
                mm(blocks, ident_bf[:], mask2T[:, 0:blocks.shape[1], :], start=True, stop=False)
                for head, t, col in st_bank(k):
                    w = S - t * P
                    ins = mm(ps[:, col:col + w], k_stack[r, p, 2 * q + head, tok(t)],
                             q_stack[r, p, 2 * q + head, t * P:S], start=False, tile_position=(64 * half, 0))
                ins.then_inc(st_full, 1)

            def weigh_values(g, p, q, t):
                n = 4 * g + q
                if t == 0:
                    pe.wait_ge(oT_ready, n + 1)
                pe.wait_ge(exp_done, ST_BANKS + 40 * g + 10 * q + (4, 8, 10, 8)[t])
                for half in range(2):
                    for head in range(2):
                        k = (head, 2 + head, 4, 2 + head)[t]
                        col = (0, 0, 2 * P * head, 3 * P)[t]
                        c = 2 * half + head
                        w = S - t * P
                        ins = mm(pv_ps[32 * c:32 * c + 32, t * P:S], v_ext[:, p, t, 4 * q + c, :],
                                 probs[:, q % 2, 2 * k + half, col:col + w], start=(t == 0), stop=(t == NT - 1),
                                 tile_position=(0, 32 * c))
                if t == NT - 1:
                    ins.then_inc(pv_done, 1)

            def d_ps_left(g_slot, q_slot, layer):
                if q_slot == 1 and layer == 0 and within(g_slot - 2, layer):
                    pe.wait_ge(x_updated, g_slot)
                if not isinstance(g_slot, int) or 4 * g_slot + q_slot > 4:
                    pe.wait_ge(attn_ready, 4 * g_slot + q_slot - 4)

            def transpose_max(g, q, g_slot, q_slot, layer):
                pe.wait_ge(s_free, S_BANKS + 40 * g + 10 * (q + 1))
                d_ps_left(g_slot, q_slot, layer)
                pe.transpose(d_ps[0:16, 0:P], neg_max[:, q, :], ident[:, :]).then_inc(maxT_full, 1)

            def transpose_o(g, q):
                n = 4 * g + q
                pe.wait_ge(oT_ready, 1 + n + 1)
                for t in range(NT):
                    ins = pe.transpose(d_ps[:, tok(t)], o_T[:, q % 2, tok(t)], ident[:, :])
                ins.then_inc(oTT_full, 1)

            def transpose_attn(g):
                pe.wait_ge(attn_ready, 4 * g + 4)
                for t in range(NT):
                    ins = pe.transpose(a_ps[:, tok(t)], attn[:, t, :], ident[:, :])
                ins.then_inc(attnT_full, 1)

            def project_out(g):
                pe.wait_ge(attnT_ready, 1 + g + 1)
                for t in range(NT):
                    mm(d_ps[:, tok(t)], attnT[:, tok(t)], w_o[:], start=(t == 0), stop=False)
                    ins = mm(d_ps[:, tok(t)], ones_row[:], b_o[:], start=False)
                ins.then_inc(proj_full, 1)

            def distances(g, ln):
                pe.wait_ge(norm_sq_ready, g + 1)
                for t in range(NT):
                    o = d_ps[:, t * E:t * E + E]
                    mm(o, xnT[:, tok(t)], cent_m2T[:], start=(t == 0), stop=False)
                    mm(o, ones_mat[:], cent_sqT[:], start=False, stop=False)
                    ins = mm(o, xnT_sq[:, tok(t)], ones_mat[:, 0:E], start=False)
                ins.then_inc(dist_full, 1)

            def count_tokens():
                mm(s_ps[0][:, 0:E * TILES], before[:], one_hot[:].rearrange("p e t -> p (e t)"))
                mm(s_ps[1][:, 0:E * TILES], ones_mat[:], one_hot[:].rearrange("p e t -> p (e t)")
                   ).then_inc(counts_full, 1)

            def transpose_rows(w):
                pe.wait_ge(rows_loaded, 16 * w + 16)
                for j in range(GROUP):
                    ins = pe.transpose(a_ps[:, j * P:(j + 1) * P], rows[:, j, :], ident[:, :])
                ins.then_inc(rowsT_full, 1)

            def experts(ffn):
                w0 = ffn * GROUPS
                hT_ps = (st_ps[0], st_ps[1], pv_ps)

                def group(w, more):
                    pe.wait_ge(rowsT_ready, w + 1)
                    e_of = []
                    for j in range(GROUP):
                        e = pe.value_load(slot_expert[0:1, bass.ds((w - w0) * GROUP + j, 1)], min_val=0, max_val=E - 1)
                        e_of.append(e)
                        mm(s_ps[j][:, 0:2 * F], rowsT[:, j, :],
                           w_up[:, bass.ds(e, 1), :].rearrange("p o n -> p (o n)")).then_inc(up_full, 1)
                    if more:
                        transpose_rows(w + 1)
                    for j in range(GROUP):
                        pe.wait_ge(hidden_ready, GROUP * w + j + 1)
                        for c in range(FC):
                            ins = pe.transpose(hT_ps[j][:, c * P:(c + 1) * P], hidden[:, j, c * P:(c + 1) * P],
                                               ident[:, :])
                        ins.then_inc(hiddenT_full, 1)
                    for j in range(GROUP):
                        pe.wait_ge(hiddenT_ready, GROUP * w + j + 1)
                        for c in range(FC):
                            ins = mm(d_ps[:, j * P:(j + 1) * P], hiddenT[:, j, c * P:(c + 1) * P],
                                     w_down[:, bass.ds(e_of[j], 1), c, :].rearrange("p o n -> p (o n)"),
                                     start=(j == 0 and c == 0), stop=(c == FC - 1))
                    ins.then_inc(y_full, 1)

                transpose_rows(w0)
                with pe.Fori(w0, w0 + GROUPS - 1) as w:
                    group(w, True)
                group(w0 + GROUPS - 1, False)

            for layer in range(2):
                if layer == 1:
                    pe.wait_ge(y_added, B)
                b0 = layer * B
                transpose_x(b0 + layer * B)
                project_q(b0, layer)
                project_k(b0, layer)
                project_v(b0, layer)

                def slot(g, p, h, q):
                    g1, p1, q1 = earlier(g, p, h, q, 1)
                    g2, p2, q2 = earlier(g, p, h, q, 2)
                    g3, p3, q3_ = earlier(g, p, h, q, 3)
                    g4 = g - 1
                    if within(g, layer) and q % 2 == 0:
                        pe.wait_ge(stacked[p][q // 2], 64 * (h + 1))
                    for u in range(10):
                        if within(g, layer):
                            scores(g, p, q, u)
                        if u == 5 and within(g2, layer):
                            pe.wait_ge(max_placed[q2 % 2], 64 * (2 * g2 + q2 // 2 + 1))
                        if u >= 5 and within(g2, layer):
                            scores_T(g2, p2, q2, u - 5)
                        if u < 5 and within(g3, layer):
                            scores_T(g3, p3, q3_, u + 5)
                        if q == 1 and within(g + 1, layer):
                            if u == 0:
                                pe.wait_ge(v_ready, 1 + g + 1)
                                if layer == 0 and within(g - 2, layer):
                                    pe.wait_ge(attnT_ready, g)
                                transpose_x(g + 1 + layer * B)
                            if u == 2:
                                project_q(g + 1, layer)
                            if u == 4:
                                project_k(g + 1, layer)
                        if q == 3 and u == 1 and within(g + 1, layer):
                            project_v(g + 1, layer)
                        if u == 1 and within(g1, layer):
                            transpose_max(g1, q1, g, q, layer)
                        if q == 0 and u == 3 and layer == 0 and within(g - 2, layer):
                            pe.wait_ge(v_ready, 1 + (g if not isinstance(g, int) else min(g + 1, b0 + B)))
                            transpose_attn(g - 2)
                        if u == 5 and within(g4, layer):
                            if within(g1, layer):
                                pe.wait_ge(maxT_ready, 4 * g + q)
                            else:
                                d_ps_left(g, q, layer)
                            transpose_o(g4, q)
                        if q == 0 and u == 7 and layer == 0 and within(g - 2, layer):
                            if within(g4, layer):
                                pe.wait_ge(attn_ready, 4 * g4 + 1)
                            project_out(g - 2)
                        if u in VALUES_AT and within(g3, layer):
                            weigh_values(g3, p3, q3_, VALUES_AT.index(u))

                run_slots(pe, layer, slot)
                pe.wait_ge(x_updated, 1 + B * (layer + 1))
                with batches(pe, layer) as g:
                    transpose_x(g + (layer + 1) * B)
                    distances(g, g + (layer + 1) * B)
                pe.wait_ge(routed, 1 + B * (layer + 1))
                count_tokens()
                pe.wait_ge(place_ready, layer + 1)
                experts(layer)

        @block.scalar
        def _(act):
            act.wait_ge(consts_ready, 7)
            act.copy(credit[0:1, 4:5], ones_row[0:1, 0:1]).then_inc(exp_done, ST_BANKS)
            act.copy(credit[0:1, 5:6], ones_row[0:1, 0:1]).then_inc(oT_ready, 1)
            act.copy(credit[0:1, 6:7], ones_row[0:1, 0:1]).then_inc(v_ready, 1)
            act.copy(credit[32:33, 4:5], ones_mat[32:33, 0:1]).then_inc(attnT_ready, 1)
            act.wait_ge(loaded, 16 * N_LOADS)

            def copy_xT(ln):
                act.wait_ge(xT_full, 1 + ln + 1)
                act.copy(xnT[:], a_ps[:]).then_inc(xT_ready, 1)

            def scale_xT(g, ln):
                act.wait_ge(xT_full, 1 + ln + 1)
                act.wait_ge(dist_full, g + 1)
                act.activation(xnT[:], a_ps[:], ACT.Identity, scale=scale_col[:, 0:1]).then_inc(xT_ready, 1)
                act.activation(xnT_sq[:], a_ps[:], ACT.Square, scale=scale_col[:, 0:1]).then_inc(norm_sq_ready, 1)

            def expert_group(w):
                for j in range(GROUP):
                    act.wait_ge(up_full, GROUP * w + j + 1)
                    act.activation(gate[:, j, :], s_ps[j][:, F:2 * F], ACT.Silu).then_inc(gate_ready, 1)

            def copy_rowsT(w):
                act.wait_ge(rowsT_full, w + 1)
                act.activation(rowsT[:].rearrange("p s t -> p (s t)"), a_ps[:, 0:GROUP * P], ACT.Identity,
                               scale=scale_col[:, 0:1]).then_inc(rowsT_ready, 1)

            def copy_q(g, layer):
                act.wait_ge(q_full, g + 1)
                act.wait_ge(q3_ready, g + 1)
                bias = {"bias": b_qk[:, 0, 0:1]} if layer == 0 else {}
                act.activation(q3[:, 0, :], a_ps[:], ACT.Identity, **bias)
                act.activation(qf[:], a_ps[:], ACT.Identity, **bias).then_inc(qf_ready, 1)

            def copy_k(g, layer):
                act.wait_ge(k_full, g + 1)
                act.wait_ge(k3_ready, g + 1)
                bias = {"bias": b_qk[:, 1, 0:1]} if layer == 0 else {}
                act.activation(k3[:, 0, :], a_ps[:], ACT.Identity, **bias)
                act.activation(kf[:], a_ps[:], ACT.Identity, **bias).then_inc(kf_ready, 1)

            def copy_v(g, p):
                act.wait_ge(v_full, g + 1)
                ins = act.copy(v_ext[:, p, :, :, 0:DH], a_ps[:].rearrange("p (t h d) -> p t h d", t=NT, h=H))
                ins.then_inc(v_ready, 1)

            def exp(g, q, u):
                if u == 0:
                    act.wait_ge(pv_done, 4 * g + q + 1)
                act.wait_ge(st_full, 40 * g + 10 * q + u + 1)
                act.activation(probs[:, q % 2, u, :], st_ps[(10 * q + u) % ST_BANKS][:], ACT.Exp,
                               scale=SCALE).then_inc(exp_done, 1)

            def copy_oT(g, q):
                n = 4 * g + q
                act.wait_ge(pv_done, PT_BUFS + n + 1)
                act.wait_ge(oTT_full, n + 1)
                act.copy(o_T[:, q % 2, :], pv_ps[:]).then_inc(oT_ready, 1)

            for layer in range(2):
                b0 = layer * B
                copy_xT(b0 + layer * B)
                copy_q(b0, layer)
                copy_k(b0, layer)
                copy_v(b0, 0)

                def slot(g, p, h, q):
                    g2, p2, q2 = earlier(g, p, h, q, 2)
                    g3, p3, q3_ = earlier(g, p, h, q, 3)
                    if within(g - 1, layer):
                        copy_oT(g - 1, q)
                    for u in range(10):
                        if u >= 5 and within(g2, layer):
                            exp(g2, q2, u - 5)
                        if u < 5 and within(g3, layer):
                            exp(g3, q3_, u + 5)
                        if q == 1 and within(g + 1, layer):
                            if u == 1:
                                copy_xT(g + 1 + layer * B)
                            if u == 3:
                                copy_q(g + 1, layer)
                            if u == 5:
                                copy_k(g + 1, layer)
                        if q == 3 and u == 2 and within(g + 1, layer):
                            copy_v(g + 1, 1 - p)
                        if q == 0 and u == 4 and layer == 0 and within(g - 2, layer):
                            act.wait_ge(attnT_full, g - 1)
                            act.copy(attnT[:], a_ps[:]).then_inc(attnT_ready, 1)

                run_slots(act, layer, slot)
                with batches(act, layer) as g:
                    scale_xT(g, g + (layer + 1) * B)
                w0 = layer * GROUPS
                copy_rowsT(w0)
                with act.Fori(w0, w0 + GROUPS - 1) as w:
                    expert_group(w)
                    copy_rowsT(w + 1)
                expert_group(w0 + GROUPS - 1)

        @block.vector
        def _(dve):
            def split_columns(dst, src):
                for half in range(2):
                    ins = dve.tensor_copy(
                        dst[:, half * 64:half * 64 + 64].rearrange("p (d q h) -> p d q h", q=QUADS, h=2),
                        src.rearrange("p (q r h d) -> p r d q h", q=QUADS, r=2, h=2)[:, half])
                return ins

            for half in range(2):
                dve.memset(k_stack[half * 64 + 32:half * 64 + 64, :, :, :], 1.0).then_inc(ones_ready, 1)
            dve.wait_ge(loaded, 16 * N_LOADS)
            for n in range(2):
                split_columns(b_ordered[:, n, :], b_natural[:, n, :])
                ins = split_columns((w_q, w_k)[n][:, 0, :], w_natural[:, n, :])
            ins.then_inc(ordered, 1)
            dve.memset(credit[:, 0:1], 0.0).then_inc(k3_ready, 1)
            dve.wait_ge(fold_done, 1)
            dve.tensor_copy(w_uqT[:], a_ps[:L, 0:C]).then_inc(fold_copied, 1)
            dve.wait_ge(fold_done, 2)
            dve.tensor_copy(w_obT[:], d_ps[:, 0:C]).then_inc(fold_copied, 1)
            dve.wait_ge(fold_done, 3)
            split_columns(w_q[:, 1, :], a_ps[:, 0:C]).then_inc(fold_copied, 1)
            dve.wait_ge(fold_done, 4)
            dve.tensor_copy(qeffT[:], d_ps[:, 0:C]).then_inc(fold_copied, 1)
            dve.wait_ge(fold_done, 5)
            dve.tensor_copy(keffT[:], a_ps[:L, 0:C]).then_inc(fold_copied, 1)
            dve.wait_ge(fold_done, 6)
            dve.tensor_copy(veff[:], d_ps[:L, 0:C]).then_inc(fold_copied, 1)
            dve.wait_ge(fold_done, 7)
            split_columns(w_k[:, 1, :], a_ps[:, 0:C]).then_inc(fold_copied, 1)
            dve.wait_ge(fold_done, 8)
            dve.tensor_copy(w_v[:, 1, :], d_ps[:, 0:C]).then_inc(fold_copied, 1)
            dve.wait_ge(fold_done, 9)
            dve.tensor_copy(centT[:], a_ps[:, 0:E]).then_inc(ffn_step, 1)
            dve.wait_ge(ffn_step, 1)
            dve.tensor_scalar(cent_m2T[:], centT[:], -2.0, None, ALU.mult)
            dve.tensor_tensor(out=cent_sqT[:], in0=centT[:], in1=centT[:], op=ALU.mult).then_inc(fold_copied, 1)
            dve.wait_ge(fold_done, 10)
            dve.tensor_copy(b_qk[:].rearrange("p n e -> p (n e)"), d_ps[:, 0:2 * E]).then_inc(fold_copied, 1)
            dve.memset(credit[:, 7:8], 0.0).then_inc(routed, 1)
            dve.memset(credit[:, 2:3], 0.0).then_inc(s_free, S_BANKS)
            dve.memset(credit[:, 3:4], 0.0).then_inc(x_updated, 1)
            dve.wait_ge(loaded_x, 16 * B)

            FFN_STEP0 = 1

            def x_tile(g, layer, t, n=1):
                return x_sb[:, bass.ds((g - layer * B) * NT + t, n), :]

            def means(g, layer, step_sem, base):
                for t in range(NT):
                    ins = dve.bn_stats(out=stats[:, t, :], in_=x_tile(g, layer, t).rearrange("p o c -> p (o c)"))
                ins.then_inc(step_sem, 1)
                dve.wait_ge(step_sem, base + 1)
                dve.sem_inc(dve_waited, 1)
                for t in range(NT):
                    ins = dve.bn_aggr(out=mean_var[:, t, :], in_=stats[:, t, :])
                ins.then_inc(mean_ready, 1)

            def attention_means(layer, b):
                for t in range(b * NT, b * NT + NT):
                    ins = dve.bn_stats(out=att_stats[:, t, :], in_=x_sb[:, t, :])
                ins.then_inc(att_stats_done, 1)
                dve.wait_ge(att_stats_done, layer * B + b + 1)
                for t in range(b * NT, b * NT + NT):
                    ins = dve.bn_aggr(out=att_mean_var[:, t, :], in_=att_stats[:, t, :])
                if b == B - 1:
                    ins.then_inc(att_mean_ready, 1)

            def flat(ap):
                return ap.rearrange("p o c -> p (o c)")

            def normalize(g, layer):
                dve.wait_ge(att_rstd_ready, layer + 1)
                dve.wait_ge(xT_full, g + layer * B + 1)
                for t in range(NT):
                    ins = dve.tensor_scalar(xn[:, t, :], x_tile(g, layer, t).rearrange("p o c -> p (o c)"),
                                            flat(att_mean_var[:, bass.ds((g - layer * B) * NT + t, 1), 0:1]),
                                            att_rstd[:, bass.ds((g - layer * B) * NT + t, 1)], ALU.subtract, ALU.mult)
                ins.then_inc(xn_ready, 1)

            def row_max(g, q, u):
                half, k = u % 2, u // 2
                dve.wait_ge(s_full, 40 * g + 10 * q + u + 1)
                ps = s_ps[(10 * q + u) % S_BANKS]
                out_ = neg_max[:, q, :].rearrange("p (h j t) -> p h j t", h=2, j=2)[:, half]
                if k == 4:
                    ins = dve.tensor_reduce(out_[:, :, 1], ps[:].rearrange("p (h w) -> p h w", h=2),
                                            axis=AX.X, op=ALU.max, negate=True)
                else:
                    for head, t, col in s_bank(k):
                        ins = dve.tensor_reduce(out_[:, head, t:t + 1], ps[:, col:col + (t + 1) * P],
                                                axis=AX.X, op=ALU.max, negate=True)
                ins.then_inc(s_free, 1)

            def copy_maxT(g, q):
                dve.wait_ge(maxT_full, 4 * g + q + 1)
                dve.tensor_copy(neg_maxT[:, q, :], d_ps[0:16, 0:P]).then_inc(maxT_ready, 1)

            def split_keys(g):
                dve.wait_ge(kf_ready, g + 1)
                dve.tensor_tensor(out=k_rest[:], in0=kf[:], in1=k3[:, 0, :], op=ALU.subtract).then_inc(k_split_step, 1)
                dve.wait_ge(k_split_step, 2 * g + 1)
                dve.tensor_copy(k3[:, 1, :], k_rest[:]).then_inc(k_split_step, 1)
                dve.wait_ge(k_split_step, 2 * g + 2)
                dve.tensor_tensor(out=k3[:, 2, :], in0=k_rest[:], in1=k3[:, 1, :],
                                  op=ALU.subtract).then_inc(k3_ready, 1)

            def divide(g, q, layer, base):
                n = 4 * g + q
                dve.wait_ge(oTT_full, OT_BUFS + n + 1)
                o = d_ps[:].rearrange("p (t h e) -> p t h e", t=NT, h=4)
                dve.reciprocal(recip[:], o[:, :, :, DH]).then_inc(dve_step, 1)
                dve.wait_ge(dve_step, base + 1)
                dve.tensor_tensor(out=attn[:, :, 32 * q:32 * q + 32].rearrange("p t (h d) -> p t h d", h=4),
                                  in0=o[:, :, :, 0:DH], in1=recip[:][:, :, :, None].broadcast_to([P, NT, 4, DH]),
                                  op=ALU.mult).then_inc(attn_ready, 1)

            ROUTE_STEPS = 8
            PLACE_STEPS = 20

            def ffn_normalize(g, ffn, ln, base):
                dve.wait_ge(rstd_ready, g + 1)
                dve.wait_ge(xT_full, ln + 1)
                dve.wait_ge(xs_copied, g)
                for t in range(NT):
                    x_t = flat(x_tile(g, ffn, t))
                    dve.tensor_scalar(xl[:, t, :], x_t, mean_var[:, t, 0:1], rstd[:, t:t + 1], ALU.subtract, ALU.mult)
                    ins = dve.tensor_scalar(xn[:, t, :], x_t, mean_var[:, t, 0:1], both_rstd[:, t:t + 1],
                                            ALU.subtract, ALU.mult)
                ins.then_inc(xn_ready, 1)
                dve.wait_ge(xn_ready, ln + 1)
                dve.tensor_tensor(out=x_tile(g, ffn, 0, NT), in0=xl[:], in1=x_tile(g, ffn, 0, NT),
                                  op=ALU.add).then_inc(ffn_step, 1)

            def choose(g, ffn, base):
                def next_reads(ins, n):
                    ins.then_inc(ffn_step, 1)
                    dve.wait_ge(ffn_step, base + n)

                dve.wait_ge(dist_full, 1 + g + 1)
                dist = d_ps[:, 0:NT * E].rearrange("p (t e) -> p t e", e=E)
                next_reads(dve.tensor_reduce(nearest[:], dist, axis=AX.X, op=ALU.min), 3)
                next_reads(dve.tensor_tensor(out=farther[:], in0=dist,
                                             in1=nearest[:].unsqueeze(2).broadcast_to([P, NT, E]), op=ALU.is_gt), 4)
                next_reads(dve.scalar_tensor_tensor(out=candidate[:].rearrange("p t e -> p (t e)"),
                                                    in0=farther[:].rearrange("p t e -> p (t e)"), scalar=float(E),
                                                    in1=expert_row[:].rearrange("p t e -> p (t e)"),
                                                    op0=ALU.mult, op1=ALU.add), 5)
                next_reads(dve.tensor_reduce(chosen[:], candidate[:], axis=AX.X, op=ALU.min), 6)
                dve.tensor_tensor(out=one_hot[:, :, bass.ds((g - ffn * B) * NT, NT)].rearrange("p e t -> p t e"),
                                  in0=expert_row[:], in1=chosen[:].unsqueeze(2).broadcast_to([P, NT, E]),
                                  op=ALU.is_equal).then_inc(routed, 1)

            def places(ffn, base):
                n = [base]

                def next_reads(ins):
                    ins.then_inc(ffn_step, 1)
                    n[0] += 1
                    dve.wait_ge(ffn_step, n[0])

                dve.wait_ge(counts_full, ffn + 1)
                next_reads(dve.tensor_copy(counts[:, 0, :, PAD:], s_ps[1][:, 0:E * TILES].rearrange(
                    "p (e t) -> p e t", e=E)))
                k, shift = 0, 1
                while shift < TILES:
                    next_reads(dve.tensor_tensor(out=counts[:, 1 - k, :, PAD:], in0=counts[:, k, :, PAD:],
                                                 in1=counts[:, k, :, PAD - shift:PAD - shift + TILES], op=ALU.add))
                    k, shift = 1 - k, 2 * shift
                next_reads(dve.tensor_scalar(slots_i[:, 0, :], counts[:, k, :, PAD + TILES - 1], float(P - 1), None,
                                             ALU.add))
                next_reads(dve.tensor_scalar(slots_i[:, 1, :], slots_i[:, 0, :], P.bit_length() - 1, None,
                                             ALU.arith_shift_right))
                next_reads(dve.tensor_copy(slots_of[:], slots_i[:, 1, :]))
                next_reads(dve.tensor_copy(slots_f[:, 0, E:], slots_of[:]))
                j, shift = 0, 1
                while shift < E:
                    next_reads(dve.tensor_tensor(out=slots_f[:, 1 - j, E:], in0=slots_f[:, j, E:],
                                                 in1=slots_f[:, j, E - shift:2 * E - shift], op=ALU.add))
                    j, shift = 1 - j, 2 * shift
                next_reads(dve.tensor_tensor(out=base_row[:], in0=slots_f[:, j, E:], in1=slots_of[:],
                                             op=ALU.subtract))
                next_reads(dve.scalar_tensor_tensor(
                    out=place[:, 0], in0=base_row[:].unsqueeze(2).broadcast_to([P, E, TILES]), scalar=float(P),
                    in1=counts[:, k, :, PAD - 1:PAD - 1 + TILES], op0=ALU.mult, op1=ALU.add))
                next_reads(dve.tensor_tensor(out=place[:, 1], in0=s_ps[0][:, 0:E * TILES].rearrange(
                    "p (e t) -> p e t", e=E), in1=place[:, 0], op=ALU.add))
                next_reads(dve.tensor_tensor(out=place[:, 2], in0=place[:, 1], in1=one_hot[:], op=ALU.mult))
                next_reads(dve.tensor_reduce(place_f[:], place[:, 2].rearrange("p e t -> p t e"), axis=AX.X,
                                             op=ALU.add))
                next_reads(dve.tensor_tensor(out=slot_past[:], in0=slot_row[:],
                                             in1=slots_f[0:1, j, E:].unsqueeze(1).broadcast_to([1, SLOTS, E]),
                                             op=ALU.is_ge))
                next_reads(dve.tensor_reduce(slot_f[:], slot_past[:], axis=AX.X, op=ALU.add))
                dve.tensor_scalar(slot_expert[:], slot_f[:], float(E - 1), None, ALU.min)
                dve.tensor_copy(place_i[:], place_f[:]).then_inc(place_ready, 1)
                assert n[0] - base == PLACE_STEPS, n[0] - base

            def expert_group(w):
                for j in range(GROUP):
                    n = GROUP * w + j + 1
                    dve.wait_ge(gate_ready, n)
                    dve.tensor_tensor(out=hidden[:, j, :], in0=s_ps[j][:, 0:F], in1=gate[:, j, :],
                                      op=ALU.mult).then_inc(hidden_ready, 1)
                hT_ps = (st_ps[0], st_ps[1], pv_ps)
                for j in range(GROUP):
                    dve.wait_ge(hiddenT_full, GROUP * w + j + 1)
                    dve.tensor_copy(hiddenT[:, j, :], hT_ps[j][:, 0:F]).then_inc(hiddenT_ready, 1)
                dve.wait_ge(y_full, w + 1)
                dve.tensor_copy(y_out[:].rearrange("p s c -> p (s c)"), d_ps[:, 0:GROUP * C]).then_inc(y_copied, 1)

            for b in range(B):
                attention_means(0, b)
            for layer in range(2):
                normalize(layer * B, layer)
                split_keys(layer * B)

                def slot(g, p, h, q):
                    g1, p1, q1 = earlier(g, p, h, q, 1)
                    if q == 1 and within(g + 1, layer):
                        normalize(g + 1, layer)
                    if q == 0 and layer == 1 and within(g - 2, layer):
                        dve.wait_ge(attn_ready, 4 * g - 4)
                        dve.tensor_tensor(out=x_tile(g - 2, 1, 0, NT), in0=attn[:], in1=x_tile(g - 2, 1, 0, NT),
                                          op=ALU.add).then_inc(x_updated, 1)
                    for u in range(10):
                        if within(g, layer):
                            row_max(g, q, u)
                        if u == 2 and within(g1, layer):
                            copy_maxT(g1, q1)
                        if q == 1 and u == 8 and within(g + 1, layer):
                            split_keys(g + 1)
                        if u == 6 and within(g - 1, layer):
                            divide(g - 1, q, layer, 4 * (g - 1) + q)
                        if u == 8 and q == 0 and layer == 0 and within(g - 2, layer):
                            dve.wait_ge(proj_full, g - 1)
                            dve.tensor_tensor(out=x_tile(g - 2, 0, 0, NT),
                                              in0=d_ps[:].rearrange("p (t c) -> p t c", t=NT),
                                              in1=x_tile(g - 2, 0, 0, NT), op=ALU.add).then_inc(x_updated, 1)

                run_slots(dve, layer, slot)
                dve.wait_ge(x_updated, 1 + B * (layer + 1))
                route0 = 1 + layer * PLACE_STEPS
                with batches(dve, layer) as g:
                    base = route0 + 6 * g
                    means(g, layer, ffn_step, base)
                    ffn_normalize(g, layer, g + (layer + 1) * B, base)
                    choose(g, layer, base)
                places(layer, route0 + 6 * B * (layer + 1))
                w0 = layer * GROUPS
                expert_group(w0)
                with dve.Fori(w0 + 1, w0 + GROUPS) as w:
                    dve.wait_ge(y_saved, 16 * w)
                    expert_group(w)
                for b in range(B):
                    dve.wait_ge(returned[b], 16 * NT * (layer + 1))
                    dve.tensor_tensor(out=x_sb[:, b * NT:(b + 1) * NT, :], in0=y_routed[:, b * NT:(b + 1) * NT, :],
                                      in1=x_sb[:, b * NT:(b + 1) * NT, :], op=ALU.add).then_inc(y_added, 1)
                    if layer == 0:
                        dve.wait_ge(y_added, b + 1)
                        attention_means(1, b)


_INS = ['L0_attn_a_x', 'L0_attn_a_W_q', 'L0_attn_a_b_q', 'L0_attn_a_W_k', 'L0_attn_a_b_k', 'L0_attn_a_W_v',
        'L0_attn_a_b_v', 'L0_attn_a_W_o', 'L0_attn_a_b_o', 'L0_attn_b_W_dq', 'L0_attn_b_W_uq', 'L0_attn_b_W_dkv',
        'L0_attn_b_W_uk', 'L0_attn_b_W_uv', 'L0_attn_b_W_o', 'L0_ffn_scale', 'L0_ffn_centroids', 'L0_ffn_up_w',
        'L0_ffn_down_w']


def kernel(**inputs):
    import numpy as _np
    import concourse.bacc as _bacc
    from concourse import mybir as _mybir
    from concourse.bass_utils import run_bass_kernel_spmd as _run

    nc = _bacc.Bacc("TRN2", target_bir_lowering=False, num_devices=1)
    arrays, args = {}, []
    for name in _INS:
        a = _np.ascontiguousarray(inputs[name])
        arrays[f"in_{name}_dram"] = a
        args.append(nc.dram_tensor(f"in_{name}_dram", a.shape, _mybir.dt.from_np(a.dtype), kind="ExternalInput").ap())
    shape = inputs['L0_attn_a_x'].shape
    args.append(nc.dram_tensor("out_0_dram", shape, _mybir.dt.float32, kind="ExternalOutput").ap())
    hybrid_layers(nc, *args)
    r = _run(nc, [arrays], core_ids=[0])
    return r.results[0]["out_0_dram"]
```

```python
from contextlib import ExitStack

import concourse.bass as bass
from concourse import mybir

F32, BF16, I32 = mybir.dt.float32, mybir.dt.bfloat16, mybir.dt.int32
ALU = mybir.AluOpType
ACT = mybir.ActivationFunctionType
AX = mybir.AxisListType

P = 128
LN_EPS = 1e-5
RMS_EPS = 1e-6
MASKED = -1e30

STACK = 48
DIAGONAL = (4, 4, 3, 3, 2)
MROWS = 2
Q_SLOTS = (0, 1, 2, 0, 1, 0)
K_SLOTS = (0, 0, 0, 1, 1, 2)


def hybrid_layers(nc, x_in, Wq, bq, Wk, bk, Wv, bv, Wo, bo, Wdq, Wuq, Wdkv, Wuk, Wuv, Wob, ffn_scale,
                  centroids, up_w, down_w, out):
    B, S, C = x_in.shape
    NT = S // P
    TILES = B * NT
    H = 16
    DH = C // H
    NJ = H // 2
    QUADS = H // 4
    SCALE = float(DH) ** -0.5
    L = Wdq.shape[0]
    E = centroids.shape[0]
    F = down_w.shape[1]
    FC = F // P
    SLOTS = (TILES * P + E * (P - 1)) // P
    GROUP = 3
    GROUPS = SLOTS // GROUP
    assert SLOTS % GROUP == 0 and 2 * F <= S and E == 8 and TILES == 32
    assert C == P and NT == 4 and DH == 8 and L == 64

    with ExitStack() as ctx:
        def sb(name, shape, dt=F32):
            return ctx.enter_context(nc.sbuf_tensor(name, shape, dt))

        def psum(name, shape, dt=F32):
            return ctx.enter_context(nc.psum_tensor(name, shape, dt))

        def sem(name):
            return ctx.enter_context(nc.semaphore(name))

        x_sb = sb("x_sb", [P, TILES, C])
        ident = sb("ident", [P, P])
        ident_bf = sb("ident_bf", [P, P], BF16)
        mask2 = sb("mask2", [P, 2, P], BF16)
        causal = sb("causal", [P, S])
        mask2T = sb("mask2T", [P, 2, P], BF16)
        ones_row = sb("ones_row", [1, P])
        minus_half = sb("minus_half", [P, TILES])
        w_q = sb("w_q", [P, 2, C])
        w_k = sb("w_k", [P, 2, C])
        w_v = sb("w_v", [P, 2, C])
        w_o = sb("w_o", [P, C])
        b_natural = sb("b_natural", [1, 2, C])
        b_ordered = sb("b_ordered", [1, 2, C])
        b_qk = sb("b_qk", [P, 2, E])
        b_v = sb("b_v", [1, 2, C])
        b_o = sb("b_o", [1, C])
        b_v_cols = sb("b_v_cols", [C, P])
        out_bias = sb("out_bias", [P, C])

        credit = sb("credit", [P, 12])
        stats = sb("stats", [P, TILES, 6])
        att_mean_var = sb("att_mean_var", [P, TILES, 2])
        att_var_eps = sb("att_var_eps", [P, TILES])
        att_rstd = sb("att_rstd", [P, TILES])
        mean_var = sb("mean_var", [P, TILES, 2])
        batch_mean_var = sb("batch_mean_var", [P, NT, 2])
        to_xl = sb("to_xl", [P, TILES])
        xn = sb("xn", [P, NT, C])
        xnT = sb("xnT", [P, S])
        qf = sb("qf", [P, S])
        kf = sb("kf", [P, S])
        q_rest = sb("q_rest", [P, S])
        k_rest = sb("k_rest", [P, S])
        q3 = sb("q3", [P, 3, S], BF16)
        k3 = sb("k3", [P, 3, S], BF16)
        q_stack = sb("q_stack", [P, 2, NJ, S], BF16)
        k_stack = sb("k_stack", [P, 2, NJ, S], BF16)
        v_ext = sb("v_ext", [P, 2, NT, H, 32])
        arena = sb("arena", [P, 2 * 10 * S])
        probs = arena[:].rearrange("p (b k s) -> p b k s", b=2, k=10)
        x_routed = arena[:, 0:TILES * C].rearrange("p (t c) -> p t c", c=C)
        y_routed = arena[:, TILES * C:2 * TILES * C].rearrange("p (t c) -> p t c", c=C)
        fold_at = 2 * TILES * C

        def fold_buffer(rows, cols):
            nonlocal fold_at
            fold_at += cols
            return arena[0:rows, fold_at - cols:fold_at]

        w_natural = fold_buffer(P, 2 * C).rearrange("p (n c) -> p n c", n=2)
        w_dq, w_dkv = fold_buffer(L, C), fold_buffer(L, C)
        w_uq, w_uk, w_uv = fold_buffer(C, L), fold_buffer(C, L), fold_buffer(C, L)
        w_ob, w_obT, qeffT = fold_buffer(C, C), fold_buffer(C, C), fold_buffer(C, C)
        w_uqT, keffT, veff = fold_buffer(L, C), fold_buffer(L, C), fold_buffer(L, C)
        neg_max = sb("neg_max", [P, 4, 16])
        neg_maxT = sb("neg_maxT", [16, 4, P])
        max_parts = sb("max_parts", [16, 4, 2, P], BF16)
        o_T = sb("o_T", [P, 2, S])
        recip = sb("recip", [P, NT, 4])
        attn = sb("attn", [P, NT, C])
        attnT = sb("attnT", [P, S])

        w_up = sb("w_up", [P, E, 2 * F])
        w_down = sb("w_down", [P, E, FC, C])
        scale_col = sb("scale_col", [P, 1])
        cent = sb("cent", [E, C])
        centT = sb("centT", [P, E])
        cent_m2T = sb("cent_m2T", [P, E])
        cent_sqT = sb("cent_sqT", [P, E])
        ones_mat = sb("ones_mat", [P, P])
        before = sb("before", [P, P])
        before_bf = sb("before_bf", [P, P], BF16)
        ones_bf = sb("ones_bf", [P, P], BF16)
        expert_row = sb("expert_row", [P, TILES, E])
        slot_no = sb("slot_no", [P, SLOTS])
        row_no = sb("row_no", [P, P])
        tile_no = sb("tile_no", [P, TILES])
        token_no = sb("token_no", [P, 1])
        unused_row = sb("unused_row", [P, SLOTS])
        rms = sb("rms", [P, 6, NT])
        both_rstd = sb("both_rstd", [P, TILES])
        nearest = sb("nearest", [P, TILES])
        farther = sb("farther", [P, TILES, E])
        candidate = sb("candidate", [P, TILES, E])
        chosen = sb("chosen", [P, TILES])
        xsT = (xnT, qf)
        xsT_sq = (kf, q_rest)
        one_hot = sb("one_hot", [P, E, TILES], BF16)
        PAD = TILES // 2
        counts = sb("counts", [P, 2, E, PAD + TILES])
        slots_f = sb("slots_f", [P, 2, 2 * E])
        slots_i = sb("slots_i", [P, 2, E], I32)
        slots_of = sb("slots_of", [P, E])
        base_row = sb("base_row", [P, E])
        place = sb("place", [P, 3, E, TILES])
        place_f = sb("place_f", [P, TILES])
        place_i = sb("place_i", [P, 3, TILES], I32)
        row_of = sb("row_of", [P, TILES])
        slot_of = sb("slot_of", [P, TILES])
        token_of = sb("token_of", [P, SLOTS])
        unused = sb("unused", [P, SLOTS])
        partition_of = sb("partition_of", [P, SLOTS])
        read_row = sb("read_row", [P, SLOTS], I32)
        write_row = sb("write_row", [P, SLOTS], I32)
        row_hot = q_stack[:, 0].rearrange("p j s -> p (j s)")[:, 0:TILES * P].rearrange("p (t r) -> p t r", r=P)
        slot_hot = q_stack[:, 1].rearrange("p j s -> p (j s)")[:, 0:TILES * 3 * SLOTS].rearrange(
            "p (t n s) -> p t n s", n=3, s=SLOTS)
        slot_past = sb("slot_past", [1, SLOTS, E])
        slot_f = sb("slot_f", [1, SLOTS])
        slot_expert = sb("slot_expert", [1, SLOTS], I32)
        rows = sb("rows", [P, 2, GROUP, C])
        rowsT = sb("rowsT", [P, GROUP, P])
        gate = sb("gate", [P, GROUP, F])
        hidden = sb("hidden", [P, GROUP, F])
        hiddenT = sb("hiddenT", [P, GROUP, F])
        y_out = sb("y_out", [P, 2, GROUP, C])

        x_rows = nc.dram_tensor("x_rows", [TILES * P, C], F32, kind="Internal").ap()
        y_rows = nc.dram_tensor("y_rows", [(TILES + SLOTS) * P, C], F32, kind="Internal").ap()
        q_rows = nc.dram_tensor("q_rows", [2, len(Q_SLOTS), 64, S], BF16, kind="Internal").ap()
        k_rows = nc.dram_tensor("k_rows", [2, len(K_SLOTS), 64, S], BF16, kind="Internal").ap()

        s_ps = [psum(f"s_ps{i}", [P, S]) for i in range(3)]
        st_ps = [psum(f"st_ps{i}", [P, S]) for i in range(2)]
        pv_ps = psum("pv_ps", [P, S])
        a_ps = psum("a_ps", [P, S])
        d_ps = psum("d_ps", [P, S])

        loaded = sem("loaded")
        loaded_late = sem("loaded_late")
        loaded_x = [sem("loaded_x0"), sem("loaded_x_rest")]
        bias_full = sem("bias_full")
        bias_ready = sem("bias_ready")
        bias_added = sem("bias_added")
        consts_ready = sem("consts_ready")
        pool_step = sem("pool_step")
        causal_step = sem("causal_step")
        ones_ready = sem("ones_ready")
        fold_done = sem("fold_done")
        fold_copied = sem("fold_copied")
        dve_step = sem("dve_step")
        pool_waited = sem("pool_waited")
        sp_waited = sem("sp_waited")
        dve_waited = sem("dve_waited")
        att_stats_done = sem("att_stats_done")
        att_root_step = sem("att_root_step")
        att_mean_ready = sem("att_mean_ready")
        att_rstd_ready = sem("att_rstd_ready")
        mean_ready = sem("mean_ready")
        batch_mean_ready = sem("batch_mean_ready")
        rstd_ready = sem("rstd_ready")
        xn_ready = sem("xn_ready")
        xT_full = sem("xT_full")
        xT_ready = sem("xT_ready")
        q_full = sem("q_full")
        k_full = sem("k_full")
        v_full = sem("v_full")
        qf_ready = sem("qf_ready")
        kf_ready = sem("kf_ready")
        v_ready = sem("v_ready")
        q3_ready = sem("q3_ready")
        k3_ready = sem("k3_ready")
        q3_saved = sem("q3_saved")
        k3_saved = sem("k3_saved")
        stacked = [[sem(f"stacked{i}_{pair}") for pair in range(2)] for i in range(2)]
        k_split_step = sem("k_split_step")
        q_split_step = sem("q_split_step")
        ordered = sem("ordered")
        s_full = sem("s_full")
        s_free = sem("s_free")
        maxT_full = sem("maxT_full")
        maxT_ready = sem("maxT_ready")
        max_parts_ready = sem("max_parts_ready")
        max_placed = [sem(f"max_placed{i}") for i in range(4)]
        st_full = sem("st_full")
        exp_done = sem("exp_done")
        pv_done = sem("pv_done")
        oT_ready = sem("oT_ready")
        oTT_full = sem("oTT_full")
        attn_ready = sem("attn_ready")
        attnT_full = sem("attnT_full")
        attnT_ready = sem("attnT_ready")
        proj_full = sem("proj_full")
        x_updated = sem("x_updated")
        stored = sem("stored")
        dist_full = sem("dist_full")
        norm_sq_ready = sem("norm_sq_ready")
        xs_ready = sem("xs_ready")
        xsT_full = sem("xsT_full")
        routed = sem("routed")
        ffn_stats_done = sem("ffn_stats_done")
        counts_full = sem("counts_full")
        place_ready = sem("place_ready")
        ffn_step = sem("ffn_step")
        skip_added = sem("skip_added")
        ffn_pool_step = sem("ffn_pool_step")
        setup_step = sem("setup_step")
        slots_marked = sem("slots_marked")
        rows_marked = sem("rows_marked")
        slots_numbered = sem("slots_numbered")
        tiles_numbered = sem("tiles_numbered")
        tokens_full = sem("tokens_full")
        tokens_ready = sem("tokens_ready")
        tokens_step = sem("tokens_step")
        x_saved = sem("x_saved")
        rows_loaded = [sem(f"rows_loaded{k}") for k in range(2)]
        rowsT_full = sem("rowsT_full")
        rowsT_ready = sem("rowsT_ready")
        up_full = sem("up_full")
        gate_ready = sem("gate_ready")
        hidden_ready = sem("hidden_ready")
        hiddenT_full = sem("hiddenT_full")
        hiddenT_ready = sem("hiddenT_ready")
        y_full = sem("y_full")
        y_copied = sem("y_copied")
        y_saved = [sem(f"y_saved{k}") for k in range(2)]
        returned = [sem(f"returned{i}") for i in range(B)]
        y_added = sem("y_added")

        S_BANKS, ST_BANKS, PT_BUFS, OT_BUFS = 3, 2, 2, 2
        N_LOADS, N_LATE_LOADS = 6, 12
        GROUPS_OF = ((GROUPS + 1) // 2, GROUPS // 2)
        XT_PS = (s_ps[0], s_ps[1])
        dist = s_ps[2][:, 0:TILES * E].rearrange("p (t e) -> p t e", e=E)
        NORMALIZED_AT = {QUADS * B + 2: range(3), QUADS * B + 3: range(3, 6), QUADS * B + 4: range(6, 7)}
        TRANSPOSED_AT = {QUADS * B + 2: range(2), QUADS * B + 3: range(2, 4), QUADS * B + 4: range(4, 7)}

        def routed_in(at, g, q, layer):
            return at.get(QUADS * (g - layer * B) + q, ()) if isinstance(g, int) else ()

        block = ctx.enter_context(nc.Block())

        def tok(t):
            return slice(t * P, (t + 1) * P)

        def run_slots(eng, layer, slot):
            b0 = layer * B
            for n in range(QUADS + 1):
                slot(b0 + n // QUADS, n // QUADS % 2, b0 // 2, n % QUADS)
            with eng.Fori(b0 // 2, b0 // 2 + B // 2 - 1) as i:
                for k in (1, 2):
                    for q in (1, 2, 3):
                        slot(2 * i + k, k % 2, i + k // 2, q)
                    slot(2 * i + k + 1, (k + 1) % 2, i + (k + 1) // 2, 0)
            for n in range(QUADS * (B - 1) + 1, QUADS * (B + 1) + 1):
                slot(b0 + n // QUADS, n // QUADS % 2, b0 // 2 + n // QUADS // 2, n % QUADS)

        def earlier(g, p, h, q, lag):
            if q >= lag:
                return g, p, q - lag
            return g - 1, 1 - p, q + QUADS - lag

        VALUES_AT = (2, 4, 7, 8)

        def within(g, layer):
            return not isinstance(g, int) or layer * B <= g < layer * B + B

        @block.sync
        def _(sp):
            def load(dst, src, loaded=loaded):
                sp.dma_start(dst, src).then_inc(loaded, 16)

            def load_late(dst, src):
                load(dst, src, loaded_late)

            for i in range(B):
                sp.dma_start(x_sb[:, i * NT:(i + 1) * NT, :],
                             x_in[i].rearrange("(t p) c -> p t c", p=P)).then_inc(loaded_x[min(i, 1)], 16)
                if i == 0:
                    for n, (w, b) in enumerate(((Wq, bq), (Wk, bk))):
                        load(w_natural[:, n, :], w)
                        load(b_natural[:, n, :], b.rearrange("(o c) -> o c", o=1))
                    load(w_v[:, 0, :], Wv)
                    load(b_v[:, 0, :], bv.rearrange("(o c) -> o c", o=1))
            load_late(w_o[:], Wo)
            load_late(b_o[:], bo.rearrange("(o c) -> o c", o=1))
            load_late(w_dq[:], Wdq)
            load_late(w_uq[:], Wuq)
            load_late(w_dkv[:], Wdkv)
            load_late(w_uk[:], Wuk)
            load_late(w_uv[:], Wuv)
            load_late(w_ob[:], Wob)
            load_late(scale_col[:], ffn_scale.rearrange("(c o) -> c o", o=1))
            load_late(cent[:], centroids)
            load_late(w_up[:], up_w.rearrange("e d n -> d e n"))
            load_late(w_down[:], down_w.rearrange("e (c f) d -> f e c d", c=FC))

            def place_max(g, p, q):
                sp.wait_ge(max_parts_ready, 4 * g + q + 1)
                for half in range(2):
                    for part in range(MROWS):
                        row = half * 64 + STACK + part
                        dst = q_stack[row:row + 1, p, 2 * q:2 * q + 2, :]
                        sp.dma_start(dst.rearrange("o j (t q) -> o (j t) q", q=P),
                                     max_parts[8 * half:8 * half + 8, q, part, :]
                                     ).then_inc(max_placed[q % 2], 16)

            def save_rows(g, ready, parts, rows, runs, saved):
                sp.wait_ge(ready, 1 + g + 1)
                for half in range(2):
                    r = slice(64 * half, 64 * half + 64)
                    for slot, n, part, part_step in runs:
                        src = (parts[r, part:part + n, :] if part_step else
                               parts[r, part, :].unsqueeze(1).broadcast_to([64, n, S]))
                        sp.dma_start(rows[half, slot:slot + n].rearrange("s r t -> r s t"), src).then_inc(saved, 16)

            Q_RUNS = ((0, 3, 0, 1), (3, 2, 0, 1), (5, 1, 0, 1))
            K_RUNS = ((0, 3, 0, 0), (3, 2, 1, 0), (5, 1, 2, 0))

            def save_keys(g):
                save_rows(g, k3_ready, k3, k_rows, K_RUNS, k3_saved)

            def save_queries(g):
                save_rows(g, q3_ready, q3, q_rows, Q_RUNS, q3_saved)

            def load_stacks(g, p, pair):
                if isinstance(g, int) and g < 2:
                    sp.wait_ge(ones_ready, 2 * g + 2)
                sp.wait_ge(k3_saved, 96 * g + 96)
                sp.wait_ge(q3_saved, 96 * g + 96)
                for rows, stack in ((k_rows, k_stack), (q_rows, q_stack)):
                    for half in range(2):
                        sp.dma_start(stack[half * 64:half * 64 + STACK, p, 4 * pair:4 * pair + 4, :],
                                     rows[half].rearrange("s (d j) t -> (s d) j t", j=NJ)[:, 4 * pair:4 * pair + 4, :]
                                     ).then_inc(stacked[p][pair], 16)

            def save_x(ffn):
                for b in range(B):
                    sp.wait_ge(xs_ready, ffn * B + b + 1)
                    sp.dma_start(x_rows[b * S:(b + 1) * S, :].rearrange("(t p) c -> p t c", p=P),
                                 x_routed[:, b * NT:(b + 1) * NT, :]).then_inc(x_saved, 16)

            def load_y(ffn):
                for k in range(2):
                    sp.wait_ge(y_saved[k], 16 * GROUP * GROUPS_OF[k] * (ffn + 1))
                for b in range(B):
                    sp.dma_start(y_routed[:, b * NT:(b + 1) * NT, :],
                                 y_rows[b * S:(b + 1) * S, :].rearrange("(t p) c -> p t c", p=P)
                                 ).then_inc(returned[b], 16)

            for layer in range(2):
                if layer == 1:
                    sp.wait_ge(stacked[1][1], 64 * (B // 2))
                save_keys(layer * B)
                save_queries(layer * B)
                for pair in range(2):
                    load_stacks(layer * B, 0, pair)

                def slot(g, p, h, q):
                    g1, p1, q1 = earlier(g, p, h, q, 1)
                    if within(g1, layer):
                        place_max(g1, p1, q1)
                    if q == 1 and within(g + 1, layer):
                        sp.wait_ge(stacked[p][1], 64 * (h + 1))
                        sp.sem_inc(sp_waited, 1)
                        save_keys(g + 1)
                    if q == 2 and within(g + 1, layer):
                        save_queries(g + 1)
                    if q >= 2 and within(g + 1, layer):
                        if not (isinstance(g, int) and g == layer * B):
                            sp.wait_ge(st_full, 40 * g - 20 if q == 2 else 40 * g)
                            sp.sem_inc(sp_waited, 1)
                        load_stacks(g + 1, 1 - p, q - 2)

                run_slots(sp, layer, slot)
                save_x(layer)
                load_y(layer)
            with sp.Fori(0, B) as i:
                sp.wait_ge(y_added, B + i + 1)
                sp.dma_start(out[i].rearrange("(t p) c -> p t c", p=P),
                             x_sb[:, bass.ds(i * NT, NT), :]).then_inc(stored, 16)
            sp.wait_ge(stored, 16 * B)

        @block.gpsimd
        def _(pool):
            def settle():
                pool.sem_inc(pool_waited, 1)

            def step(ins, n):
                ins.then_inc(pool_step, 1)
                pool.wait_ge(pool_step, n)
                if not isinstance(n, int):
                    settle()

            pool.memset(ones_mat[:], 1.0).then_inc(setup_step, 2)
            step(pool.memset(ident[:], 0.0), 1)
            step(pool.affine_select(out=ident[:], in_=ident[:], compare_op=ALU.not_equal, fill=1.0, base=0,
                                    pattern=[[-1, P]], channel_multiplier=1), 2)
            pool.tensor_copy(ident_bf[:], ident[:]).then_inc(consts_ready, 1)
            step(pool.memset(mask2[:], 0.0), 3)
            pool.affine_select(out=mask2[:], in_=mask2[:], compare_op=ALU.is_ge, fill=MASKED, base=0,
                               pattern=[[0, 2], [-1, P]], channel_multiplier=1).then_inc(consts_ready, 1)
            pool.memset(causal[:], 0.0).then_inc(causal_step, 1)
            pool.wait_ge(causal_step, 1)
            pool.affine_select(out=causal[:, S - P:], in_=causal[:, S - P:], compare_op=ALU.is_ge, fill=MASKED, base=0,
                               pattern=[[-1, P]], channel_multiplier=1).then_inc(causal_step, 1)
            step(pool.memset(mask2T[:], 0.0), 4)
            pool.affine_select(out=mask2T[:], in_=mask2T[:], compare_op=ALU.is_ge, fill=MASKED, base=0,
                               pattern=[[0, 2], [1, P]], channel_multiplier=-1).then_inc(consts_ready, 1)
            pool.memset(ones_row[:], 1.0).then_inc(consts_ready, 1)
            pool.memset(minus_half[:], -0.5).then_inc(consts_ready, 1)
            pool.iota(expert_row[:], pattern=[[0, TILES], [1, E]], base=0, channel_multiplier=0,
                      allow_small_or_imprecise_dtypes=True).then_inc(setup_step, 1)
            for numbers, pattern, base, step_p in ((slot_no, [[1, SLOTS]], 0, 0), (row_no, [[1, P]], 0, 0),
                                                   (tile_no, [[1, TILES]], 0, 0), (token_no, [[0, 1]], 1, 1),
                                                   (unused_row, [[P, SLOTS]], TILES * P + 1, 1)):
                pool.iota(numbers[:], pattern=pattern, base=base, channel_multiplier=step_p,
                          allow_small_or_imprecise_dtypes=True).then_inc(setup_step, 1)
            pool.memset(counts[:], 0.0).then_inc(setup_step, 1)
            pool.memset(slots_f[:], 0.0).then_inc(setup_step, 1)
            pool.wait_ge(setup_step, 10)
            pool.affine_select(out=before[:], in_=ones_mat[:], compare_op=ALU.is_gt, fill=0.0, base=0,
                               pattern=[[1, P]], channel_multiplier=-1).then_inc(setup_step, 1)
            pool.wait_ge(setup_step, 11)
            pool.tensor_copy(before_bf[:], before[:]).then_inc(setup_step, 1)
            pool.tensor_copy(ones_bf[:], ones_mat[:]).then_inc(setup_step, 1)
            pool.wait_ge(setup_step, 13)
            pool.memset(v_ext[:], 0.0).then_inc(consts_ready, 1)
            pool.wait_ge(consts_ready, 6)
            pool.memset(v_ext[:, :, :, :, DH:DH + 1], 1.0).then_inc(consts_ready, 1)
            pool.memset(credit[:, 1:2], 0.0).then_inc(q3_ready, 1)
            pool.memset(credit[:, 8:9], 0.0).then_inc(rstd_ready, 1)
            STEP0 = 4
            STEPS = 2 + 4

            def attention_root(layer, part):
                tiles = slice(0, NT) if part == 0 else slice(NT, TILES)
                n = 2 * layer + part + 1
                pool.wait_ge(att_mean_ready, n)
                pool.tensor_scalar(att_var_eps[:, tiles], att_mean_var[:, tiles, 1], LN_EPS, None,
                                   ALU.add).then_inc(att_root_step, 1)
                pool.wait_ge(att_root_step, n)
                pool.tensor_tensor(out=att_rstd[:, tiles], in0=att_var_eps[:, tiles], in1=minus_half[:, tiles],
                                   op=ALU.pow).then_inc(att_rstd_ready, 1)

            def split_queries(g, base):
                pool.wait_ge(qf_ready, g + 1)
                settle()
                step(pool.tensor_tensor(out=q_rest[:], in0=qf[:], in1=q3[:, 0, :], op=ALU.subtract), base + 1)
                step(pool.tensor_copy(q3[:, 1, :], q_rest[:]), base + 2)
                pool.tensor_tensor(out=q3[:, 2, :], in0=q_rest[:], in1=q3[:, 1, :],
                                   op=ALU.subtract).then_inc(q3_ready, 1)

            def split_max(g, base, q):
                pool.wait_ge(maxT_ready, 4 * g + q + 1)
                settle()
                step(pool.tensor_copy(max_parts[:, q, 0, :], neg_maxT[:, q, :]), base + 1)
                pool.tensor_tensor(out=max_parts[:, q, 1, :], in0=neg_maxT[:, q, :],
                                   in1=max_parts[:, q, 0, :], op=ALU.subtract).then_inc(max_parts_ready, 1)

            def add_bias(g):
                x_rows_of = x_sb[:, bass.ds(g * NT, NT), :]
                if isinstance(g, int) and g == 0:
                    pool.wait_ge(fold_copied, 11)
                pool.wait_ge(xn_ready, g + 1)
                settle()
                pool.tensor_tensor(out=x_rows_of, in0=x_rows_of,
                                   in1=out_bias[:].unsqueeze(1).broadcast_to([P, NT, C]),
                                   op=ALU.add).then_inc(bias_added, 1)

            def ffn_root(g, ffn):
                n = [6 * g]

                def next_reads(ins):
                    ins.then_inc(ffn_pool_step, 1)
                    n[0] = n[0] + 1
                    pool.wait_ge(ffn_pool_step, n[0])
                    settle()

                tiles = bass.ds((g - ffn * B) * NT, NT)
                half = minus_half[:, 0:NT]
                pool.wait_ge(mean_ready, g + 1)
                settle()
                next_reads(pool.tensor_scalar(rms[:, 0, :], batch_mean_var[:, :, 1], LN_EPS, None, ALU.add))
                next_reads(pool.tensor_tensor(out=rms[:, 1, :], in0=rms[:, 0, :], in1=half, op=ALU.pow))
                next_reads(pool.tensor_tensor(out=rms[:, 2, :], in0=batch_mean_var[:, :, 1], in1=rms[:, 1, :],
                                              op=ALU.mult))
                next_reads(pool.tensor_tensor(out=rms[:, 3, :], in0=rms[:, 2, :], in1=rms[:, 1, :], op=ALU.mult))
                next_reads(pool.tensor_scalar(rms[:, 4, :], rms[:, 3, :], RMS_EPS, None, ALU.add))
                next_reads(pool.tensor_tensor(out=rms[:, 5, :], in0=rms[:, 4, :], in1=half, op=ALU.pow))
                pool.tensor_tensor(out=to_xl[:, tiles], in0=rms[:, 4, :], in1=rms[:, 5, :], op=ALU.mult)
                pool.tensor_tensor(out=both_rstd[:, tiles], in0=rms[:, 5, :], in1=rms[:, 1, :],
                                   op=ALU.mult).then_inc(rstd_ready, 1)

            def number_tiles(ffn):
                pool.wait_ge(slots_marked, ffn + 1)
                pool.tensor_tensor(out=slot_hot[:, :, 1, :], in0=slot_hot[:, :, 0, :],
                                   in1=tile_no[:].unsqueeze(2).broadcast_to([P, TILES, SLOTS]),
                                   op=ALU.mult).then_inc(tiles_numbered, 1)

            def move_rows(ffn):
                w0 = ffn * GROUPS

                def fetch(w):
                    if w >= 2:
                        pool.wait_ge(rowsT_full, w0 + w - 1)
                    for j in range(GROUP):
                        n = GROUP * w + j
                        pool.indirect_dma_start(rows[:, w % 2, j, :], None, x_rows,
                                                bass.IndirectOffsetOnAxis(ap=read_row[:, n:n + 1], axis=0)
                                                ).then_inc(rows_loaded[w % 2], 16)

                def send(w):
                    pool.wait_ge(y_copied, w0 + w + 1)
                    for j in range(GROUP):
                        n = GROUP * w + j
                        pool.indirect_dma_start(y_rows, bass.IndirectOffsetOnAxis(ap=write_row[:, n:n + 1], axis=0),
                                                y_out[:, w % 2, j, :], None).then_inc(y_saved[w % 2], 16)

                pool.wait_ge(tokens_ready, ffn + 1)
                pool.wait_ge(x_saved, 16 * B * (ffn + 1))
                fetch(0)
                fetch(1)
                for w in range(GROUPS):
                    if w + 2 < GROUPS:
                        fetch(w + 2)
                    if w >= 1:
                        send(w - 1)
                send(GROUPS - 1)

            for layer in range(2):
                attention_root(layer, 0)
                attention_root(layer, 1)

                def slot(g, p, h, q):
                    g1, p1, q1 = earlier(g, p, h, q, 1)
                    base = STEP0 - 2 * layer + STEPS * g
                    if within(g1, layer):
                        if q == 0:
                            n = base - 1 if within(g, layer) else base - 1 - 2
                        else:
                            n = base + q - 1 + (2 if q >= 2 and within(g + 1, layer) else 0)
                        split_max(g1, n, q1)
                    if q == 1 and within(g + 1, layer):
                        split_queries(g + 1, base + 1)
                    if q == 0 and within(g - 2, layer):
                        ffn_root(g - 2, layer)
                    if q == 3 and layer == 0 and within(g, layer):
                        add_bias(g)

                run_slots(pool, layer, slot)
                number_tiles(layer)
                move_rows(layer)

        def s_bank(k):
            if k < 2:
                return [(k, NT - 1, 0)]
            if k < 4:
                return [(k - 2, 2, 0), (k - 2, 0, 3 * P)]
            return [(0, 1, 0), (1, 1, 2 * P)]

        def st_bank(k):
            if k < 2:
                return [(k, 0, 0)]
            if k < 4:
                return [(k - 2, 1, 0), (k - 2, 3, 3 * P)]
            return [(0, 2, 0), (1, 2, 2 * P)]

        @block.tensor
        def _(pe):
            def mm(o, l, r, start=True, stop=True, **kw):
                return pe.matmul(o, l, r, start=start, stop=stop, skip_group_check=True, **kw)

            pe.wait_ge(consts_ready, 7)
            pe.wait_ge(causal_step, 2)
            mm(s_ps[0][:, 0:P], ident_bf[:], ident_bf[:]).then_inc(xT_full, 1)
            mm(s_ps[1][:, 0:P], ident_bf[:], ident_bf[:]).then_inc(pv_done, PT_BUFS)
            mm(s_ps[2][:, 0:P], ident_bf[:], ident_bf[:]).then_inc(oTT_full, OT_BUFS)

            

            pe.wait_ge(loaded, 16 * N_LOADS)
            pe.wait_ge(ordered, 1)
            for n in range(2):
                ins = mm(d_ps[:, n * E:n * E + E], b_ordered[:, n, :], ones_row[:, 0:E])
            ins.then_inc(bias_full, 1)

            def fold():
                pe.wait_ge(loaded_late, 16 * N_LATE_LOADS)
                pe.wait_ge(v_ready, 2)
                pe.transpose(a_ps[:L, 0:C], w_uq[:], ident[:, :]).then_inc(fold_done, 1)
                pe.transpose(d_ps[:, 0:C], w_ob[:], ident[:, :]).then_inc(fold_done, 1)
                pe.wait_ge(fold_copied, 2)
                mm(a_ps[:, 0:C], w_dq[:], w_uqT[:]).then_inc(fold_done, 1)
                mm(d_ps[:, 0:C], w_uqT[:], w_dq[:]).then_inc(fold_done, 1)
                pe.wait_ge(fold_copied, 4)
                mm(a_ps[:L, 0:C], w_uk[:], qeffT[:]).then_inc(fold_done, 1)
                mm(d_ps[:L, 0:C], w_uv[:], w_obT[:]).then_inc(fold_done, 1)
                pe.wait_ge(fold_copied, 6)
                mm(a_ps[:, 0:C], w_dkv[:], keffT[:]).then_inc(fold_done, 1)
                mm(d_ps[:, 0:C], w_dkv[:], veff[:]).then_inc(fold_done, 1)
                pe.wait_ge(fold_copied, 8)
                pe.transpose(a_ps[:, 0:E], cent[:], ident[0:E, 0:E]).then_inc(fold_done, 1)
                mm(d_ps[:, 0:C], b_v[:, 0, :], ones_row[:]).then_inc(fold_done, 1)
                pe.wait_ge(fold_copied, 10)
                mm(d_ps[:, 0:C], b_v_cols[:], w_o[:], start=True, stop=False)
                mm(d_ps[:, 0:C], ones_row[:], b_o[:], start=False).then_inc(fold_done, 1)
                pe.wait_ge(fold_copied, 11)

            def transpose_x(g):
                pe.wait_ge(xn_ready, g + 1)
                for t in range(NT):
                    ins = pe.transpose(a_ps[:, tok(t)], xn[:, t, :], ident[:, :])
                ins.then_inc(xT_full, 1)

            def project_q(g, layer):
                pe.wait_ge(kf_ready, g + 1)
                mm(a_ps[:], w_q[:, layer, :], xnT[:]).then_inc(q_full, 1)

            def project_k(g, layer):
                pe.wait_ge(xT_ready, g + 1)
                mm(a_ps[:], w_k[:, layer, :], xnT[:]).then_inc(k_full, 1)

            def project_v(g, layer):
                pe.wait_ge(qf_ready, g + 1)
                for t in range(NT):
                    ins = mm(a_ps[:, tok(t)], xnT[:, tok(t)], w_v[:, layer, :], start=(t == 0))
                ins.then_inc(v_full, 1)

            def scores(g, p, q, u):
                half, k = u % 2, u // 2
                n = 40 * g + 10 * q + u
                pe.wait_ge(s_free, S_BANKS + n if 10 * q + u == 0 else n + 1)
                ps = s_ps[(10 * q + u) % S_BANKS]
                if k == 4:
                    mm(ps[:, :].rearrange("p (n w) -> p n w", n=2)[:, :, P:2 * P], ident_bf[:], mask2[:],
                       start=True, stop=False)
                r = slice(64 * half, 64 * half + STACK)
                for n, (head, t, col) in enumerate(s_bank(k)):
                    w = (t + 1) * P
                    ins = mm(ps[:, col:col + w], q_stack[r, p, 2 * q + head, tok(t)],
                             k_stack[r, p, 2 * q + head, 0:w], start=(n == 0 and k < 4),
                             tile_position=(64 * half, 0))
                ins.then_inc(s_full, 1)

            def scores_T(g, p, q, u):
                half, k = u % 2, u // 2
                n = 40 * g + 10 * q + u
                pe.wait_ge(exp_done, n + 1)
                ps = st_ps[(10 * q + u) % ST_BANKS]
                r = slice(64 * half, 64 * half + STACK + MROWS)
                blocks = ps[:].rearrange("p (n w) -> p n w", w=P)[:, ::DIAGONAL[k], :]
                mm(blocks, ident_bf[:], mask2T[:, 0:blocks.shape[1], :], start=True, stop=False)
                for head, t, col in st_bank(k):
                    w = S - t * P
                    ins = mm(ps[:, col:col + w], k_stack[r, p, 2 * q + head, tok(t)],
                             q_stack[r, p, 2 * q + head, t * P:S], start=False, tile_position=(64 * half, 0))
                ins.then_inc(st_full, 1)

            def weigh_values(g, p, q, t):
                n = 4 * g + q
                if t == 0:
                    pe.wait_ge(oT_ready, n + 1)
                pe.wait_ge(exp_done, ST_BANKS + 40 * g + 10 * q + (4, 8, 10, 8)[t])
                for half in range(2):
                    for head in range(2):
                        k = (head, 2 + head, 4, 2 + head)[t]
                        col = (0, 0, 2 * P * head, 3 * P)[t]
                        c = 2 * half + head
                        w = S - t * P
                        ins = mm(pv_ps[32 * c:32 * c + 32, t * P:S], v_ext[:, p, t, 4 * q + c, :],
                                 probs[:, q % 2, 2 * k + half, col:col + w], start=(t == 0), stop=(t == NT - 1),
                                 tile_position=(0, 32 * c))
                if t == NT - 1:
                    ins.then_inc(pv_done, 1)

            def d_ps_left(g_slot, q_slot, layer):
                if not isinstance(g_slot, int) or 4 * g_slot + q_slot > 4:
                    pe.wait_ge(attn_ready, 4 * g_slot + q_slot - 4)

            def transpose_max(g, q, g_slot, q_slot, layer):
                pe.wait_ge(s_free, S_BANKS + 40 * g + 10 * (q + 1))
                d_ps_left(g_slot, q_slot, layer)
                pe.transpose(d_ps[0:16, 0:P], neg_max[:, q, :], ident[:, :]).then_inc(maxT_full, 1)

            def transpose_o(g, q):
                n = 4 * g + q
                pe.wait_ge(oT_ready, 1 + n + 1)
                for t in range(NT):
                    ins = pe.transpose(d_ps[:, tok(t)], o_T[:, q % 2, tok(t)], ident[:, :])
                ins.then_inc(oTT_full, 1)

            def transpose_attn(g):
                pe.wait_ge(attn_ready, 4 * g + 4)
                for t in range(NT):
                    ins = pe.transpose(a_ps[:, tok(t)], attn[:, t, :], ident[:, :])
                ins.then_inc(attnT_full, 1)

            def project_out(g):
                pe.wait_ge(attnT_ready, 1 + g + 1)
                for t in range(NT):
                    ins = mm(d_ps[:, tok(t)], attnT[:, tok(t)], w_o[:], start=(t == 0))
                ins.then_inc(proj_full, 1)

            def distances(b, ffn):
                pe.wait_ge(norm_sq_ready, ffn * B + b + 1)
                if b == 0:
                    mm(dist, ones_mat[:], cent_sqT[:].unsqueeze(1).broadcast_to([P, TILES, E]), start=True, stop=False)
                for t in range(NT):
                    o = dist[:, b * NT + t, :]
                    mm(o, xsT[b % 2][:, tok(t)], cent_m2T[:], start=False, stop=False)
                    ins = mm(o, xsT_sq[b % 2][:, tok(t)], ones_mat[:, 0:E], start=False)
                ins.then_inc(dist_full, 1)

            def route(b, ffn):
                pe.wait_ge(xs_ready, ffn * B + b + 1)
                for t in range(NT):
                    ins = pe.transpose(XT_PS[b % 2][:, tok(t)], x_routed[:, b * NT + t, :], ident[:, :])
                ins.then_inc(xsT_full, 1)
                if b > 0:
                    distances(b - 1, ffn)

            def count_tokens():
                mm(s_ps[0][:, 0:E * TILES], before_bf[:], one_hot[:].rearrange("p e t -> p (e t)"))
                mm(s_ps[1][:, 0:E * TILES], ones_bf[:], one_hot[:].rearrange("p e t -> p (e t)")
                   ).then_inc(counts_full, 1)

            def find_tokens(ffn):
                pe.wait_ge(slots_numbered, ffn + 1)
                pe.wait_ge(tiles_numbered, ffn + 1)
                pe.wait_ge(rows_marked, ffn + 1)
                for t in range(TILES):
                    ins = mm(s_ps[0][:, 0:2 * SLOTS], row_hot[:, t, :],
                             slot_hot[:, t, 1:3, :].rearrange("p n s -> p (n s)"), start=(t == 0),
                             stop=(t == TILES - 1))
                ins.then_inc(tokens_full, 1)

            def experts(ffn):
                w0 = ffn * GROUPS
                hT_ps = (st_ps[0], st_ps[1], pv_ps)

                def transpose_rows(k, m):
                    pe.wait_ge(rows_loaded[k], 16 * GROUP * (m + 1 + GROUPS_OF[k] * ffn))
                    for j in range(GROUP):
                        ins = pe.transpose(a_ps[:, j * P:(j + 1) * P], rows[:, k, j, :], ident[:, :])
                    ins.then_inc(rowsT_full, 1)

                def up(w):
                    pe.wait_ge(rowsT_ready, w0 + w + 1)
                    for j in range(GROUP):
                        e = pe.value_load(slot_expert[0:1, bass.ds(w * GROUP + j, 1)], min_val=0, max_val=E - 1)
                        mm(s_ps[j][:, 0:2 * F], rowsT[:, j, :],
                           w_up[:, bass.ds(e, 1), :].rearrange("p o n -> p (o n)")).then_inc(up_full, 1)

                def transpose_hidden(w):
                    for j in range(GROUP):
                        pe.wait_ge(hidden_ready, GROUP * (w0 + w) + j + 1)
                        for c in range(FC):
                            ins = pe.transpose(hT_ps[j][:, c * P:(c + 1) * P], hidden[:, j, c * P:(c + 1) * P],
                                               ident[:, :])
                        ins.then_inc(hiddenT_full, 1)

                def down(w):
                    for j in range(GROUP):
                        e = pe.value_load(slot_expert[0:1, bass.ds(w * GROUP + j, 1)], min_val=0, max_val=E - 1)
                        pe.wait_ge(hiddenT_ready, GROUP * (w0 + w) + j + 1)
                        for c in range(FC):
                            ins = mm(d_ps[:, j * P:(j + 1) * P], hiddenT[:, j, c * P:(c + 1) * P],
                                     w_down[:, bass.ds(e, 1), c, :].rearrange("p o n -> p (o n)"),
                                     start=(j == 0 and c == 0), stop=(c == FC - 1))
                    ins.then_inc(y_full, 1)

                def group(w, k, m):
                    transpose_hidden(w)
                    up(w + 1)
                    transpose_rows(k, m + 1)
                    down(w)

                transpose_rows(0, 0)
                up(0)
                transpose_rows(1, 0)
                with pe.Fori(0, (GROUPS - 3) // 2) as i:
                    group(2 * i, 0, i)
                    group(2 * i + 1, 1, i)
                group(GROUPS - 3, 0, (GROUPS - 3) // 2)
                transpose_hidden(GROUPS - 2)
                up(GROUPS - 1)
                down(GROUPS - 2)
                transpose_hidden(GROUPS - 1)
                down(GROUPS - 1)

            for layer in range(2):
                b0 = layer * B
                transpose_x(b0)
                project_k(b0, layer)
                project_q(b0, layer)
                project_v(b0, layer)
                if layer == 0:
                    fold()

                def slot(g, p, h, q):
                    g1, p1, q1 = earlier(g, p, h, q, 1)
                    g2, p2, q2 = earlier(g, p, h, q, 2)
                    g3, p3, q3_ = earlier(g, p, h, q, 3)
                    g4 = g - 1
                    if within(g, layer) and q % 2 == 0:
                        pe.wait_ge(stacked[p][q // 2], 64 * (h + 1))
                    for u in range(10):
                        if within(g, layer):
                            scores(g, p, q, u)
                        if u == 5 and within(g2, layer):
                            pe.wait_ge(max_placed[q2 % 2], 64 * (2 * g2 + q2 // 2 + 1))
                        if u >= 5 and within(g2, layer):
                            scores_T(g2, p2, q2, u - 5)
                        if u < 5 and within(g3, layer):
                            scores_T(g3, p3, q3_, u + 5)
                        if q == 1 and within(g + 1, layer):
                            if u == 3:
                                pe.wait_ge(v_ready, 1 + g + 1)
                                if layer == 0 and within(g - 2, layer):
                                    pe.wait_ge(attnT_ready, g)
                                transpose_x(g + 1)
                            if u == 5:
                                project_k(g + 1, layer)
                            if u == 8:
                                project_q(g + 1, layer)
                        if q == 3 and u == 1 and within(g + 1, layer):
                            project_v(g + 1, layer)
                        if u == 1 and within(g1, layer):
                            transpose_max(g1, q1, g, q, layer)
                        if q == 0 and layer == 0 and within(g - 2, layer):
                            if u == 1:
                                last = min(g + 1, b0 + B) if isinstance(g, int) else g
                                pe.wait_ge(v_ready, 1 + last)
                                transpose_attn(g - 2)
                            if u == 3:
                                if within(g1, layer):
                                    pe.wait_ge(maxT_ready, 4 * g + q)
                                else:
                                    d_ps_left(g, q, layer)
                                project_out(g - 2)
                        if u == 6 and within(g4, layer):
                            if q == 0 and layer == 0 and within(g - 2, layer):
                                pe.wait_ge(x_updated, g)
                            elif within(g1, layer):
                                pe.wait_ge(maxT_ready, 4 * g + q)
                            else:
                                d_ps_left(g, q, layer)
                            transpose_o(g4, q)
                        if u in VALUES_AT and within(g3, layer):
                            weigh_values(g3, p3, q3_, VALUES_AT.index(u))
                    for b in routed_in(TRANSPOSED_AT, g, q, layer):
                        route(b, layer)

                run_slots(pe, layer, slot)
                pe.wait_ge(x_updated, 1 + B * (layer + 1))
                route(B - 1, layer)
                distances(B - 1, layer)
                pe.wait_ge(routed, layer + 1)
                count_tokens()
                find_tokens(layer)
                pe.wait_ge(place_ready, layer + 1)
                experts(layer)

        @block.scalar
        def _(act):
            def fill_ones(p):
                act.wait_ge(setup_step, 2)
                for half in range(2):
                    rows = slice(half * 64 + 32, half * 64 + 64)
                    act.copy(k_stack[rows, p, :, :].rearrange("r j s -> r (j s)"),
                             ones_mat[rows, 0:1].broadcast_to([32, NJ * S])).then_inc(ones_ready, 1)

            fill_ones(0)
            act.wait_ge(consts_ready, 7)
            act.copy(credit[0:1, 4:5], ones_row[0:1, 0:1]).then_inc(exp_done, ST_BANKS)
            act.copy(credit[0:1, 5:6], ones_row[0:1, 0:1]).then_inc(oT_ready, 1)
            act.copy(credit[0:1, 6:7], ones_row[0:1, 0:1]).then_inc(v_ready, 1)
            act.copy(credit[32:33, 4:5], ones_mat[32:33, 0:1]).then_inc(attnT_ready, 1)

            def copy_xT(g):
                act.wait_ge(xT_full, 1 + g + 1)
                act.copy(xnT[:], a_ps[:]).then_inc(xT_ready, 1)

            def scale_xT(b, ffn):
                act.wait_ge(loaded_late, 16 * N_LATE_LOADS)
                act.wait_ge(xsT_full, ffn * B + b + 1)
                if ffn * B + b >= 2:
                    act.wait_ge(dist_full, ffn * B + b - 1)
                act.activation(xsT[b % 2][:], XT_PS[b % 2][:], ACT.Identity, scale=scale_col[:, 0:1])
                act.activation(xsT_sq[b % 2][:], XT_PS[b % 2][:], ACT.Square, scale=scale_col[:, 0:1]
                               ).then_inc(norm_sq_ready, 1)

            def expert_group(w):
                for j in range(GROUP):
                    act.wait_ge(up_full, GROUP * w + j + 1)
                    act.activation(gate[:, j, :], s_ps[j][:, F:2 * F], ACT.Silu).then_inc(gate_ready, 1)

            def number_partitions(ffn):
                act.wait_ge(slots_marked, ffn + 1)
                act.activation(slot_hot[:, :, 2, :], slot_hot[:, :, 0, :], ACT.Identity,
                               scale=token_no[:, 0:1]).then_inc(slots_numbered, 1)

            def copy_rowsT(w):
                act.wait_ge(rowsT_full, w + 1)
                act.activation(rowsT[:].rearrange("p s t -> p (s t)"), a_ps[:, 0:GROUP * P], ACT.Identity,
                               scale=scale_col[:, 0:1]).then_inc(rowsT_ready, 1)

            def copy_q(g, layer):
                act.wait_ge(q_full, g + 1)
                act.wait_ge(q3_ready, g + 1)
                bias = {"bias": b_qk[:, 0, 0:1]} if layer == 0 else {}
                act.activation(q3[:, 0, :], a_ps[:], ACT.Identity, **bias)
                act.activation(qf[:], a_ps[:], ACT.Identity, **bias).then_inc(qf_ready, 1)

            def copy_k(g, layer):
                act.wait_ge(k_full, g + 1)
                act.wait_ge(k3_ready, g + 1)
                if layer == 0:
                    act.wait_ge(bias_ready, 1)
                bias = {"bias": b_qk[:, 1, 0:1]} if layer == 0 else {}
                act.activation(k3[:, 0, :], a_ps[:], ACT.Identity, **bias)
                act.activation(kf[:], a_ps[:], ACT.Identity, **bias).then_inc(kf_ready, 1)

            def copy_v(g, p):
                act.wait_ge(v_full, g + 1)
                ins = act.copy(v_ext[:, p, :, :, 0:DH], a_ps[:].rearrange("p (t h d) -> p t h d", t=NT, h=H))
                ins.then_inc(v_ready, 1)

            def exp(g, q, u):
                if u == 0:
                    act.wait_ge(pv_done, 4 * g + q + 1)
                act.wait_ge(st_full, 40 * g + 10 * q + u + 1)
                act.activation(probs[:, q % 2, u, :], st_ps[(10 * q + u) % ST_BANKS][:], ACT.Exp,
                               scale=SCALE).then_inc(exp_done, 1)

            def copy_oT(g, q):
                n = 4 * g + q
                act.wait_ge(pv_done, PT_BUFS + n + 1)
                act.wait_ge(oTT_full, n + 1)
                act.copy(o_T[:, q % 2, :], pv_ps[:]).then_inc(oT_ready, 1)

            for layer in range(2):
                b0 = layer * B
                copy_xT(b0)
                copy_k(b0, layer)
                copy_q(b0, layer)
                copy_v(b0, 0)
                if layer == 0:
                    fill_ones(1)

                def slot(g, p, h, q):
                    g2, p2, q2 = earlier(g, p, h, q, 2)
                    g3, p3, q3_ = earlier(g, p, h, q, 3)
                    if within(g - 1, layer):
                        copy_oT(g - 1, q)
                    for u in range(10):
                        if u >= 5 and within(g2, layer):
                            exp(g2, q2, u - 5)
                        if u < 5 and within(g3, layer):
                            exp(g3, q3_, u + 5)
                        if q == 1 and within(g + 1, layer):
                            if u == 4:
                                copy_xT(g + 1)
                            if u == 6:
                                copy_k(g + 1, layer)
                            if u == 8:
                                copy_q(g + 1, layer)
                        if q == 3 and u == 2 and within(g + 1, layer):
                            copy_v(g + 1, 1 - p)
                        if q == 0 and u == 2 and layer == 0 and within(g - 2, layer):
                            act.wait_ge(attnT_full, g - 1)
                            act.copy(attnT[:], a_ps[:]).then_inc(attnT_ready, 1)
                    for b in routed_in(TRANSPOSED_AT, g, q, layer):
                        scale_xT(b, layer)

                run_slots(act, layer, slot)
                scale_xT(B - 1, layer)
                number_partitions(layer)
                w0 = layer * GROUPS
                copy_rowsT(w0)
                expert_group(w0)
                with act.Fori(w0 + 1, w0 + GROUPS) as w:
                    copy_rowsT(w)
                    expert_group(w)

        @block.vector
        def _(dve):
            def split_columns(dst, src):
                for half in range(2):
                    ins = dve.tensor_copy(
                        dst[:, half * 64:half * 64 + 64].rearrange("p (d q h) -> p d q h", q=QUADS, h=2),
                        src.rearrange("p (q r h d) -> p r d q h", q=QUADS, r=2, h=2)[:, half])
                return ins

            dve.wait_ge(loaded, 16 * N_LOADS)
            for n in range(2):
                split_columns(b_ordered[:, n, :], b_natural[:, n, :])
                ins = split_columns((w_q, w_k)[n][:, 0, :], w_natural[:, n, :])
            ins.then_inc(ordered, 1)
            dve.memset(credit[:, 0:1], 0.0).then_inc(k3_ready, 1)
            dve.wait_ge(bias_full, 1)
            dve.tensor_copy(b_qk[:].rearrange("p n e -> p (n e)"), d_ps[:, 0:2 * E]).then_inc(bias_ready, 1)
            dve.memset(credit[:, 2:3], 0.0).then_inc(s_free, S_BANKS)
            dve.memset(credit[:, 3:4], 0.0).then_inc(x_updated, 1)

            def x_tile(g, layer, t, n=1):
                return x_sb[:, bass.ds((g - layer * B) * NT + t, n), :]

            def update_stats(g, layer):
                dve.wait_ge(x_updated, 1 + g + 1)
                dve.sem_inc(dve_waited, 1)
                for t in range(NT):
                    ins = dve.bn_stats(out=stats[:, t, :], in_=flat(x_tile(g, layer, t)))
                ins.then_inc(ffn_stats_done, 1)

            def update_means(g, layer):
                dve.wait_ge(ffn_stats_done, g + 1)
                dve.wait_ge(rstd_ready, g + 1)
                dve.sem_inc(dve_waited, 1)
                for t in range(NT):
                    ins = dve.bn_aggr(out=batch_mean_var[:, t, :], in_=stats[:, t, :])
                ins.then_inc(batch_mean_ready, 1)
                dve.wait_ge(batch_mean_ready, g + 1)
                dve.tensor_copy(mean_var[:, bass.ds((g - layer * B) * NT, NT), :],
                                batch_mean_var[:]).then_inc(mean_ready, 1)

            def attention_means(layer, b):
                for t in range(b * NT, b * NT + NT):
                    ins = dve.bn_stats(out=stats[:, t, :], in_=x_sb[:, t, :])
                ins.then_inc(att_stats_done, 1)
                dve.wait_ge(att_stats_done, layer * B + b + 1)
                for t in range(b * NT, b * NT + NT):
                    ins = dve.bn_aggr(out=att_mean_var[:, t, :], in_=stats[:, t, :])
                if b in (0, B - 1):
                    ins.then_inc(att_mean_ready, 1)

            def flat(ap):
                return ap.rearrange("p o c -> p (o c)")

            def normalize(g, layer, tiles=range(NT)):
                if 0 in tiles:
                    dve.wait_ge(att_rstd_ready, 2 * layer + (1 if isinstance(g, int) and g == layer * B else 2))
                    dve.wait_ge(xT_full, g + 1)
                for t in tiles:
                    ins = dve.tensor_scalar(xn[:, t, :], flat(x_tile(g, layer, t)),
                                            flat(att_mean_var[:, bass.ds((g - layer * B) * NT + t, 1), 0:1]),
                                            att_rstd[:, bass.ds((g - layer * B) * NT + t, 1)], ALU.subtract, ALU.mult)
                if NT - 1 in tiles:
                    ins.then_inc(xn_ready, 1)

            def row_max(g, q, u):
                half, k = u % 2, u // 2
                dve.wait_ge(s_full, 40 * g + 10 * q + u + 1)
                ps = s_ps[(10 * q + u) % S_BANKS]
                out_ = neg_max[:, q, :].rearrange("p (h j t) -> p h j t", h=2, j=2)[:, half]
                if k < 4:
                    dve.sem_inc(dve_waited, 1)
                    for head, t, col in s_bank(k):
                        w = (t + 1) * P
                        scores = ps[:, col:col + w]
                        ins = dve.tensor_tensor_reduce(out=scores, in0=scores, in1=causal[:, S - w:], scale=-1.0,
                                                       scalar=-MASKED, op0=ALU.add, op1=ALU.min,
                                                       accum_out=out_[:, head, t:t + 1])
                else:
                    ins = dve.tensor_reduce(out_[:, :, 1], ps[:].rearrange("p (h w) -> p h w", h=2),
                                            axis=AX.X, op=ALU.max, negate=True)
                ins.then_inc(s_free, 1)

            def copy_maxT(g, q):
                dve.wait_ge(maxT_full, 4 * g + q + 1)
                dve.tensor_copy(neg_maxT[:, q, :], d_ps[0:16, 0:P]).then_inc(maxT_ready, 1)

            def split_first_queries(layer):
                dve.wait_ge(qf_ready, layer * B + 1)
                dve.tensor_tensor(out=q_rest[:], in0=qf[:], in1=q3[:, 0, :], op=ALU.subtract).then_inc(q_split_step, 1)
                dve.wait_ge(q_split_step, 2 * layer + 1)
                dve.tensor_copy(q3[:, 1, :], q_rest[:]).then_inc(q_split_step, 1)
                dve.wait_ge(q_split_step, 2 * layer + 2)
                dve.tensor_tensor(out=q3[:, 2, :], in0=q_rest[:], in1=q3[:, 1, :],
                                  op=ALU.subtract).then_inc(q3_ready, 1)

            def split_keys(g, steps=range(3)):
                if 0 in steps:
                    dve.wait_ge(kf_ready, g + 1)
                    dve.tensor_tensor(out=k_rest[:], in0=kf[:], in1=k3[:, 0, :],
                                      op=ALU.subtract).then_inc(k_split_step, 1)
                if 1 in steps:
                    dve.wait_ge(k_split_step, 2 * g + 1)
                    dve.tensor_copy(k3[:, 1, :], k_rest[:]).then_inc(k_split_step, 1)
                if 2 in steps:
                    dve.wait_ge(k_split_step, 2 * g + 2)
                    dve.tensor_tensor(out=k3[:, 2, :], in0=k_rest[:], in1=k3[:, 1, :],
                                      op=ALU.subtract).then_inc(k3_ready, 1)

            def divide(g, q, layer, base):
                n = 4 * g + q
                dve.wait_ge(oTT_full, OT_BUFS + n + 1)
                o = d_ps[:].rearrange("p (t h e) -> p t h e", t=NT, h=4)
                dve.reciprocal(recip[:], o[:, :, :, DH]).then_inc(dve_step, 1)
                dve.wait_ge(dve_step, base + 1)
                dve.tensor_tensor(out=attn[:, :, 32 * q:32 * q + 32].rearrange("p t (h d) -> p t h d", h=4),
                                  in0=o[:, :, :, 0:DH], in1=recip[:][:, :, :, None].broadcast_to([P, NT, 4, DH]),
                                  op=ALU.mult).then_inc(attn_ready, 1)

            CHOOSE_STEPS, PLACE_STEPS = 4, 23

            def ffn_normalize(b, ffn):
                done = ffn * B + b
                if b == 0:
                    dve.wait_ge(pv_done, PT_BUFS + QUADS * B * (ffn + 1) - 1)
                dve.wait_ge(rstd_ready, 1 + done + 1)
                tiles = range(b * NT, b * NT + NT)
                for t in tiles:
                    ins = dve.tensor_scalar(x_routed[:, t, :], x_sb[:, t, :], mean_var[:, t, 0:1],
                                            both_rstd[:, t:t + 1], ALU.subtract, ALU.mult)
                ins.then_inc(xs_ready, 1)
                dve.wait_ge(xs_ready, done + 1)
                for t in tiles:
                    ins = dve.scalar_tensor_tensor(out=x_sb[:, t, :], in0=x_routed[:, t, :],
                                                   scalar=to_xl[:, t:t + 1], in1=x_sb[:, t, :],
                                                   op0=ALU.mult, op1=ALU.add)
                ins.then_inc(skip_added, 1)

            def choose(ffn, base):
                def next_reads(ins, n):
                    ins.then_inc(ffn_step, 1)
                    dve.wait_ge(ffn_step, base + n)

                dve.wait_ge(dist_full, B * (ffn + 1))
                next_reads(dve.tensor_reduce(nearest[:], dist, axis=AX.X, op=ALU.min), 1)
                next_reads(dve.tensor_tensor(out=farther[:], in0=dist,
                                             in1=nearest[:].unsqueeze(2).broadcast_to([P, TILES, E]),
                                             op=ALU.is_gt), 2)
                next_reads(dve.scalar_tensor_tensor(out=candidate[:].rearrange("p t e -> p (t e)"),
                                                    in0=farther[:].rearrange("p t e -> p (t e)"), scalar=float(E),
                                                    in1=expert_row[:].rearrange("p t e -> p (t e)"),
                                                    op0=ALU.mult, op1=ALU.add), 3)
                next_reads(dve.tensor_reduce(chosen[:], candidate[:], axis=AX.X, op=ALU.min), 4)
                dve.tensor_tensor(out=one_hot[:].rearrange("p e t -> p t e"), in0=expert_row[:],
                                  in1=chosen[:].unsqueeze(2).broadcast_to([P, TILES, E]),
                                  op=ALU.is_equal).then_inc(routed, 1)

            def places(ffn, base):
                n = [base]

                def next_reads(ins):
                    ins.then_inc(ffn_step, 1)
                    n[0] += 1
                    dve.wait_ge(ffn_step, n[0])

                dve.wait_ge(counts_full, ffn + 1)
                next_reads(dve.tensor_copy(counts[:, 0, :, PAD:], s_ps[1][:, 0:E * TILES].rearrange(
                    "p (e t) -> p e t", e=E)))
                k, shift = 0, 1
                while shift < TILES:
                    next_reads(dve.tensor_tensor(out=counts[:, 1 - k, :, PAD:], in0=counts[:, k, :, PAD:],
                                                 in1=counts[:, k, :, PAD - shift:PAD - shift + TILES], op=ALU.add))
                    k, shift = 1 - k, 2 * shift
                next_reads(dve.tensor_scalar(slots_i[:, 0, :], counts[:, k, :, PAD + TILES - 1], float(P - 1), None,
                                             ALU.add))
                next_reads(dve.tensor_scalar(slots_i[:, 1, :], slots_i[:, 0, :], P.bit_length() - 1, None,
                                             ALU.arith_shift_right))
                next_reads(dve.tensor_copy(slots_of[:], slots_i[:, 1, :]))
                next_reads(dve.tensor_copy(slots_f[:, 0, E:], slots_of[:]))
                j, shift = 0, 1
                while shift < E:
                    next_reads(dve.tensor_tensor(out=slots_f[:, 1 - j, E:], in0=slots_f[:, j, E:],
                                                 in1=slots_f[:, j, E - shift:2 * E - shift], op=ALU.add))
                    j, shift = 1 - j, 2 * shift
                next_reads(dve.tensor_tensor(out=base_row[:], in0=slots_f[:, j, E:], in1=slots_of[:],
                                             op=ALU.subtract))
                next_reads(dve.scalar_tensor_tensor(
                    out=place[:, 0], in0=base_row[:].unsqueeze(2).broadcast_to([P, E, TILES]), scalar=float(P),
                    in1=counts[:, k, :, PAD - 1:PAD - 1 + TILES], op0=ALU.mult, op1=ALU.add))
                next_reads(dve.tensor_tensor(out=place[:, 1], in0=s_ps[0][:, 0:E * TILES].rearrange(
                    "p (e t) -> p e t", e=E), in1=place[:, 0], op=ALU.add))
                next_reads(dve.tensor_tensor(out=place[:, 2], in0=place[:, 1], in1=one_hot[:], op=ALU.mult))
                next_reads(dve.tensor_reduce(place_f[:], place[:, 2].rearrange("p e t -> p t e"), axis=AX.X,
                                             op=ALU.add))
                next_reads(dve.tensor_copy(place_i[:, 0], place_f[:]))
                dve.tensor_scalar(place_i[:, 1], place_i[:, 0], P.bit_length() - 1, None, ALU.arith_shift_right)
                next_reads(dve.tensor_scalar(place_i[:, 2], place_i[:, 0], P - 1, None, ALU.bitwise_and))
                dve.tensor_copy(slot_of[:], place_i[:, 1])
                next_reads(dve.tensor_copy(row_of[:], place_i[:, 2]))
                dve.tensor_tensor(out=slot_hot[:, :, 0, :], in0=slot_no[:].unsqueeze(1).broadcast_to([P, TILES, SLOTS]),
                                  in1=slot_of[:].unsqueeze(2).broadcast_to([P, TILES, SLOTS]),
                                  op=ALU.is_equal).then_inc(slots_marked, 1)
                dve.tensor_tensor(out=row_hot, in0=row_no[:].unsqueeze(1).broadcast_to([P, TILES, P]),
                                  in1=row_of[:].unsqueeze(2).broadcast_to([P, TILES, P]),
                                  op=ALU.is_equal).then_inc(rows_marked, 1)
                next_reads(dve.tensor_tensor(out=slot_past[:],
                                             in0=slot_no[0:1, :].unsqueeze(2).broadcast_to([1, SLOTS, E]),
                                             in1=slots_f[0:1, j, E:].unsqueeze(1).broadcast_to([1, SLOTS, E]),
                                             op=ALU.is_ge))
                next_reads(dve.tensor_reduce(slot_f[:], slot_past[:], axis=AX.X, op=ALU.add))
                dve.tensor_scalar(slot_expert[:], slot_f[:], float(E - 1), None, ALU.min).then_inc(place_ready, 1)
                dve.wait_ge(tokens_full, ffn + 1)
                tile, partition = s_ps[0][:, 0:SLOTS], s_ps[0][:, SLOTS:2 * SLOTS]
                dve.tensor_copy(partition_of[:], partition).then_inc(tokens_step, 1)
                dve.wait_ge(tokens_step, 2 * ffn + 1)
                dve.scalar_tensor_tensor(out=token_of[:], in0=tile, scalar=float(P), in1=partition_of[:],
                                         op0=ALU.mult, op1=ALU.add)
                dve.scalar_tensor_tensor(out=unused[:], in0=partition_of[:], scalar=0.0, in1=unused_row[:],
                                         op0=ALU.is_equal, op1=ALU.mult).then_inc(tokens_step, 1)
                dve.wait_ge(tokens_step, 2 * ffn + 2)
                dve.tensor_scalar(read_row[:], token_of[:], -1.0, 0.0, ALU.add, ALU.max)
                dve.scalar_tensor_tensor(out=write_row[:], in0=token_of[:], scalar=-1.0, in1=unused[:],
                                         op0=ALU.add, op1=ALU.add).then_inc(tokens_ready, 1)
                assert n[0] - base == PLACE_STEPS, n[0] - base

            hT_ps = (st_ps[0], st_ps[1], pv_ps)

            def gate_hidden(w):
                for j in range(GROUP):
                    dve.wait_ge(gate_ready, GROUP * w + j + 1)
                    dve.tensor_tensor(out=hidden[:, j, :], in0=s_ps[j][:, 0:F], in1=gate[:, j, :],
                                      op=ALU.mult).then_inc(hidden_ready, 1)

            def copy_hiddenT(w):
                for j in range(GROUP):
                    dve.wait_ge(hiddenT_full, GROUP * w + j + 1)
                    dve.tensor_copy(hiddenT[:, j, :], hT_ps[j][:, 0:F]).then_inc(hiddenT_ready, 1)

            def copy_y(w, k):
                dve.wait_ge(y_full, w + 1)
                dve.tensor_copy(y_out[:, k].rearrange("p s c -> p (s c)"), d_ps[:, 0:GROUP * C]).then_inc(y_copied, 1)

            def expert_groups(ffn):
                w0 = ffn * GROUPS

                def y_sent(k, groups):
                    dve.wait_ge(y_saved[k], 16 * GROUP * (groups + GROUPS_OF[k] * ffn))

                gate_hidden(w0)
                copy_hiddenT(w0)
                for w in (w0 + 1, w0 + 2):
                    gate_hidden(w)
                    copy_y(w - 1, w - w0 - 1)
                    copy_hiddenT(w)
                with dve.Fori(0, (GROUPS - 3) // 2) as i:
                    for k in range(2):
                        w = w0 + 2 * i + 3 + k
                        gate_hidden(w)
                        y_sent(k, i + 1)
                        copy_y(w - 1, k)
                        copy_hiddenT(w)
                y_sent(0, GROUPS // 2)
                copy_y(w0 + GROUPS - 1, 0)

            def fold_copies():
                dve.wait_ge(fold_done, 1)
                dve.tensor_copy(w_uqT[:], a_ps[:L, 0:C]).then_inc(fold_copied, 1)
                dve.wait_ge(fold_done, 2)
                dve.tensor_copy(w_obT[:], d_ps[:, 0:C]).then_inc(fold_copied, 1)
                dve.wait_ge(fold_done, 3)
                split_columns(w_q[:, 1, :], a_ps[:, 0:C]).then_inc(fold_copied, 1)
                dve.wait_ge(fold_done, 4)
                dve.tensor_copy(qeffT[:], d_ps[:, 0:C]).then_inc(fold_copied, 1)
                dve.wait_ge(fold_done, 5)
                dve.tensor_copy(keffT[:], a_ps[:L, 0:C]).then_inc(fold_copied, 1)
                dve.wait_ge(fold_done, 6)
                dve.tensor_copy(veff[:], d_ps[:L, 0:C]).then_inc(fold_copied, 1)
                dve.wait_ge(fold_done, 7)
                split_columns(w_k[:, 1, :], a_ps[:, 0:C]).then_inc(fold_copied, 1)
                dve.wait_ge(fold_done, 8)
                dve.tensor_copy(w_v[:, 1, :], d_ps[:, 0:C]).then_inc(fold_copied, 1)
                dve.wait_ge(fold_done, 9)
                dve.tensor_copy(centT[:], a_ps[:, 0:E]).then_inc(ffn_step, 1)
                dve.wait_ge(ffn_step, 1)
                dve.tensor_scalar(cent_m2T[:], centT[:], -2.0, None, ALU.mult)
                dve.tensor_tensor(out=cent_sqT[:], in0=centT[:], in1=centT[:], op=ALU.mult).then_inc(fold_copied, 1)
                dve.wait_ge(fold_done, 10)
                dve.tensor_copy(b_v_cols[:], d_ps[:, 0:P]).then_inc(fold_copied, 1)
                dve.wait_ge(fold_done, 11)
                dve.tensor_copy(out_bias[:], d_ps[:, 0:C]).then_inc(fold_copied, 1)

            def add_y(b):
                dve.wait_ge(returned[b], 16)
                if b == 0:
                    dve.wait_ge(skip_added, B)
                dve.tensor_tensor(out=x_sb[:, b * NT:(b + 1) * NT, :], in0=y_routed[:, b * NT:(b + 1) * NT, :],
                                  in1=x_sb[:, b * NT:(b + 1) * NT, :], op=ALU.add).then_inc(y_added, 1)
                dve.wait_ge(y_added, b + 1)

            def start_batch(layer, b):
                if layer == 0:
                    dve.wait_ge(loaded_x[min(b, 1)], 16 if b == 0 else 16 * (B - 1))
                else:
                    add_y(b)
                attention_means(layer, b)

            for layer in range(2):
                start_batch(layer, 0)
                normalize(layer * B, layer)
                start_batch(layer, 1)
                start_batch(layer, 2)
                split_keys(layer * B)
                start_batch(layer, 3)
                split_first_queries(layer)
                for b in range(4, B):
                    start_batch(layer, b)
                if layer == 0:
                    fold_copies()

                def slot(g, p, h, q):
                    g1, p1, q1 = earlier(g, p, h, q, 1)
                    if q == 0 and layer == 1 and within(g - 2, layer):
                        dve.wait_ge(attn_ready, 4 * g - 4)
                        dve.tensor_tensor(out=x_tile(g - 2, 1, 0, NT), in0=attn[:], in1=x_tile(g - 2, 1, 0, NT),
                                          op=ALU.add).then_inc(x_updated, 1)
                    for b in routed_in(NORMALIZED_AT, g, q, layer):
                        ffn_normalize(b, layer)
                    for u in range(10):
                        if within(g, layer):
                            row_max(g, q, u)
                        if u == 2 and within(g1, layer):
                            copy_maxT(g1, q1)
                        if q == 1 and u < NT // 2 and within(g + 1, layer):
                            normalize(g + 1, layer, (2 * u, 2 * u + 1))
                        if q == 1 and 7 <= u <= 9 and within(g + 1, layer):
                            split_keys(g + 1, (u - 7,))
                        if u == 7 and within(g - 1, layer):
                            divide(g - 1, q, layer, 4 * (g - 1) + q)
                        if q == 0 and within(g - 2, layer):
                            if u == 4 and layer == 0:
                                dve.wait_ge(proj_full, g - 1)
                                dve.wait_ge(bias_added, g - 1)
                                dve.tensor_tensor(out=x_tile(g - 2, 0, 0, NT),
                                                  in0=d_ps[:].rearrange("p (t c) -> p t c", t=NT),
                                                  in1=x_tile(g - 2, 0, 0, NT), op=ALU.add).then_inc(x_updated, 1)
                            if u == 5:
                                update_stats(g - 2, layer)
                            if u == 8:
                                update_means(g - 2, layer)

                run_slots(dve, layer, slot)
                ffn_normalize(B - 1, layer)
                base = 1 + layer * (CHOOSE_STEPS + PLACE_STEPS)
                choose(layer, base)
                places(layer, base + CHOOSE_STEPS)
                expert_groups(layer)
                if layer == 1:
                    dve.wait_ge(skip_added, 2 * B)
                    for b in range(B):
                        dve.wait_ge(returned[b], 16 * 2)
                        dve.tensor_tensor(out=x_sb[:, b * NT:(b + 1) * NT, :], in0=y_routed[:, b * NT:(b + 1) * NT, :],
                                          in1=x_sb[:, b * NT:(b + 1) * NT, :], op=ALU.add).then_inc(y_added, 1)


_INS = ['L0_attn_a_x', 'L0_attn_a_W_q', 'L0_attn_a_b_q', 'L0_attn_a_W_k', 'L0_attn_a_b_k', 'L0_attn_a_W_v',
        'L0_attn_a_b_v', 'L0_attn_a_W_o', 'L0_attn_a_b_o', 'L0_attn_b_W_dq', 'L0_attn_b_W_uq', 'L0_attn_b_W_dkv',
        'L0_attn_b_W_uk', 'L0_attn_b_W_uv', 'L0_attn_b_W_o', 'L0_ffn_scale', 'L0_ffn_centroids', 'L0_ffn_up_w',
        'L0_ffn_down_w']


def kernel(**inputs):
    import numpy as _np
    import concourse.bacc as _bacc
    from concourse import mybir as _mybir
    from concourse.bass_utils import run_bass_kernel_spmd as _run

    nc = _bacc.Bacc("TRN2", target_bir_lowering=False, num_devices=1)
    arrays, args = {}, []
    for name in _INS:
        a = _np.ascontiguousarray(inputs[name])
        arrays[f"in_{name}_dram"] = a
        args.append(nc.dram_tensor(f"in_{name}_dram", a.shape, _mybir.dt.from_np(a.dtype), kind="ExternalInput").ap())
    shape = inputs['L0_attn_a_x'].shape
    args.append(nc.dram_tensor("out_0_dram", shape, _mybir.dt.float32, kind="ExternalOutput").ap())
    hybrid_layers(nc, *args)
    r = _run(nc, [arrays], core_ids=[0])
    return r.results[0]["out_0_dram"]
```
